# Optimizing a Trainium2 kernel written in Bass

```python
import numpy as np
import jax
import jax.numpy as jnp

def _softmax(x, axis=-1):
    return jax.nn.softmax(x, axis=axis)

def _gelu(x):
    return jax.nn.gelu(x, approximate=True)

def _silu(x):
    return jax.nn.silu(x)

def _sigmoid(x):
    return jax.nn.sigmoid(x)

def _layernorm(x, axis=-1, eps=1e-05):
    m = jnp.mean(x, axis=axis, keepdims=True)
    v = jnp.var(x, axis=axis, keepdims=True)
    return (x - m) / jnp.sqrt(v + eps)

def _scatter_add(tgt, idx, src, axis=0):
    return tgt.at[idx].add(src)

def _segment_sum(src, seg, n):
    return jax.ops.segment_sum(src, seg, n)
kernel_name = 'mk_adaln_d2_jaxref_r8_9cf02e'

def setup_inputs(seed: int=0):
    np.random.seed(seed)
    _w = jnp.asarray

    def _L0_attn_setup():
        import jax, jax.numpy as jnp
        import numpy as np
        NORM_EPS = 1e-06
        QK_SCALE = 1.0 / 128.0
        ROTARY_BASE = 1250
        INFTY_APPROX = 1e+30
        B, T, M, H, D = (2, 256, 128, 8, 128)

        def _rmsnorm(x, eps=NORM_EPS):
            ms = jnp.mean(jnp.square(x), axis=-1, keepdims=True)
            return x / jnp.sqrt(ms + eps)

        def _rope(x, base=ROTARY_BASE):
            length, width = (x.shape[-2], x.shape[-1])
            half = width // 2
            pos = jnp.arange(length, dtype=x.dtype)[:, None]
            freqs = jnp.power(jnp.asarray(base, x.dtype), -jnp.arange(half, dtype=x.dtype) / half)[None, :]
            rad = pos * freqs
            cos = jnp.cos(rad)[None, None]
            sin = jnp.sin(rad)[None, None]
            even, odd = jnp.split(x, 2, axis=-1)
            return jnp.concatenate([even * cos - odd * sin, even * sin + odd * cos], axis=-1)
        key = jax.random.key(seed)
        ks = jax.random.split(key, 5)
        std = M ** (-0.5)
        return {'x': jax.random.normal(ks[0], (B, T, M), jnp.float32), 'wq': jax.random.normal(ks[1], (M, H, D), jnp.float32) * std, 'wk': jax.random.normal(ks[2], (M, H, D), jnp.float32) * std, 'wv': jax.random.normal(ks[3], (M, H, D), jnp.float32) * std, 'wo': jax.random.normal(ks[4], (H, D, M), jnp.float32) * std}
    _L0_attn_in = _L0_attn_setup()

    def _L0_ffn_setup():
        import jax, jax.numpy as jnp
        import numpy as np
        D = 128
        LW = 16
        DEPTH = 8
        NN = 2 ** DEPTH - 1
        NL = 2 ** DEPTH
        B, S = (2, 128)

        def _fff(x, nw, nb, w1, b1, w2, b2, act):
            node = jnp.zeros(x.shape[:2], dtype=jnp.int32)
            for _ in range(DEPTH):
                logit = jnp.einsum('bsd,bsd->bs', x, nw[node]) + nb[node]
                node = 2 * node + 1 + (logit > 0).astype(jnp.int32)
            leaf = node - NN
            h = act(jnp.einsum('bsd,bsdl->bsl', x, w1[leaf]) + b1[leaf])
            return jnp.einsum('bsl,bsld->bsd', h, w2[leaf]) + b2[leaf]

        def _forward(x, q_nw, q_nb, q_w1, q_b1, q_w2, q_b2, k_nw, k_nb, k_w1, k_b1, k_w2, k_b2, v_nw, v_nb, v_w1, v_b1, v_w2, v_b2, f_nw, f_nb, f_w1, f_b1, f_w2, f_b2):
            mu = jnp.mean(x, -1, keepdims=True)
            sd = jnp.std(x, -1, ddof=1, keepdims=True)
            xn = (x - mu) / jnp.sqrt(sd + 1e-05)
            relu = jax.nn.relu
            q = _fff(xn, q_nw, q_nb, q_w1, q_b1, q_w2, q_b2, relu)
            k = _fff(xn, k_nw, k_nb, k_w1, k_b1, k_w2, k_b2, relu)
            v = _fff(xn, v_nw, v_nb, v_w1, v_b1, v_w2, v_b2, relu)
            att = jax.nn.softmax(jnp.einsum('bqd,bkd->bqk', q, k) / jnp.sqrt(jnp.float32(D)), axis=-1)
            y = xn + jnp.einsum('bqk,bkd->bqd', att, v)
            gelu = lambda t: jax.nn.gelu(t, approximate=False)
            return y + _fff(y, f_nw, f_nb, f_w1, f_b1, f_w2, f_b2, gelu)

        def _make_fff_params(key, scale_in, scale_leaf):
            ks = jax.random.split(key, 4)
            nw = jax.random.normal(ks[0], (NN, D), jnp.float32) * scale_in
            nb = jnp.zeros((NN,), jnp.float32)
            w1 = jax.random.normal(ks[1], (NL, D, LW), jnp.float32) * scale_in
            b1 = jax.random.normal(ks[2], (NL, LW), jnp.float32) * 0.01
            w2 = jax.random.normal(ks[3], (NL, LW, D), jnp.float32) * scale_leaf
            b2 = jnp.zeros((NL, D), jnp.float32)
            return (nw, nb, w1, b1, w2, b2)
        key = jax.random.key(seed)
        kx, kq, kk, kv, kf = jax.random.split(key, 5)
        s_in = 1.0 / np.sqrt(D)
        s_lf = 1.0 / np.sqrt(LW)
        inp = {'x': jax.random.normal(kx, (B, S, D), jnp.float32)}
        for name, kk_ in (('q', kq), ('k', kk), ('v', kv), ('f', kf)):
            nw, nb, w1, b1, w2, b2 = _make_fff_params(kk_, s_in, s_lf)
            inp.update({f'{name}_nw': nw, f'{name}_nb': nb, f'{name}_w1': w1, f'{name}_b1': b1, f'{name}_w2': w2, f'{name}_b2': b2})
        return inp
    _L0_ffn_in = _L0_ffn_setup()
    _L0_c = _w((lambda *s: np.random.randn(*s).astype(np.float32) * 0.05)(8, 128))
    _L0_wmod = _w((lambda *s: np.random.randn(*s).astype(np.float32) * 0.05)(128, 6 * 128) * 128 ** (-0.5))

    def _L1_attn_setup():
        import jax, jax.numpy as jnp
        import numpy as np
        from jax import lax
        D_MODEL, D_INNER, D_STATE, D_CONV, DT_RANK = (128, 256, 16, 4, 64)
        B, L = (1, 256)

        def _reference_tuple_inner(x, W_in, conv_w, conv_b, W_x, W_dt, b_dt, A_log, D, W_out):
            b, l, dm = x.shape
            di, n = (A_log.shape[0], A_log.shape[1])
            x_and_res = x @ W_in
            xc, res = (x_and_res[..., :di], x_and_res[..., di:])
            k = conv_w.shape[1]
            xp = jnp.pad(xc, ((0, 0), (k - 1, 0), (0, 0)))
            xconv = conv_b
            for j in range(k):
                xconv = xconv + xp[:, j:j + l, :] * conv_w[:, j]
            xs = jax.nn.silu(xconv)
            x_dbl = xs @ W_x
            dt_r = x_dbl[..., :DT_RANK]
            Bm = x_dbl[..., DT_RANK:DT_RANK + n]
            Cm = x_dbl[..., DT_RANK + n:]
            dt = jax.nn.softplus(dt_r @ W_dt + b_dt)
            A = -jnp.exp(A_log)
            dA = jnp.exp(jnp.einsum('bld,dn->bldn', dt, A))
            dBx = jnp.einsum('bld,bln->bldn', dt, Bm) * xs[..., None]

            def step(h, inp):
                dA_t, dBx_t, C_t = inp
                h = dA_t * h + dBx_t
                y = jnp.einsum('bdn,bn->bd', h, C_t)
                return (h, y)
            h0 = jnp.zeros((b, di, n), x.dtype)
            hT, ys = lax.scan(step, h0, (dA.transpose(1, 0, 2, 3), dBx.transpose(1, 0, 2, 3), Cm.transpose(1, 0, 2)))
            y = ys.transpose(1, 0, 2) + xs * D
            y = y * jax.nn.silu(res)
            out = y @ W_out
            return (out, hT)
        key = jax.random.key(seed)
        ks = jax.random.split(key, 10)
        s = lambda d: 1.0 / np.sqrt(d)
        return {'x': jax.random.normal(ks[0], (B, L, D_MODEL), jnp.float32), 'W_in': jax.random.normal(ks[1], (D_MODEL, 2 * D_INNER), jnp.float32) * s(D_MODEL), 'conv_w': jax.random.normal(ks[2], (D_INNER, D_CONV), jnp.float32) * s(D_CONV), 'conv_b': jax.random.normal(ks[3], (D_INNER,), jnp.float32) * 0.01, 'W_x': jax.random.normal(ks[4], (D_INNER, DT_RANK + 2 * D_STATE), jnp.float32) * s(D_INNER), 'W_dt': jax.random.normal(ks[5], (DT_RANK, D_INNER), jnp.float32) * s(DT_RANK), 'b_dt': jax.random.normal(ks[6], (D_INNER,), jnp.float32) * 0.01, 'A_log': jnp.log(jnp.tile(jnp.arange(1.0, D_STATE + 1.0, dtype=jnp.float32), (D_INNER, 1))), 'D': jnp.ones((D_INNER,), jnp.float32), 'W_out': jax.random.normal(ks[7], (D_INNER, D_MODEL), jnp.float32) * s(D_INNER)}
    _L1_attn_in = _L1_attn_setup()

    def _L1_ffn_setup():
        import jax, jax.numpy as jnp
        import numpy as np
        DIM = 128
        DEPTH = 6
        HEADS = 16
        DIM_HEAD = 64
        WINDOW = 32
        INNER = HEADS * DIM_HEAD
        DIM_INNER = int(DIM * 4 * 2 / 3)
        QK_SCALE = 8.0

        def shift_tokens(t):
            a, s = jnp.split(t, 2, -1)
            s = jnp.pad(s, ((0, 0), (1, 0), (0, 0)))[:, :-1]
            return jnp.concatenate([a, s], -1)

        def l2norm(t):
            return t / jnp.maximum(jnp.linalg.norm(t, axis=-1, keepdims=True), 1e-12)

        def rotate_half(x):
            x1, x2 = jnp.split(x, 2, -1)
            return jnp.concatenate([-x2, x1], -1)

        def rotary_tables(n):
            half = jnp.arange(0, DIM_HEAD, 2, dtype=jnp.float32)
            inv_freq = 1.0 / 10000.0 ** (half / DIM_HEAD)
            t = jnp.arange(n, dtype=jnp.float32)
            freqs = t[:, None] * inv_freq[None, :]
            freqs = jnp.concatenate([freqs, freqs], -1)
            base_scale = (half + 0.4 * DIM_HEAD) / (1.4 * DIM_HEAD)
            power = (t - n // 2) / (WINDOW // 2)
            scale = base_scale[None, :] ** power[:, None]
            scale = jnp.concatenate([scale, scale], -1)
            return (freqs, scale)

        def local_attention(q, k, v):
            b, h, n, d = q.shape
            w = WINDOW
            nw = n // w
            bq = q.reshape(b, h, nw, w, d)
            bk = k.reshape(b, h, nw, w, d)
            bv = v.reshape(b, h, nw, w, d)

            def look(t):
                p = jnp.pad(t, ((0, 0), (0, 0), (1, 0), (0, 0), (0, 0)))
                return jnp.concatenate([p[:, :, :nw], p[:, :, 1:]], axis=3)
            bk2, bv2 = (look(bk), look(bv))
            seq = jnp.arange(n).reshape(nw, w)
            seq_p = jnp.pad(seq, ((1, 0), (0, 0)), constant_values=-1)
            jt = jnp.concatenate([seq_p[:nw], seq_p[1:]], axis=1)
            it = seq[:, :, None]
            jb = jt[:, None, :]
            mask = (it < jb) | (it > jb + w) | (jb == -1)
            sim = jnp.einsum('bhwie,bhwje->bhwij', bq, bk2) * QK_SCALE
            sim = jnp.where(mask, -jnp.finfo(sim.dtype).max, sim)
            attn = jax.nn.softmax(sim, -1)
            out = jnp.einsum('bhwij,bhwje->bhwie', attn, bv2)
            return out.reshape(b, h, n, d)

        def attn_layer(x, Wqkv, qs, ksc, Wo):
            b, n, _ = x.shape
            qkv = x @ Wqkv
            q, k, v = jnp.split(qkv, 3, -1)
            sh = lambda t: t.reshape(b, n, HEADS, DIM_HEAD).transpose(0, 2, 1, 3)
            q, k, v = (sh(q), sh(k), sh(v))
            q = l2norm(q) * qs
            k = l2norm(k) * ksc
            freqs, scale = rotary_tables(n)
            cos, sin = (jnp.cos(freqs), jnp.sin(freqs))
            q = q * cos * scale + rotate_half(q) * sin * scale
            inv = 1.0 / scale
            k = k * cos * inv + rotate_half(k) * sin * inv
            out = local_attention(q, k, v)
            out = out.transpose(0, 2, 1, 3).reshape(b, n, INNER)
            return out @ Wo

        def ffn_layer(x, g, bln, W1, b1, W2, b2):
            mu = x.mean(-1, keepdims=True)
            var = ((x - mu) ** 2).mean(-1, keepdims=True)
            xn = (x - mu) / jnp.sqrt(var + 1e-05) * g + bln
            hg = xn @ W1 + b1
            a, gate = jnp.split(hg, 2, -1)
            return a * jax.nn.gelu(gate, approximate=False) @ W2 + b2
        key = jax.random.key(seed)
        ks = jax.random.split(key, 8)
        B, N = (2, 256)
        init = lambda k, shape: jax.random.normal(k, shape, jnp.float32) * 0.02
        return {'x': jax.random.normal(ks[0], (B, N, DIM), jnp.float32), 'Wqkv': init(ks[1], (DEPTH, DIM, 3 * INNER)), 'q_scale': jnp.ones((DEPTH, DIM_HEAD), jnp.float32), 'k_scale': jnp.ones((DEPTH, DIM_HEAD), jnp.float32), 'Wo': init(ks[2], (DEPTH, INNER, DIM)), 'ln_g': jnp.ones((DEPTH, DIM), jnp.float32), 'ln_b': jnp.zeros((DEPTH, DIM), jnp.float32), 'W1': init(ks[3], (DEPTH, DIM, 2 * DIM_INNER)), 'b1': jnp.zeros((DEPTH, 2 * DIM_INNER), jnp.float32), 'W2': init(ks[4], (DEPTH, DIM_INNER, DIM)), 'b2': jnp.zeros((DEPTH, DIM), jnp.float32)}
    _L1_ffn_in = _L1_ffn_setup()
    _L1_c = _w((lambda *s: np.random.randn(*s).astype(np.float32) * 0.05)(8, 128))
    _L1_wmod = _w((lambda *s: np.random.randn(*s).astype(np.float32) * 0.05)(128, 6 * 128) * 128 ** (-0.5))
    _d = {'L0_attn_x': _L0_attn_in['x'], 'L0_attn_wq': _L0_attn_in['wq'], 'L0_attn_wk': _L0_attn_in['wk'], 'L0_attn_wv': _L0_attn_in['wv'], 'L0_attn_wo': _L0_attn_in['wo'], 'L0_ffn_q_nw': _L0_ffn_in['q_nw'], 'L0_ffn_q_nb': _L0_ffn_in['q_nb'], 'L0_ffn_q_w1': _L0_ffn_in['q_w1'], 'L0_ffn_q_b1': _L0_ffn_in['q_b1'], 'L0_ffn_q_w2': _L0_ffn_in['q_w2'], 'L0_ffn_q_b2': _L0_ffn_in['q_b2'], 'L0_ffn_k_nw': _L0_ffn_in['k_nw'], 'L0_ffn_k_nb': _L0_ffn_in['k_nb'], 'L0_ffn_k_w1': _L0_ffn_in['k_w1'], 'L0_ffn_k_b1': _L0_ffn_in['k_b1'], 'L0_ffn_k_w2': _L0_ffn_in['k_w2'], 'L0_ffn_k_b2': _L0_ffn_in['k_b2'], 'L0_ffn_v_nw': _L0_ffn_in['v_nw'], 'L0_ffn_v_nb': _L0_ffn_in['v_nb'], 'L0_ffn_v_w1': _L0_ffn_in['v_w1'], 'L0_ffn_v_b1': _L0_ffn_in['v_b1'], 'L0_ffn_v_w2': _L0_ffn_in['v_w2'], 'L0_ffn_v_b2': _L0_ffn_in['v_b2'], 'L0_ffn_f_nw': _L0_ffn_in['f_nw'], 'L0_ffn_f_nb': _L0_ffn_in['f_nb'], 'L0_ffn_f_w1': _L0_ffn_in['f_w1'], 'L0_ffn_f_b1': _L0_ffn_in['f_b1'], 'L0_ffn_f_w2': _L0_ffn_in['f_w2'], 'L0_ffn_f_b2': _L0_ffn_in['f_b2'], 'L0_c': _L0_c, 'L0_wmod': _L0_wmod, 'L1_attn_W_in': _L1_attn_in['W_in'], 'L1_attn_conv_w': _L1_attn_in['conv_w'], 'L1_attn_conv_b': _L1_attn_in['conv_b'], 'L1_attn_W_x': _L1_attn_in['W_x'], 'L1_attn_W_dt': _L1_attn_in['W_dt'], 'L1_attn_b_dt': _L1_attn_in['b_dt'], 'L1_attn_A_log': _L1_attn_in['A_log'], 'L1_attn_D': _L1_attn_in['D'], 'L1_attn_W_out': _L1_attn_in['W_out'], 'L1_ffn_Wqkv': _L1_ffn_in['Wqkv'], 'L1_ffn_q_scale': _L1_ffn_in['q_scale'], 'L1_ffn_k_scale': _L1_ffn_in['k_scale'], 'L1_ffn_Wo': _L1_ffn_in['Wo'], 'L1_ffn_ln_g': _L1_ffn_in['ln_g'], 'L1_ffn_ln_b': _L1_ffn_in['ln_b'], 'L1_ffn_W1': _L1_ffn_in['W1'], 'L1_ffn_b1': _L1_ffn_in['b1'], 'L1_ffn_W2': _L1_ffn_in['W2'], 'L1_ffn_b2': _L1_ffn_in['b2'], 'L1_c': _L1_c, 'L1_wmod': _L1_wmod}
    _x0 = _d['L0_attn_x']
    _d['L0_attn_x'] = jax.random.normal(jax.random.fold_in(jax.random.key(seed), 1), (8, 256, 128), dtype=_x0.dtype)
    del _x0
    return _d

def reference(L0_attn_x, L0_attn_wq, L0_attn_wk, L0_attn_wv, L0_attn_wo, L0_ffn_q_nw, L0_ffn_q_nb, L0_ffn_q_w1, L0_ffn_q_b1, L0_ffn_q_w2, L0_ffn_q_b2, L0_ffn_k_nw, L0_ffn_k_nb, L0_ffn_k_w1, L0_ffn_k_b1, L0_ffn_k_w2, L0_ffn_k_b2, L0_ffn_v_nw, L0_ffn_v_nb, L0_ffn_v_w1, L0_ffn_v_b1, L0_ffn_v_w2, L0_ffn_v_b2, L0_ffn_f_nw, L0_ffn_f_nb, L0_ffn_f_w1, L0_ffn_f_b1, L0_ffn_f_w2, L0_ffn_f_b2, L0_c, L0_wmod, L1_attn_W_in, L1_attn_conv_w, L1_attn_conv_b, L1_attn_W_x, L1_attn_W_dt, L1_attn_b_dt, L1_attn_A_log, L1_attn_D, L1_attn_W_out, L1_ffn_Wqkv, L1_ffn_q_scale, L1_ffn_k_scale, L1_ffn_Wo, L1_ffn_ln_g, L1_ffn_ln_b, L1_ffn_W1, L1_ffn_b1, L1_ffn_W2, L1_ffn_b2, L1_c, L1_wmod):

    def _L0_attn_ref(x, wq, wk, wv, wo):
        import jax, jax.numpy as jnp
        import numpy as np
        NORM_EPS = 1e-06
        QK_SCALE = 1.0 / 128.0
        ROTARY_BASE = 1250
        INFTY_APPROX = 1e+30
        B, T, M, H, D = (2, 256, 128, 8, 128)

        def _rmsnorm(x, eps=NORM_EPS):
            ms = jnp.mean(jnp.square(x), axis=-1, keepdims=True)
            return x / jnp.sqrt(ms + eps)

        def _rope(x, base=ROTARY_BASE):
            length, width = (x.shape[-2], x.shape[-1])
            half = width // 2
            pos = jnp.arange(length, dtype=x.dtype)[:, None]
            freqs = jnp.power(jnp.asarray(base, x.dtype), -jnp.arange(half, dtype=x.dtype) / half)[None, :]
            rad = pos * freqs
            cos = jnp.cos(rad)[None, None]
            sin = jnp.sin(rad)[None, None]
            even, odd = jnp.split(x, 2, axis=-1)
            return jnp.concatenate([even * cos - odd * sin, even * sin + odd * cos], axis=-1)
        q = jnp.einsum('bim,mhd->bhid', x, wq)
        k = jnp.einsum('bim,mhd->bhid', x, wk)
        v = jnp.einsum('bim,mhd->bhid', x, wv)
        q = _rmsnorm(q)
        k = _rmsnorm(k)
        q = _rope(q)
        k = _rope(k)
        mult = jnp.asarray(QK_SCALE ** 0.5, q.dtype)
        s = jnp.einsum('bhid,bhjd->bhij', q * mult, k * mult)
        t = s.shape[-1]
        mask = (jnp.arange(t)[:, None] < jnp.arange(t)[None, :]).astype(s.dtype)
        s = s - jnp.asarray(INFTY_APPROX, s.dtype) * mask[None, None]
        p = jax.nn.softmax(s, axis=-1)
        o = jnp.einsum('bhij,bhjd->bhid', p, v)
        return jnp.einsum('bhid,hdm->bim', o, wo)

    def _L0_ffn_ref(x, q_nw, q_nb, q_w1, q_b1, q_w2, q_b2, k_nw, k_nb, k_w1, k_b1, k_w2, k_b2, v_nw, v_nb, v_w1, v_b1, v_w2, v_b2, f_nw, f_nb, f_w1, f_b1, f_w2, f_b2):
        import jax, jax.numpy as jnp
        import numpy as np
        D = 128
        LW = 16
        DEPTH = 8
        NN = 2 ** DEPTH - 1
        NL = 2 ** DEPTH
        B, S = (2, 128)

        def _fff(x, nw, nb, w1, b1, w2, b2, act):
            node = jnp.zeros(x.shape[:2], dtype=jnp.int32)
            for _ in range(DEPTH):
                logit = jnp.einsum('bsd,bsd->bs', x, nw[node]) + nb[node]
                node = 2 * node + 1 + (logit > 0).astype(jnp.int32)
            leaf = node - NN
            h = act(jnp.einsum('bsd,bsdl->bsl', x, w1[leaf]) + b1[leaf])
            return jnp.einsum('bsl,bsld->bsd', h, w2[leaf]) + b2[leaf]

        def _forward(x, q_nw, q_nb, q_w1, q_b1, q_w2, q_b2, k_nw, k_nb, k_w1, k_b1, k_w2, k_b2, v_nw, v_nb, v_w1, v_b1, v_w2, v_b2, f_nw, f_nb, f_w1, f_b1, f_w2, f_b2):
            mu = jnp.mean(x, -1, keepdims=True)
            sd = jnp.std(x, -1, ddof=1, keepdims=True)
            xn = (x - mu) / jnp.sqrt(sd + 1e-05)
            relu = jax.nn.relu
            q = _fff(xn, q_nw, q_nb, q_w1, q_b1, q_w2, q_b2, relu)
            k = _fff(xn, k_nw, k_nb, k_w1, k_b1, k_w2, k_b2, relu)
            v = _fff(xn, v_nw, v_nb, v_w1, v_b1, v_w2, v_b2, relu)
            att = jax.nn.softmax(jnp.einsum('bqd,bkd->bqk', q, k) / jnp.sqrt(jnp.float32(D)), axis=-1)
            y = xn + jnp.einsum('bqk,bkd->bqd', att, v)
            gelu = lambda t: jax.nn.gelu(t, approximate=False)
            return y + _fff(y, f_nw, f_nb, f_w1, f_b1, f_w2, f_b2, gelu)

        def _make_fff_params(key, scale_in, scale_leaf):
            ks = jax.random.split(key, 4)
            nw = jax.random.normal(ks[0], (NN, D), jnp.float32) * scale_in
            nb = jnp.zeros((NN,), jnp.float32)
            w1 = jax.random.normal(ks[1], (NL, D, LW), jnp.float32) * scale_in
            b1 = jax.random.normal(ks[2], (NL, LW), jnp.float32) * 0.01
            w2 = jax.random.normal(ks[3], (NL, LW, D), jnp.float32) * scale_leaf
            b2 = jnp.zeros((NL, D), jnp.float32)
            return (nw, nb, w1, b1, w2, b2)
        return _forward(x, q_nw, q_nb, q_w1, q_b1, q_w2, q_b2, k_nw, k_nb, k_w1, k_b1, k_w2, k_b2, v_nw, v_nb, v_w1, v_b1, v_w2, v_b2, f_nw, f_nb, f_w1, f_b1, f_w2, f_b2)

    def _L1_attn_ref(x, W_in, conv_w, conv_b, W_x, W_dt, b_dt, A_log, D, W_out):
        import jax, jax.numpy as jnp
        import numpy as np
        from jax import lax
        D_MODEL, D_INNER, D_STATE, D_CONV, DT_RANK = (128, 256, 16, 4, 64)
        B, L = (1, 256)

        def _reference_tuple_inner(x, W_in, conv_w, conv_b, W_x, W_dt, b_dt, A_log, D, W_out):
            b, l, dm = x.shape
            di, n = (A_log.shape[0], A_log.shape[1])
            x_and_res = x @ W_in
            xc, res = (x_and_res[..., :di], x_and_res[..., di:])
            k = conv_w.shape[1]
            xp = jnp.pad(xc, ((0, 0), (k - 1, 0), (0, 0)))
            xconv = conv_b
            for j in range(k):
                xconv = xconv + xp[:, j:j + l, :] * conv_w[:, j]
            xs = jax.nn.silu(xconv)
            x_dbl = xs @ W_x
            dt_r = x_dbl[..., :DT_RANK]
            Bm = x_dbl[..., DT_RANK:DT_RANK + n]
            Cm = x_dbl[..., DT_RANK + n:]
            dt = jax.nn.softplus(dt_r @ W_dt + b_dt)
            A = -jnp.exp(A_log)
            dA = jnp.exp(jnp.einsum('bld,dn->bldn', dt, A))
            dBx = jnp.einsum('bld,bln->bldn', dt, Bm) * xs[..., None]

            def step(h, inp):
                dA_t, dBx_t, C_t = inp
                h = dA_t * h + dBx_t
                y = jnp.einsum('bdn,bn->bd', h, C_t)
                return (h, y)
            h0 = jnp.zeros((b, di, n), x.dtype)
            hT, ys = lax.scan(step, h0, (dA.transpose(1, 0, 2, 3), dBx.transpose(1, 0, 2, 3), Cm.transpose(1, 0, 2)))
            y = ys.transpose(1, 0, 2) + xs * D
            y = y * jax.nn.silu(res)
            out = y @ W_out
            return (out, hT)
        return _reference_tuple_inner(x, W_in, conv_w, conv_b, W_x, W_dt, b_dt, A_log, D, W_out)[0]

    def _L1_ffn_ref(x, Wqkv, q_scale, k_scale, Wo, ln_g, ln_b, W1, b1, W2, b2):
        import jax, jax.numpy as jnp
        import numpy as np
        DIM = 128
        DEPTH = 6
        HEADS = 16
        DIM_HEAD = 64
        WINDOW = 32
        INNER = HEADS * DIM_HEAD
        DIM_INNER = int(DIM * 4 * 2 / 3)
        QK_SCALE = 8.0

        def shift_tokens(t):
            a, s = jnp.split(t, 2, -1)
            s = jnp.pad(s, ((0, 0), (1, 0), (0, 0)))[:, :-1]
            return jnp.concatenate([a, s], -1)

        def l2norm(t):
            return t / jnp.maximum(jnp.linalg.norm(t, axis=-1, keepdims=True), 1e-12)

        def rotate_half(x):
            x1, x2 = jnp.split(x, 2, -1)
            return jnp.concatenate([-x2, x1], -1)

        def rotary_tables(n):
            half = jnp.arange(0, DIM_HEAD, 2, dtype=jnp.float32)
            inv_freq = 1.0 / 10000.0 ** (half / DIM_HEAD)
            t = jnp.arange(n, dtype=jnp.float32)
            freqs = t[:, None] * inv_freq[None, :]
            freqs = jnp.concatenate([freqs, freqs], -1)
            base_scale = (half + 0.4 * DIM_HEAD) / (1.4 * DIM_HEAD)
            power = (t - n // 2) / (WINDOW // 2)
            scale = base_scale[None, :] ** power[:, None]
            scale = jnp.concatenate([scale, scale], -1)
            return (freqs, scale)

        def local_attention(q, k, v):
            b, h, n, d = q.shape
            w = WINDOW
            nw = n // w
            bq = q.reshape(b, h, nw, w, d)
            bk = k.reshape(b, h, nw, w, d)
            bv = v.reshape(b, h, nw, w, d)

            def look(t):
                p = jnp.pad(t, ((0, 0), (0, 0), (1, 0), (0, 0), (0, 0)))
                return jnp.concatenate([p[:, :, :nw], p[:, :, 1:]], axis=3)
            bk2, bv2 = (look(bk), look(bv))
            seq = jnp.arange(n).reshape(nw, w)
            seq_p = jnp.pad(seq, ((1, 0), (0, 0)), constant_values=-1)
            jt = jnp.concatenate([seq_p[:nw], seq_p[1:]], axis=1)
            it = seq[:, :, None]
            jb = jt[:, None, :]
            mask = (it < jb) | (it > jb + w) | (jb == -1)
            sim = jnp.einsum('bhwie,bhwje->bhwij', bq, bk2) * QK_SCALE
            sim = jnp.where(mask, -jnp.finfo(sim.dtype).max, sim)
            attn = jax.nn.softmax(sim, -1)
            out = jnp.einsum('bhwij,bhwje->bhwie', attn, bv2)
            return out.reshape(b, h, n, d)

        def attn_layer(x, Wqkv, qs, ksc, Wo):
            b, n, _ = x.shape
            qkv = x @ Wqkv
            q, k, v = jnp.split(qkv, 3, -1)
            sh = lambda t: t.reshape(b, n, HEADS, DIM_HEAD).transpose(0, 2, 1, 3)
            q, k, v = (sh(q), sh(k), sh(v))
            q = l2norm(q) * qs
            k = l2norm(k) * ksc
            freqs, scale = rotary_tables(n)
            cos, sin = (jnp.cos(freqs), jnp.sin(freqs))
            q = q * cos * scale + rotate_half(q) * sin * scale
            inv = 1.0 / scale
            k = k * cos * inv + rotate_half(k) * sin * inv
            out = local_attention(q, k, v)
            out = out.transpose(0, 2, 1, 3).reshape(b, n, INNER)
            return out @ Wo

        def ffn_layer(x, g, bln, W1, b1, W2, b2):
            mu = x.mean(-1, keepdims=True)
            var = ((x - mu) ** 2).mean(-1, keepdims=True)
            xn = (x - mu) / jnp.sqrt(var + 1e-05) * g + bln
            hg = xn @ W1 + b1
            a, gate = jnp.split(hg, 2, -1)
            return a * jax.nn.gelu(gate, approximate=False) @ W2 + b2
        for i in range(DEPTH):
            x = attn_layer(shift_tokens(x), Wqkv[i], q_scale[i], k_scale[i], Wo[i]) + x
            x = ffn_layer(shift_tokens(x), ln_g[i], ln_b[i], W1[i], b1[i], W2[i], b2[i]) + x
        return x
    x = L0_attn_x
    mod = (_silu(L0_c) @ L0_wmod).reshape(L0_c.shape[0], 6, 1, -1)
    sa, ca, ga, sb, cb, gb = (mod[:, 0], mod[:, 1], mod[:, 2], mod[:, 3], mod[:, 4], mod[:, 5])
    ga = (2 * (ga >= 0) - 1) * jnp.maximum(jnp.abs(ga), 0.25)
    gb = (2 * (gb >= 0) - 1) * jnp.maximum(jnp.abs(gb), 0.25)
    h = _layernorm(x, axis=-1) * (1 + ca) + sa
    x = x + ga * _L0_attn_ref(h, L0_attn_wq, L0_attn_wk, L0_attn_wv, L0_attn_wo)
    h = _layernorm(x, axis=-1) * (1 + cb) + sb
    x = x + gb * _L0_ffn_ref(h, L0_ffn_q_nw, L0_ffn_q_nb, L0_ffn_q_w1, L0_ffn_q_b1, L0_ffn_q_w2, L0_ffn_q_b2, L0_ffn_k_nw, L0_ffn_k_nb, L0_ffn_k_w1, L0_ffn_k_b1, L0_ffn_k_w2, L0_ffn_k_b2, L0_ffn_v_nw, L0_ffn_v_nb, L0_ffn_v_w1, L0_ffn_v_b1, L0_ffn_v_w2, L0_ffn_v_b2, L0_ffn_f_nw, L0_ffn_f_nb, L0_ffn_f_w1, L0_ffn_f_b1, L0_ffn_f_w2, L0_ffn_f_b2)
    mod = (_silu(L1_c) @ L1_wmod).reshape(L1_c.shape[0], 6, 1, -1)
    sa, ca, ga, sb, cb, gb = (mod[:, 0], mod[:, 1], mod[:, 2], mod[:, 3], mod[:, 4], mod[:, 5])
    ga = (2 * (ga >= 0) - 1) * jnp.maximum(jnp.abs(ga), 0.25)
    gb = (2 * (gb >= 0) - 1) * jnp.maximum(jnp.abs(gb), 0.25)
    h = _layernorm(x, axis=-1) * (1 + ca) + sa
    x = x + ga * _L1_attn_ref(h, L1_attn_W_in, L1_attn_conv_w, L1_attn_conv_b, L1_attn_W_x, L1_attn_W_dt, L1_attn_b_dt, L1_attn_A_log, L1_attn_D, L1_attn_W_out)
    h = _layernorm(x, axis=-1) * (1 + cb) + sb
    x = x + gb * _L1_ffn_ref(h, L1_ffn_Wqkv, L1_ffn_q_scale, L1_ffn_k_scale, L1_ffn_Wo, L1_ffn_ln_g, L1_ffn_ln_b, L1_ffn_W1, L1_ffn_b1, L1_ffn_W2, L1_ffn_b2)
    return x

_drawn_inputs = setup_inputs


def setup_inputs(seed=0):
    import zlib

    import numpy as np

    out = dict(_drawn_inputs(seed))
    spreads = {'L0_ffn_q_nb': (0.0, 0.1),
     'L0_ffn_q_b2': (0.0, 0.31),
     'L0_ffn_k_nb': (0.0, 0.1),
     'L0_ffn_k_b2': (0.0, 0.351),
     'L0_ffn_v_nb': (0.0, 0.1),
     'L0_ffn_v_b2': (0.0, 0.1),
     'L0_ffn_f_nb': (0.0, 0.1),
     'L0_ffn_f_b2': (0.0, 0.321),
     'L1_attn_D': (1.0, 0.6),
     'L1_ffn_q_scale': (1.0, 0.6),
     'L1_ffn_k_scale': (1.0, 0.6),
     'L1_ffn_ln_g': (1.0, 0.6),
     'L1_ffn_ln_b': (0.0, 0.8),
     'L1_ffn_b1': (0.0, 0.8),
     'L1_ffn_b2': (0.0, 0.723)}
    factors = {'L0_ffn_q_b1': 8.0,
     'L0_ffn_k_b1': 8.0,
     'L0_ffn_v_b1': 7.098,
     'L0_ffn_f_b1': 21.553,
     'L1_attn_conv_b': 8.0,
     'L1_attn_b_dt': 41.444,
     'L1_ffn_W1': 7.968,
     'L1_ffn_W2': 7.835}
    for name, (base, spread) in spreads.items():
        noise = np.random.default_rng([zlib.crc32(name.encode()), seed]).standard_normal(out[name].shape)
        drawn = base * np.exp(spread * noise) if base else spread * noise
        out[name] = jnp.asarray(drawn.astype(out[name].dtype))
    for name, factor in factors.items():
        out[name] = (out[name] * factor).astype(out[name].dtype)
    return out
```

```python
import math

import numpy as np
import concourse.bass as bass
from concourse import mybir
from contextlib import ExitStack

F32 = mybir.dt.float32
BF16 = mybir.dt.bfloat16
ALU = mybir.AluOpType
ACT = mybir.ActivationFunctionType
AX = mybir.AxisListType

NB, T, D = 8, 256, 128
NT = T // 128
H0 = 8
NLEAF, LW, DEPTH = 256, 16, 8
NCH = NLEAF * LW // 128
DI, NS, DTR, KC = 256, 16, 64, 4
L1, H1, E1, W = 6, 16, 64, 32
EH = E1 // 2
FI = int(D * 4 * 2 / 3)
FCH = [(c, min(128, FI - c)) for c in range(0, FI, 128)]
BIG = 1e30
LN_EPS = 1e-5


class Count:

    def __init__(self, sem, per, credit=0):
        self.sem, self.per, self.credit = sem, per, credit

    def at(self, it, k, lag=0):
        return it * self.per + (k + self.credit - lag)


class Banks:

    def __init__(self, nc, ctx):
        self.ps = ctx.enter_context(nc.psum_tensor("ps", [128, 8, 512], F32))
        self.filled = [ctx.enter_context(nc.semaphore(f"filled{b}")) for b in range(8)]
        self.drained = [ctx.enter_context(nc.semaphore(f"drained{b}")) for b in range(8)]
        self.base_filled, self.base_drained = [0] * 8, [0] * 8


class Jobs:

    def __init__(self, banks, plan, iterations):
        self.banks, self.iterations, self.at = banks, iterations, {}
        self.nf, self.nd = [0] * 8, [0] * 8
        for name, b, readers in plan:
            assert name not in self.at
            self.at[name] = (b, self.nf[b] + 1, self.nd[b])
            self.nf[b] += 1
            self.nd[b] += readers

    def out(self, name):
        return self.banks.ps[:, self.at[name][0], :]

    def free(self, it, name):
        b, _, before = self.at[name]
        return self.banks.drained[b], it * self.nd[b] + (self.banks.base_drained[b] + before + 1)

    def filled(self, it, name):
        b, n, _ = self.at[name]
        return self.banks.filled[b], it * self.nf[b] + (self.banks.base_filled[b] + n)

    def sem_filled(self, name):
        return self.banks.filled[self.at[name][0]]

    def sem_drained(self, name):
        return self.banks.drained[self.at[name][0]]

    def close(self):
        for b in range(8):
            self.banks.base_filled[b] += self.iterations * self.nf[b]
            self.banks.base_drained[b] += self.iterations * self.nd[b]


class Core:

    def __init__(self, nc, ctx, dram):
        self.nc, self.ctx, self.dram = nc, ctx, dram
        self.banks = Banks(nc, ctx)
        self.xT = self.sb(ctx, "xT", [128, NB * T])
        self.mod = [self.sb(ctx, f"mod{i}", [128, 6, NB]) for i in range(2)]
        self.mean_w = self.sb(ctx, "mean_w", [128, 128])
        self.ident = self.sb(ctx, "ident", [128, 128])
        self.eps = self.sb(ctx, "eps", [128, 6])
        self.tiny = self.sb(ctx, "tiny", [128, 1])
        self.one = self.sem("one")

    def sb(self, ctx, name, shape, dt=F32):
        return ctx.enter_context(self.nc.sbuf_tensor(name, shape, dt))

    def sem(self, name):
        return self.ctx.enter_context(self.nc.semaphore(name))


EPS_LN, EPS_RMS, EPS_TINY, EPS_HALFLOG, EPS_ONE = range(5)
EPS_VALUES = (LN_EPS, 1e-6, 1e-5, 0.5 * math.log(2.0 ** 16), 1.0)


class Norm:

    def __init__(self, core, jobs, name, cent, sq, rs, centered, squared, scaled):
        self.c, self.jobs, self.name = core, jobs, name
        self.cent, self.sq, self.rs = cent, sq, rs
        self.centered, self.squared, self.scaled = centered, squared, scaled

    def pe_mean(self, pe, it, src):
        pe.wait_ge(*self.jobs.free(it, self.name + "mean"))
        self.c.nc.tensor.matmul(self.jobs.out(self.name + "mean")[:, 0:T], self.c.mean_w[:, :], src,
                                               start=True, stop=True).then_inc(self.jobs.sem_filled(self.name + "mean"), 1)

    def pe_var(self, pe, it, k):
        pe.wait_ge(self.squared.sem, self.squared.at(it, k))
        self.pe_var_ready(pe, it)

    def pe_var_ready(self, pe, it):
        pe.wait_ge(*self.jobs.free(it, self.name + "var"))
        self.c.nc.tensor.matmul(self.jobs.out(self.name + "var")[:, 0:T], self.c.mean_w[:, :],
                                               self.sq[:, :], start=True, stop=True).then_inc(self.jobs.sem_filled(self.name + "var"), 1)

    def dve_center(self, dve, it, src):
        dve.wait_ge(*self.jobs.filled(it, self.name + "mean"))
        self.c.nc.vector.tensor_tensor(self.cent[:, :], src,
                                                         self.jobs.out(self.name + "mean")[:, 0:T],
                                                         ALU.subtract).then_inc(self.jobs.sem_drained(self.name + "mean"), 1)
        dve.drain()
        dve.sem_inc(self.centered.sem, 1)

    def act_square(self, act, it, k=1):
        act.wait_ge(self.centered.sem, self.centered.at(it, k))
        self.c.nc.scalar.activation(self.sq[:, :], self.cent[:, :], ACT.Square).then_inc(self.squared.sem, 1)

    def act_root(self, act, it, k, sample=False):
        self.act_square(act, it, k)
        self.act_rsqrt(act, it, sample)

    def act_rsqrt(self, act, it, sample=False):
        nc, eps = self.c.nc, self.c.eps
        act.wait_ge(*self.jobs.filled(it, self.name + "var"))
        out = self.jobs.out(self.name + "var")[:, 0:T]
        if sample:
            act.wait_ge(self.c.one, 1)
            nc.scalar.activation(self.rs[:, :], out, ACT.Ln, scale=D / (D - 1.0), bias=self.c.tiny[:, 0:1])
            act.drain()
            nc.scalar.activation(self.rs[:, :], self.rs[:, :], ACT.Exp, scale=0.5)
            act.drain()
            nc.scalar.activation(self.rs[:, :], self.rs[:, :], ACT.Ln, bias=eps[:, EPS_TINY:EPS_TINY + 1])
        else:
            nc.scalar.activation(self.rs[:, :], out, ACT.Ln, bias=eps[:, EPS_LN:EPS_LN + 1])
        act.drain()
        last = nc.scalar.activation(self.rs[:, :], self.rs[:, :], ACT.Exp, scale=-0.5)
        last.then_inc(self.jobs.sem_drained(self.name + "var"), 1)
        act.drain()
        act.sem_inc(self.scaled.sem, 1)


def cols(b):
    return bass.ds(b * T, T)


def spread(ap, n, at=1):
    shape = list(ap.shape)
    shape.insert(at, n)
    return ap.unsqueeze(at).broadcast_to(shape)



def prepare(core):
    nc, d = core.nc, core.dram
    with ExitStack() as ctx:
        sb = lambda *a: core.sb(ctx, *a)
        c = sb("c", [128, 2, NB])
        s = sb("s", [128, 2, NB])
        wmod = sb("wmod", [128, 2, 6 * D])
        sign = sb("sign", [128, 2, NB])
        loads, ready, silu, have_one = (core.sem(n) for n in ("prep_loads", "prep_consts", "prep_silu", "prep_mod"))
        jobs = Jobs(core.banks, [("mod0", 0, 1), ("mod1", 1, 1)], 1)
        with nc.Block() as block:
            @block.sync
            def _(sp):
                for i in range(2):
                    sp.dma_start(c[:, i, :], d[f"c{i}"]).then_inc(loads, 16)
                    sp.dma_start(wmod[:, i, :], d[f"wmod{i}"]).then_inc(loads, 16)
                sp.dma_start(core.xT[:, :], d["xT"]).then_inc(loads, 16)
                sp.dma_start(core.ident[:, :], d["ident"]).then_inc(loads, 16)
                sp.wait_ge(loads, 96)

            @block.gpsimd
            def _(pool):
                for b in range(8):
                    pool.sem_inc(core.banks.drained[b], 1)
                pool.sem_inc(core.one, 1)
                nc.gpsimd.memset(core.mean_w[:, :], 1.0 / D)
                for j, v in enumerate(EPS_VALUES):
                    nc.gpsimd.memset(core.eps[:, j:j + 1], v)
                nc.gpsimd.memset(core.tiny[:, :], 1e-19)
                pool.drain()

            @block.scalar
            def _(act):
                act.wait_ge(loads, 96)
                nc.scalar.activation(s[:, :, :], c[:, :, :], ACT.Silu).then_inc(silu, 1)

            @block.tensor
            def _(pe):
                pe.wait_ge(silu, 1)
                for i in range(2):
                    pe.wait_ge(*jobs.free(0, f"mod{i}"))
                    for j in range(6):
                        last = nc.tensor.matmul(jobs.out(f"mod{i}")[:, j * NB:(j + 1) * NB],
                                                wmod[:, i, j * D:(j + 1) * D], s[:, i, :], start=True, stop=True)
                    last.then_inc(jobs.sem_filled(f"mod{i}"), 1)

            @block.vector
            def _(dve):
                for i in range(2):
                    m = core.mod[i]
                    dve.wait_ge(*jobs.filled(0, f"mod{i}"))
                    nc.vector.tensor_copy(m[:, :, :].rearrange("p a b -> p (a b)"),
                                                       jobs.out(f"mod{i}")[:, 0:6 * NB]).then_inc(jobs.sem_drained(f"mod{i}"), 1)
                    dve.drain()
                    for j in (1, 4):
                        nc.vector.tensor_scalar(m[:, j, :], m[:, j, :], 1.0, None, ALU.add)
                    for j in (2, 5):
                        nc.vector.tensor_scalar(sign[:, j // 3, :], m[:, j, :], 0.0, 2.0, ALU.is_ge, ALU.mult)
                        dve.drain()
                        nc.vector.scalar_tensor_tensor(m[:, j, :], m[:, j, :], -1.0, m[:, j, :], ALU.mult, ALU.max)
                        dve.drain()
                        nc.vector.tensor_scalar(m[:, j, :], m[:, j, :], 0.25, None, ALU.max)
                        dve.drain()
                        nc.vector.scalar_tensor_tensor(m[:, j, :], sign[:, j // 3, :], -1.0, m[:, j, :],
                                                       ALU.add, ALU.mult)
                        dve.drain()
        jobs.close()



def attention0(core):
    nc, d = core.nc, core.dram
    with ExitStack() as ctx:
        sb = lambda *a: core.sb(ctx, *a)
        wq, wk, wv, wo = (sb(n, [128, H0 * D]) for n in ("wq0", "wk0", "wv0", "wo0"))
        cos, sin = sb("cos0", [128, 2, T]), sb("sin0", [128, 2, T])
        tri = sb("tri0", [128, 2, 128])
        ones = sb("ones0", [128, 128])
        h = sb("h0", [128, T])
        cent, lsq, lrs = sb("cent0", [128, T]), sb("lsq0", [128, T]), sb("lrs0", [128, T])
        V = sb("V0", [128, NT, H0 * D])
        sq, a, bq, c, rq, qk = (sb(n + "0", [128, 2, 2 * T]) for n in ("sq", "a", "bq", "cq", "rq", "qkn"))
        P = sb("P0", [128, 2, 384])
        rd = sb("rd0", [128, 2, T])
        oT = sb("oT0", [128, H0, T])
        loads = core.sem("l0a_loads")
        S = lambda n, per, credit=0: Count(core.sem("l0a_" + n), per, credit)
        centered, squared, scaled, h_ready = S("centered", 1), S("squared", 1), S("scaled", 1), S("h_ready", 1)
        V_ready, sq_ready, ab_ready, c_ready = S("V_ready", 4), S("sq_ready", H0), S("ab_ready", H0), S("c_ready", H0)
        rq_ready, qkn_ready = S("rq_ready", H0), S("qkn_ready", H0, 2)
        P_ready, P_masked = S("P_ready", H0, 2), S("P_masked", H0)
        rd_ready, o_ready = S("rd_ready", H0), S("o_ready", H0, 2)
        plan = [("mean", 6, 1), ("var", 7, 1)] + [(f"V{j}", j % 4, 1) for j in range(4)]
        for s in range(H0 + 3):
            if s < H0:
                plan.append((f"qk{s}", s % 2, 1))
            if 0 <= s - 1 < H0:
                plan.append((f"ss{s - 1}", 2, 1))
            if 0 <= s - 2 < H0:
                plan.append((f"S{s - 2}", 3 + s % 2, 1))
            if 0 <= s - 3 < H0:
                plan.append((f"OD{s - 3}", 5 + s % 2, 1))
        plan.append(("WO", 7, 1))
        jobs = Jobs(core.banks, plan, NB)
        norm = Norm(core, jobs, "", cent, lsq, lrs, centered, squared, scaled)
        x = core.xT

        with nc.Block() as block:
            @block.sync
            def _(sp):
                for dst, n in ((wq, "wq"), (wk, "wk"), (wv, "wv"), (wo, "wo0")):
                    sp.dma_start(dst[:, :], d[n]).then_inc(loads, 16)
                for i in range(2):
                    sp.dma_start(cos[:, i, :], d["cos0"]).then_inc(loads, 16)
                    sp.dma_start(sin[:, i, :], d["sin0"]).then_inc(loads, 16)
                    sp.dma_start(tri[:, i, :], d["tri"]).then_inc(loads, 16)
                core.routed.load(core, sp)
                sp.wait_ge(loads, 160)

            @block.tensor
            def _(pe):
                pe.wait_ge(loads, 160)
                with pe.Fori(0, NB) as b:
                    norm.pe_mean(pe, b, x[:, cols(b)])
                    norm.pe_var(pe, b, 1)
                    pe.wait_ge(h_ready.sem, h_ready.at(b, 1))
                    for t in range(NT):
                        for j in range(2):
                            n = f"V{2 * t + j}"
                            pe.wait_ge(*jobs.free(b, n))
                            nc.tensor.matmul(jobs.out(n), h[:, t * 128:(t + 1) * 128],
                                                       wv[:, j * 512:(j + 1) * 512], start=True, stop=True).then_inc(jobs.sem_filled(n), 1)
                    for s in range(H0 + 3):
                        if s < H0:
                            n = f"qk{s}"
                            pe.wait_ge(*jobs.free(b, n))
                            nc.tensor.matmul(jobs.out(n)[:, 0:T], wq[:, s * D:(s + 1) * D], h[:, :], start=True, stop=True)
                            nc.tensor.matmul(jobs.out(n)[:, T:2 * T], wk[:, s * D:(s + 1) * D], h[:, :],
                                                       start=True, stop=True).then_inc(jobs.sem_filled(n), 1)
                        if 0 <= s - 1 < H0:
                            n, i = f"ss{s - 1}", s - 1
                            pe.wait_ge(sq_ready.sem, sq_ready.at(b, i + 1))
                            pe.wait_ge(*jobs.free(b, n))
                            nc.tensor.matmul(jobs.out(n), core.mean_w[:, :], sq[:, i % 2, :],
                                                       start=True, stop=True).then_inc(jobs.sem_filled(n), 1)
                        if 0 <= s - 2 < H0:
                            n, i = f"S{s - 2}", s - 2
                            pe.wait_ge(qkn_ready.sem, qkn_ready.at(b, i + 1))
                            pe.wait_ge(*jobs.free(b, n))
                            q = qk[:, i % 2, :]
                            nc.tensor.matmul(jobs.out(n)[:, 0:T], q[:, T:T + 128], q[:, 0:T], start=True, stop=True)
                            nc.tensor.matmul(jobs.out(n)[:, T:T + 128], q[:, T + 128:2 * T], q[:, 128:T],
                                                       start=True, stop=True).then_inc(jobs.sem_filled(n), 1)
                        if 0 <= s - 3 < H0:
                            n, i = f"OD{s - 3}", s - 3
                            pe.wait_ge(V_ready.sem, V_ready.at(b, 4))
                            pe.wait_ge(P_masked.sem, P_masked.at(b, i + 1))
                            pe.wait_ge(*jobs.free(b, n))
                            for k, (w0, w1) in enumerate(((V[:, 0, i * D:(i + 1) * D], V[:, 1, i * D:(i + 1) * D]),
                                                          (ones[:, :], ones[:, :]))):
                                o = jobs.out(n)[:, k * T:(k + 1) * T]
                                nc.tensor.matmul(o[:, 0:128], w0, P[:, i % 2, 0:128], start=True, stop=True)
                                nc.tensor.matmul(o[:, 128:T], w0, P[:, i % 2, 128:T], start=True, stop=False)
                                last = nc.tensor.matmul(o[:, 128:T], w1, P[:, i % 2, T:384], start=False, stop=True)
                            last.then_inc(jobs.sem_filled(n), 1)
                    pe.wait_ge(o_ready.sem, o_ready.at(b, H0))
                    pe.wait_ge(*jobs.free(b, "WO"))
                    for i in range(H0):
                        last = nc.tensor.matmul(jobs.out("WO")[:, 0:T], wo[:, i * D:(i + 1) * D], oT[:, i, :],
                                                start=(i == 0), stop=(i == H0 - 1))
                    last.then_inc(jobs.sem_filled("WO"), 1)

            @block.scalar
            def _(act):
                act.wait_ge(loads, 160)
                act.preload_act_table_set("natural_log_exp_and_others")
                with act.Fori(0, NB) as b:
                    norm.act_root(act, b, 1)
                    for j in range(4):
                        act.wait_ge(*jobs.filled(b, f"V{j}"))
                        last = nc.scalar.activation(V[:, j // 2, (j % 2) * 512:(j % 2 + 1) * 512], jobs.out(f"V{j}"), ACT.Copy)
                        last.then_inc(jobs.sem_drained(f"V{j}"), 1)
                        act.drain()
                        act.sem_inc(V_ready.sem, 1)
                    for s in range(H0 + 3):
                        if s < H0:
                            act.wait_ge(*jobs.filled(b, f"qk{s}"))
                            nc.scalar.activation(sq[:, s % 2, :], jobs.out(f"qk{s}"), ACT.Square)
                            act.drain()
                            act.sem_inc(sq_ready.sem, 1)
                        if 0 <= s - 1 < H0:
                            i = s - 1
                            act.wait_ge(*jobs.filled(b, f"ss{i}"))
                            act.wait_ge(qkn_ready.sem, qkn_ready.at(b, i + 1, 2))
                            act.wait_ge(core.one, 1)
                            nc.scalar.activation(rq[:, i % 2, :], jobs.out(f"ss{i}"), ACT.Ln,
                                                              bias=core.eps[:, EPS_RMS:EPS_RMS + 1]).then_inc(jobs.sem_drained(f"ss{i}"), 1)
                            act.drain()
                            nc.scalar.activation(rq[:, i % 2, :], rq[:, i % 2, :], ACT.Exp, scale=-0.5)\
                                .then_inc(rq_ready.sem, 1)
                            act.drain()
                        if 0 <= s - 2 < H0:
                            i = s - 2
                            act.wait_ge(*jobs.filled(b, f"S{i}"))
                            nc.scalar.activation(P[:, i % 2, :], jobs.out(f"S{i}")[:, 0:384], ACT.Exp,
                                                              scale=1.0 / D).then_inc(jobs.sem_drained(f"S{i}"), 1)
                            act.drain()
                            act.sem_inc(P_ready.sem, 1)
                        if 0 <= s - 3 < H0:
                            i = s - 3
                            act.wait_ge(*jobs.filled(b, f"OD{i}"))
                            act.wait_ge(o_ready.sem, o_ready.at(b, i + 1, 2))
                            act.wait_ge(core.one, 1)
                            nc.scalar.activation(rd[:, i % 2, :], jobs.out(f"OD{i}")[:, T:2 * T], ACT.Ln)
                            act.drain()
                            nc.scalar.activation(rd[:, i % 2, :], rd[:, i % 2, :], ACT.Exp, scale=-1.0)\
                                .then_inc(rd_ready.sem, 1)
                            act.drain()

            @block.gpsimd
            def _(pool):
                nc.gpsimd.memset(ones[:, :], 1.0)
                pool.drain()
                pool.wait_ge(loads, 160)
                pool.sem_inc(P_ready.sem, P_ready.credit)
                with pool.Fori(0, NB) as b:
                    for s in range(H0 + 2):
                        if s < H0:
                            pool.wait_ge(ab_ready.sem, ab_ready.at(b, s + 1))
                            pool.wait_ge(qkn_ready.sem, qkn_ready.at(b, s + 1, 2))
                            nc.gpsimd.tensor_tensor(c[:, s % 2, :], a[:, s % 2, :], bq[:, s % 2, :], ALU.add)\
                                .then_inc(c_ready.sem, 1)
                        if 0 <= s - 2 < H0:
                            i = s - 2
                            pool.wait_ge(P_ready.sem, P_ready.at(b, i + 1))
                            p = P[:, i % 2, :].rearrange("p (n q) -> p n q", q=128)[:, 0:3:2, :]
                            nc.gpsimd.tensor_tensor(p, p, tri[:, :, :], ALU.mult).then_inc(P_masked.sem, 1)
                    pool.drain()

            @block.vector
            def _(dve):
                dve.wait_ge(loads, 160)
                dve.sem_inc(qkn_ready.sem, qkn_ready.credit)
                dve.sem_inc(o_ready.sem, o_ready.credit)
                with dve.Fori(0, NB) as b:
                    norm.dve_center(dve, b, x[:, cols(b)])
                    dve.wait_ge(scaled.sem, scaled.at(b, 1))
                    nc.vector.tensor_tensor(cent[:, :], cent[:, :], lrs[:, :], ALU.mult)
                    dve.drain()
                    nc.vector.tensor_scalar(h[:, :], cent[:, :], core.mod[0][:, 1, bass.ds(b, 1)],
                                            core.mod[0][:, 0, bass.ds(b, 1)], ALU.mult, ALU.add)\
                        .then_inc(h_ready.sem, 1)
                    dve.drain()
                    for s in range(H0 + 3):
                        if s < H0:
                            dve.wait_ge(*jobs.filled(b, f"qk{s}"))
                            dve.wait_ge(sq_ready.sem, sq_ready.at(b, s + 1))
                            o = jobs.out(f"qk{s}")
                            cs = cos[:, :, :].rearrange("p a b -> p (a b)")
                            sn = sin[:, :, :].rearrange("p a b -> p (a b)")
                            nc.vector.tensor_tensor(a[:, s % 2, :], o, cs, ALU.mult)
                            nc.vector.tensor_tensor(bq[0:64, s % 2, :], o[64:128, :], sn[0:64, :], ALU.mult)
                            nc.vector.tensor_tensor(bq[64:128, s % 2, :], o[0:64, :], sn[64:128, :],
                                                                 ALU.mult).then_inc(jobs.sem_drained(f"qk{s}"), 1)
                            dve.drain()
                            dve.sem_inc(ab_ready.sem, 1)
                        if 0 <= s - 1 < H0:
                            i = s - 1
                            dve.wait_ge(c_ready.sem, c_ready.at(b, i + 1))
                            dve.wait_ge(rq_ready.sem, rq_ready.at(b, i + 1))
                            dve.wait_ge(P_ready.sem, P_ready.at(b, i + 1, 2))
                            nc.vector.tensor_tensor(qk[:, i % 2, :], c[:, i % 2, :], rq[:, i % 2, :], ALU.mult)\
                                .then_inc(qkn_ready.sem, 1)
                        if 0 <= s - 3 < H0:
                            i = s - 3
                            dve.wait_ge(*jobs.filled(b, f"OD{i}"))
                            dve.wait_ge(rd_ready.sem, rd_ready.at(b, i + 1))
                            last = nc.vector.tensor_tensor(oT[:, i, :], jobs.out(f"OD{i}")[:, 0:T], rd[:, i % 2, :], ALU.mult)
                            last.then_inc(jobs.sem_drained(f"OD{i}"), 1)
                            dve.drain()
                            dve.sem_inc(o_ready.sem, 1)
                    dve.wait_ge(*jobs.filled(b, "WO"))
                    nc.vector.scalar_tensor_tensor(x[:, cols(b)], jobs.out("WO")[:, 0:T],
                                                                core.mod[0][:, 2, bass.ds(b, 1)], x[:, cols(b)],
                                                                ALU.mult, ALU.add).then_inc(jobs.sem_drained("WO"), 1)
                    dve.drain()
        jobs.close()



NETS = ("q", "k", "v", "f")


class Routed:

    def __init__(self, core, ctx, nets):
        sb = lambda *a: core.sb(ctx, *a)
        self.nets = nets
        self.nw = [sb(f"nw_{n}", [128, NLEAF]) for n in nets]
        self.nb = [sb(f"nb_{n}", [1, NLEAF]) for n in nets]
        self.w1 = [sb(f"w1_{n}", [128, NCH * 128]) for n in nets]
        self.b1 = [sb(f"b1_{n}", [128, NCH]) for n in nets]
        self.w2 = [sb(f"w2_{n}", [128, NCH * D]) for n in nets]
        self.b2 = [sb(f"b2_{n}", [128, 2 * D]) for n in nets]
        self.loads = core.sem(f"loads_{nets}")
        self.total = 16 * 6 * len(nets)

    def load(self, core, sp):
        for i, n in enumerate(self.nets):
            for part in ("nw", "nb", "w1", "b1", "w2", "b2"):
                dst = {"nw": self.nw, "nb": self.nb, "w1": self.w1, "b1": self.b1, "w2": self.w2, "b2": self.b2}[part][i]
                sp.dma_start(dst[:, :], core.dram[f"{n}_{part}"]).then_inc(self.loads, 16)


def routed0(core):
    nc, R = core.nc, core.routed
    G = 3 * NT
    NP = NCH // 2
    net_of = lambda i: R if i < 3 else F
    with ExitStack() as ctx:
        sb = lambda *a: core.sb(ctx, *a)
        F = Routed(core, ctx, "f")
        h, xn, yT = (sb(n, [128, T]) for n in ("h1", "xn1", "yT1"))
        cent, lsq, lrs = sb("cent1", [128, T]), sb("lsq1", [128, T]), sb("lrs1", [128, T])
        rows1 = sb("rows1", [1, 128])
        expand = sb("expand", [128, 16 * 128], BF16)
        bits, pa, pb = (sb(n, [128, G, NLEAF]) for n in ("bits", "path_a", "path_b"))
        ohT = sb("ohT", [128, 3, 2 * T])
        mask = sb("leafmask", [128, 3, 2 * T], BF16)
        hid = sb("hid", [128, 4, 2 * T])
        qkv = sb("qkv1", [128, 3, T])
        V = sb("V1", [128, T])
        P, PT = sb("P1", [128, NT, T]), sb("PT1", [128, NT, T])
        mx, sm, rsm = (sb(n, [128, NT]) for n in ("mx1", "sm1", "rsm1"))
        S = lambda n, per, credit=0: Count(core.sem("l0f_" + n), per, credit)
        centered, squared, scaled = S("centered", 2), S("squared", 2), S("scaled", 2)
        h_ready, xn_ready, oh_ready, mask_ready, oht_ready = S("h_ready", 1), S("xn_ready", 1), S("onehot", 2), S("mask", 4), S("ohT", 4)
        hid_act, hid_dve, hid_used = S("hid_act", 4 * NP // 2), S("hid_dve", 4 * NP // 2), S("hid_used", 4 * NP, 4)
        qkv_ready, V_ready, mx_ready, e_ready, P_ready, PT_ready, y_ready = (
            S("qkv", 3), S("V", 1), S("max", 1), S("exps", 1), S("P", 1), S("PT", 1), S("y", 1))
        consts = S("consts", 1)
        plan = [("mean", 6, 1), ("var", 7, 1), ("xmean", 6, 1), ("xvar", 7, 1)]
        plan += [(f"R{i}", 6 + i % 2, 1) for i in range(3)] + [(f"T{i}", 6 + (i + 1) % 2, 1) for i in range(3)]
        ring = 0

        def net_plan(i):
            nonlocal ring
            out = [(f"A{i}", 4 + i % 2, 1)]
            for p in range(NP):
                out.append((f"H{i}.{p}", ring % 4, 1))
                ring += 1
            return out
        for i in range(3):
            plan += net_plan(i)
        plan += [("Vt", 6, 1), ("S", 7, 1), ("PT", 6, 1), ("AV", 7, 1), ("R3", 6, 1), ("T3", 7, 1)] + net_plan(3)
        jobs = Jobs(core.banks, plan, NB)
        args = (cent, lsq, lrs, centered, squared, scaled)
        norm, xnorm = Norm(core, jobs, "", *args), Norm(core, jobs, "x", *args)
        x = core.xT

        with nc.Block() as block:
            @block.sync
            def _(sp):
                F.load(core, sp)

            @block.tensor
            def _(pe):
                pe.wait_ge(R.loads, R.total)
                pe.wait_ge(consts.sem, 1)
                pe.sem_inc(hid_used.sem, hid_used.credit)

                def route(b, i, src):
                    pe.wait_ge(*jobs.free(b, f"R{i}"))
                    for t in range(NT):
                        o = jobs.out(f"R{i}")[:, t * NLEAF:(t + 1) * NLEAF]
                        nc.tensor.matmul(o, src[:, t * 128:(t + 1) * 128], net_of(i).nw[i % 3][:, :], start=True, stop=False)
                        last = nc.tensor.matmul(o, rows1[:, :], net_of(i).nb[i % 3][:, :], start=False, stop=True)
                    last.then_inc(jobs.sem_filled(f"R{i}"), 1)

                def turn(b, i, g):
                    pe.wait_ge(*jobs.free(b, f"T{i}"))
                    for lt in range(2):
                        for t in range(NT):
                            last = nc.tensor.transpose(jobs.out(f"T{i}")[:, lt * T + t * 128:lt * T + (t + 1) * 128],
                                                       pb[:, g + t, lt * 128:(lt + 1) * 128], core.ident[:, :])
                    last.then_inc(jobs.sem_filled(f"T{i}"), 1)

                def net(b, i, src):
                    k = i % 3
                    pe.wait_ge(mask_ready.sem, mask_ready.at(b, i + 1))
                    pe.wait_ge(oht_ready.sem, oht_ready.at(b, i + 1))
                    acc = jobs.out(f"A{i}")[:, 0:T]
                    pe.wait_ge(*jobs.free(b, f"A{i}"))
                    for p in range(NP + 1):
                        if p < NP:
                            n = f"H{i}.{p}"
                            pe.wait_ge(*jobs.free(b, n))
                            for c in (2 * p, 2 * p + 1):
                                o = jobs.out(n)[:, (c % 2) * T:(c % 2 + 1) * T]
                                lt = c // 16
                                nc.tensor.matmul(o, expand[:, (c % 16) * 128:(c % 16 + 1) * 128],
                                                 mask[:, k, lt * T:(lt + 1) * T], start=True, stop=False)
                                last = nc.tensor.matmul(o, net_of(i).w1[i % 3][:, c * 128:(c + 1) * 128], src[:, :],
                                                        start=False, stop=True)
                            last.then_inc(jobs.sem_filled(n), 1)
                        if p == 0:
                            for lt in range(2):
                                nc.tensor.matmul(acc, net_of(i).b2[i % 3][:, lt * D:(lt + 1) * D], ohT[:, k, lt * T:(lt + 1) * T],
                                                 start=(lt == 0), stop=False)
                        else:
                            m = p - 1
                            made = hid_act if m % 2 == 0 else hid_dve
                            pe.wait_ge(made.sem, made.at(b, i * (NP // 2) + m // 2 + 1))
                            for c in (2 * m, 2 * m + 1):
                                last = nc.tensor.matmul(acc, net_of(i).w2[i % 3][:, c * D:(c + 1) * D],
                                                        hid[:, m % 4, (c % 2) * T:(c % 2 + 1) * T],
                                                        start=False, stop=(c == NCH - 1))
                            if m < NP - 1:
                                last.then_inc(hid_used.sem, 1)
                    last.then_inc(jobs.sem_filled(f"A{i}"), 1)
                    pe.sem_inc(hid_used.sem, 1)

                with pe.Fori(0, NB) as b:
                    norm.pe_mean(pe, b, x[:, cols(b)])
                    norm.pe_var(pe, b, 1)
                    pe.wait_ge(h_ready.sem, h_ready.at(b, 1))
                    xnorm.pe_mean(pe, b, h[:, :])
                    xnorm.pe_var(pe, b, 2)
                    pe.wait_ge(xn_ready.sem, xn_ready.at(b, 1))
                    for i in range(3):
                        route(b, i, xn)
                    pe.wait_ge(oh_ready.sem, oh_ready.at(b, 1))
                    for i in range(3):
                        turn(b, i, i * NT)
                    for i in range(3):
                        net(b, i, xn)
                    pe.wait_ge(qkv_ready.sem, qkv_ready.at(b, 3))
                    pe.wait_ge(*jobs.free(b, "Vt"))
                    for t in range(NT):
                        last = nc.tensor.transpose(jobs.out("Vt")[:, t * 128:(t + 1) * 128],
                                                   qkv[:, 2, t * 128:(t + 1) * 128], core.ident[:, :])
                    last.then_inc(jobs.sem_filled("Vt"), 1)
                    pe.wait_ge(*jobs.free(b, "S"))
                    for t in range(NT):
                        last = nc.tensor.matmul(jobs.out("S")[:, t * T:(t + 1) * T], qkv[:, 0, t * 128:(t + 1) * 128],
                                                qkv[:, 1, :], start=True, stop=True)
                    last.then_inc(jobs.sem_filled("S"), 1)
                    pe.wait_ge(P_ready.sem, P_ready.at(b, 1))
                    pe.wait_ge(*jobs.free(b, "PT"))
                    for kt in range(NT):
                        for t in range(NT):
                            last = nc.tensor.transpose(jobs.out("PT")[:, kt * T + t * 128:kt * T + (t + 1) * 128],
                                                       P[:, t, kt * 128:(kt + 1) * 128], core.ident[:, :])
                    last.then_inc(jobs.sem_filled("PT"), 1)
                    pe.wait_ge(PT_ready.sem, PT_ready.at(b, 1))
                    pe.wait_ge(V_ready.sem, V_ready.at(b, 1))
                    pe.wait_ge(*jobs.free(b, "AV"))
                    for kt in range(NT):
                        last = nc.tensor.matmul(jobs.out("AV")[:, 0:T], V[:, kt * 128:(kt + 1) * 128], PT[:, kt, :],
                                                start=(kt == 0), stop=(kt == NT - 1))
                    last.then_inc(jobs.sem_filled("AV"), 1)
                    pe.wait_ge(y_ready.sem, y_ready.at(b, 1))
                    pe.wait_ge(F.loads, F.total)
                    route(b, 3, yT)
                    pe.wait_ge(oh_ready.sem, oh_ready.at(b, 2))
                    turn(b, 3, 0)
                    net(b, 3, yT)

            @block.scalar
            def _(act):
                act.wait_ge(R.loads, R.total)
                act.preload_act_table_set("natural_log_exp_and_others")

                def hidden(b, i, func, pairs):
                    for p in pairs:
                        n = f"H{i}.{p}"
                        act.wait_ge(hid_used.sem, hid_used.at(b, i * NP + p + 1, 4))
                        act.wait_ge(*jobs.filled(b, n))
                        for c in (2 * p, 2 * p + 1):
                            last = nc.scalar.activation(hid[:, p % 4, (c % 2) * T:(c % 2 + 1) * T],
                                                        jobs.out(n)[:, (c % 2) * T:(c % 2 + 1) * T], func,
                                                        bias=net_of(i).b1[i % 3][:, c:c + 1])
                        last.then_inc(jobs.sem_drained(n), 1)
                        act.drain()
                        act.sem_inc((hid_act if p % 2 == 0 else hid_dve).sem, 1)

                with act.Fori(0, NB) as b:
                    norm.act_root(act, b, 1)
                    xnorm.act_root(act, b, 2, sample=True)
                    for i in range(3):
                        act.wait_ge(*jobs.filled(b, f"T{i}"))
                        nc.scalar.activation(mask[:, i, :], jobs.out(f"T{i}"), ACT.Copy, scale=BIG, bias=-BIG).then_inc(jobs.sem_drained(f"T{i}"), 1)
                        act.drain()
                        act.sem_inc(mask_ready.sem, 1)
                    for i in range(3):
                        hidden(b, i, ACT.Relu, range(0, NP, 2))
                        act.wait_ge(*jobs.filled(b, f"A{i}"))
                        nc.scalar.activation(qkv[:, i, :], jobs.out(f"A{i}")[:, 0:T], ACT.Copy).then_inc(jobs.sem_drained(f"A{i}"), 1)
                        act.drain()
                        act.sem_inc(qkv_ready.sem, 1)
                    act.wait_ge(*jobs.filled(b, "Vt"))
                    nc.scalar.activation(V[:, :], jobs.out("Vt")[:, 0:T], ACT.Copy).then_inc(jobs.sem_drained("Vt"), 1)
                    act.drain()
                    act.sem_inc(V_ready.sem, 1)
                    act.wait_ge(mx_ready.sem, mx_ready.at(b, 1))
                    for t in range(NT):
                        last = nc.scalar.activation(P[:, t, :], jobs.out("S")[:, t * T:(t + 1) * T], ACT.Exp,
                                                    scale=1.0 / math.sqrt(D), bias=mx[:, t:t + 1], accum_out=sm[:, t:t + 1])
                    last.then_inc(jobs.sem_drained("S"), 1)
                    act.drain()
                    act.sem_inc(e_ready.sem, 1)
                    act.wait_ge(*jobs.filled(b, "PT"))
                    nc.scalar.activation(PT[:, :, :].rearrange("p a b -> p (a b)"), jobs.out("PT"), ACT.Copy).then_inc(jobs.sem_drained("PT"), 1)
                    act.drain()
                    act.sem_inc(PT_ready.sem, 1)
                    act.wait_ge(*jobs.filled(b, "T3"))
                    nc.scalar.activation(mask[:, 0, :], jobs.out("T3"), ACT.Copy, scale=BIG, bias=-BIG).then_inc(jobs.sem_drained("T3"), 1)
                    act.drain()
                    act.sem_inc(mask_ready.sem, 1)
                    act.wait_ge(F.loads, F.total)
                    hidden(b, 3, ACT.Gelu, range(NP))

            @block.gpsimd
            def _(pool):
                nc.gpsimd.memset(expand[:, :], 1.0)
                nc.gpsimd.memset(rows1[:, :], 1.0)
                pool.drain()
                nc.gpsimd.affine_select(out=expand[:, :], in_=expand[:, :], compare_op=ALU.is_ge, fill=0.0, base=0,
                                        pattern=[[1, 16 * 128]], channel_multiplier=-LW)
                pool.drain()
                nc.gpsimd.affine_select(out=expand[:, :], in_=expand[:, :], compare_op=ALU.is_ge, fill=0.0, base=LW - 1,
                                        pattern=[[-1, 16 * 128]], channel_multiplier=LW)
                pool.drain()
                pool.sem_inc(consts.sem, 1)

            @block.vector
            def _(dve):
                dve.wait_ge(R.loads, R.total)

                def decide(b, ids, g):
                    for i in ids:
                        dve.wait_ge(*jobs.filled(b, f"R{i}"))
                        k = (i % 3) * NT
                        nc.vector.tensor_scalar(bits[:, k:k + NT, :].rearrange("p a b -> p (a b)"),
                                                             jobs.out(f"R{i}"), 0.0, None, ALU.is_gt).then_inc(jobs.sem_drained(f"R{i}"), 1)
                    dve.drain()
                    path = [pa, pb]
                    two = lambda t, n: t[:, 0:g, 0:2 * n].rearrange("p g (n two) -> p g n two", two=2)
                    nc.vector.tensor_copy(two(pa, 1)[:, :, :, 1], bits[:, 0:g, 0:1])
                    nc.vector.tensor_scalar(two(pa, 1)[:, :, :, 0], bits[:, 0:g, 0:1], -1.0, 1.0, ALU.mult, ALU.add)
                    dve.drain()
                    for lv in range(1, DEPTH):
                        n = 2 ** lv
                        src, dst = path[(lv + 1) % 2][:, 0:g, 0:n], two(path[lv % 2], n)
                        nc.vector.tensor_tensor(dst[:, :, :, 1], src, bits[:, 0:g, n - 1:2 * n - 1], ALU.mult)
                        dve.drain()
                        nc.vector.tensor_tensor(dst[:, :, :, 0], src, dst[:, :, :, 1], ALU.subtract)
                        dve.drain()
                    dve.sem_inc(oh_ready.sem, 1)

                def onehots(b, i):
                    dve.wait_ge(mask_ready.sem, mask_ready.at(b, i + 1))
                    nc.vector.tensor_scalar(ohT[:, i % 3, :], mask[:, i % 3, :], 0.0, None, ALU.is_equal)
                    dve.drain()
                    dve.sem_inc(oht_ready.sem, 1)

                def hidden(b, i):
                    for p in range(1, NP, 2):
                        n = f"H{i}.{p}"
                        dve.wait_ge(hid_used.sem, hid_used.at(b, i * NP + p + 1, 4))
                        dve.wait_ge(*jobs.filled(b, n))
                        for c in (2 * p, 2 * p + 1):
                            last = nc.vector.tensor_scalar(hid[:, p % 4, (c % 2) * T:(c % 2 + 1) * T],
                                                           jobs.out(n)[:, (c % 2) * T:(c % 2 + 1) * T],
                                                           net_of(i).b1[i % 3][:, c:c + 1], 0.0, ALU.add, ALU.max)
                        last.then_inc(jobs.sem_drained(n), 1)
                        dve.drain()
                        dve.sem_inc(hid_dve.sem, 1)

                with dve.Fori(0, NB) as b:
                    norm.dve_center(dve, b, x[:, cols(b)])
                    dve.wait_ge(scaled.sem, scaled.at(b, 1))
                    nc.vector.tensor_tensor(cent[:, :], cent[:, :], lrs[:, :], ALU.mult)
                    dve.drain()
                    nc.vector.tensor_scalar(h[:, :], cent[:, :], core.mod[0][:, 4, bass.ds(b, 1)],
                                            core.mod[0][:, 3, bass.ds(b, 1)], ALU.mult, ALU.add)
                    dve.drain()
                    dve.sem_inc(h_ready.sem, 1)
                    xnorm.dve_center(dve, b, h[:, :])
                    dve.wait_ge(scaled.sem, scaled.at(b, 2))
                    nc.vector.tensor_tensor(xn[:, :], cent[:, :], lrs[:, :], ALU.mult)
                    dve.drain()
                    dve.sem_inc(xn_ready.sem, 1)
                    decide(b, range(3), G)
                    for i in range(3):
                        onehots(b, i)
                    for i in range(3):
                        hidden(b, i)
                    dve.wait_ge(*jobs.filled(b, "S"))
                    nc.vector.tensor_reduce(mx[:, :], jobs.out("S").rearrange("p (a b) -> p a b", a=NT), axis=AX.X, op=ALU.max)
                    dve.drain()
                    nc.vector.tensor_scalar(mx[:, :], mx[:, :], -1.0 / math.sqrt(D), None, ALU.mult)
                    dve.drain()
                    dve.sem_inc(mx_ready.sem, 1)
                    dve.wait_ge(e_ready.sem, e_ready.at(b, 1))
                    nc.vector.reciprocal(rsm[:, :], sm[:, :])
                    dve.drain()
                    for t in range(NT):
                        nc.vector.tensor_scalar(P[:, t, :], P[:, t, :], rsm[:, t:t + 1], None, ALU.mult)
                    dve.drain()
                    dve.sem_inc(P_ready.sem, 1)
                    dve.wait_ge(*jobs.filled(b, "AV"))
                    nc.vector.tensor_tensor(yT[:, :], jobs.out("AV")[:, 0:T], xn[:, :], ALU.add).then_inc(jobs.sem_drained("AV"), 1)
                    dve.drain()
                    dve.sem_inc(y_ready.sem, 1)
                    decide(b, (3,), NT)
                    onehots(b, 3)
                    dve.wait_ge(*jobs.filled(b, "A3"))
                    nc.vector.tensor_tensor(cent[:, :], jobs.out("A3")[:, 0:T], yT[:, :], ALU.add).then_inc(jobs.sem_drained("A3"), 1)
                    dve.drain()
                    nc.vector.scalar_tensor_tensor(x[:, cols(b)], cent[:, :], core.mod[0][:, 5, bass.ds(b, 1)],
                                                   x[:, cols(b)], ALU.mult, ALU.add)
                    dve.drain()
        jobs.close()



def mamba1(core):
    nc, d = core.nc, core.dram
    NG = NS // 2
    with ExitStack() as ctx:
        sb = lambda *a: core.sb(ctx, *a)
        win, wx, wdt, wout = sb("win", [128, 2 * DI]), sb("wx", [128, 2, 96]), sb("wdt", [64, DI]), sb("wout", [128, 2, D])
        cw, cb, bdt = sb("convw", [128, 2, KC]), sb("convb", [128, 2]), sb("bdt", [128, 2])
        A, Dp = sb("A", [128, 2, NS]), sb("Dp", [128, 2])
        sel = sb("sel", [96, 2 * NS * 128])
        h = sb("h2", [128, T])
        cent, lsq, lrs = sb("cent2", [128, T]), sb("lsq2", [128, T]), sb("lrs2", [128, T])
        xp = sb("xp", [128, 2, T + KC - 1])
        xc, xs, sres, u, e, dt, du, yy = (sb(n + "2", [128, 2, T]) for n in ("xc", "xs", "sres", "u", "e", "dt", "du", "yy"))
        xdbl = sb("xdbl", [96, T])
        dA, dBx, hs, hC = (sb(n, [128, 2, 2, 2, T]) for n in ("dA", "dBx", "hs", "hC"))
        loads = core.sem("l1a_loads")
        S = lambda n, per, credit=0: Count(core.sem("l1a_" + n), per, credit)
        centered, squared, scaled, h_ready = S("centered", 1), S("squared", 1), S("scaled", 1), S("h_ready", 1)
        xp_ready, conv_ready, xs_ready, xdbl_ready, u_ready, soft_ready = (
            S(n, 1) for n in ("xp", "conv", "xs", "xdbl", "u", "soft"))
        dt_ready, dA_ready, hC_ready, hC_used, yy_ready = (
            S("dt", 1), S("dA", NG), S("hC", NG, 2), S("hC_used", NG, 2), S("yy", 1))
        consts = core.sem("l1a_consts")
        plan = [("mean", 6, 1), ("var", 7, 1), ("X0", 6, 1), ("X1", 7, 1), ("XD", 6, 1), ("DT", 7, 1), ("Y0", 0, 1), ("Y1", 1, 1)]
        for g in range(NG):
            plan += [(f"B{g}", 2 + g % 2, 1), (f"C{g}", 4 + g % 2, 1)]
        plan += [("OUT", 6, 1)]
        jobs = Jobs(core.banks, plan, NB)
        norm = Norm(core, jobs, "", cent, lsq, lrs, centered, squared, scaled)
        x = core.xT
        flat = lambda ap: ap.rearrange("p a b -> p (a b)")

        with nc.Block() as block:
            @block.sync
            def _(sp):
                for dst, n in ((win[:, :], "win"), (wx[:, :, :], "wx"), (wdt[:, :], "wdt"), (wout[:, :, :], "wout"),
                               (cw[:, :, :], "convw"), (cb[:, :], "convb"), (bdt[:, :], "bdt"), (A[:, :, :], "A_log"),
                               (Dp[:, :], "Dp"), (sel[:, :], "sel")):
                    sp.dma_start(dst, d[n]).then_inc(loads, 16)
                sp.wait_ge(loads, 160)

            @block.gpsimd
            def _(pool):
                nc.gpsimd.memset(dA[:, :, :, :, 0:1], 0.0)
                nc.gpsimd.memset(xp[:, :, 0:KC - 1], 0.0)
                pool.drain()
                pool.sem_inc(consts, 1)

            @block.tensor
            def _(pe):
                pe.wait_ge(loads, 160)
                pe.sem_inc(hC_used.sem, hC_used.credit)
                with pe.Fori(0, NB) as b:
                    norm.pe_mean(pe, b, x[:, cols(b)])
                    norm.pe_var(pe, b, 1)
                    pe.wait_ge(h_ready.sem, h_ready.at(b, 1))
                    for i in range(2):
                        pe.wait_ge(*jobs.free(b, f"X{i}"))
                        for k in range(2):
                            last = nc.tensor.matmul(jobs.out(f"X{i}")[:, k * T:(k + 1) * T],
                                                    win[:, (2 * i + k) * 128:(2 * i + k + 1) * 128], h[:, :],
                                                    start=True, stop=True)
                        last.then_inc(jobs.sem_filled(f"X{i}"), 1)
                    pe.wait_ge(xs_ready.sem, xs_ready.at(b, 1))
                    pe.wait_ge(*jobs.free(b, "XD"))
                    for k in range(2):
                        last = nc.tensor.matmul(jobs.out("XD")[0:96, 0:T], wx[:, k, :], xs[:, k, :], start=(k == 0), stop=(k == 1))
                    last.then_inc(jobs.sem_filled("XD"), 1)
                    pe.wait_ge(xdbl_ready.sem, xdbl_ready.at(b, 1))
                    pe.wait_ge(*jobs.free(b, "DT"))
                    for k in range(2):
                        last = nc.tensor.matmul(jobs.out("DT")[:, k * T:(k + 1) * T], wdt[:, k * 128:(k + 1) * 128],
                                                xdbl[0:DTR, :], start=True, stop=True)
                    last.then_inc(jobs.sem_filled("DT"), 1)
                    for g in range(NG + 1):
                        if g < NG:
                            for name, at in ((f"B{g}", 0), (f"C{g}", NS)):
                                pe.wait_ge(*jobs.free(b, name))
                                for j in range(2):
                                    n = at + 2 * g + j
                                    last = nc.tensor.matmul(jobs.out(name)[:, j * T:(j + 1) * T],
                                                            sel[DTR:96, n * 128:(n + 1) * 128], xdbl[DTR:96, :],
                                                            start=True, stop=True)
                                last.then_inc(jobs.sem_filled(name), 1)
                        if g >= 1:
                            i = g - 1
                            pe.wait_ge(hC_ready.sem, hC_ready.at(b, i + 1))
                            for k in range(2):
                                if i == 0:
                                    pe.wait_ge(*jobs.free(b, f"Y{k}"))
                                for j in range(2):
                                    last = nc.tensor.matmul(jobs.out(f"Y{k}")[:, 0:T], core.ident[:, :], hC[:, i % 2, k, j, :],
                                                            start=(i == 0 and j == 0), stop=(i == NG - 1 and j == 1))
                                if i == NG - 1:
                                    last.then_inc(jobs.sem_filled(f"Y{k}"), 1)
                            if i < NG - 1:
                                last.then_inc(hC_used.sem, 1)
                            else:
                                pe.sem_inc(hC_used.sem, 1)
                    pe.wait_ge(yy_ready.sem, yy_ready.at(b, 1))
                    pe.wait_ge(*jobs.free(b, "OUT"))
                    for k in range(2):
                        last = nc.tensor.matmul(jobs.out("OUT")[:, 0:T], wout[:, k, :], yy[:, k, :], start=(k == 0), stop=(k == 1))
                    last.then_inc(jobs.sem_filled("OUT"), 1)

            @block.scalar
            def _(act):
                act.wait_ge(loads, 160)
                act.wait_ge(consts, 1)
                act.preload_act_table_set("natural_log_exp_and_others")
                nc.scalar.activation(flat(A[:, :, :]), flat(A[:, :, :]), ACT.Exp)
                act.drain()
                nc.scalar.activation(flat(A[:, :, :]), flat(A[:, :, :]), ACT.Copy, scale=-1.0)
                act.drain()
                with act.Fori(0, NB) as b:
                    norm.act_root(act, b, 1)
                    act.wait_ge(*jobs.filled(b, "X0"))
                    nc.scalar.activation(xp[:, :, KC - 1:], jobs.out("X0").rearrange("p (a b) -> p a b", a=2), ACT.Copy).then_inc(jobs.sem_drained("X0"), 1)
                    act.drain()
                    act.sem_inc(xp_ready.sem, 1)
                    act.wait_ge(*jobs.filled(b, "X1"))
                    nc.scalar.activation(flat(sres[:, :, :]), jobs.out("X1"), ACT.Silu).then_inc(jobs.sem_drained("X1"), 1)
                    act.wait_ge(conv_ready.sem, conv_ready.at(b, 1))
                    nc.scalar.activation(flat(xs[:, :, :]), flat(xc[:, :, :]), ACT.Silu)
                    act.drain()
                    act.sem_inc(xs_ready.sem, 1)
                    act.preload_act_table_set("natural_log_exp_and_others")
                    act.wait_ge(*jobs.filled(b, "XD"))
                    nc.scalar.activation(xdbl[:, :], jobs.out("XD")[0:96, 0:T], ACT.Copy).then_inc(jobs.sem_drained("XD"), 1)
                    act.drain()
                    act.sem_inc(xdbl_ready.sem, 1)
                    act.wait_ge(u_ready.sem, u_ready.at(b, 1))
                    nc.scalar.activation(flat(e[:, :, :]), flat(e[:, :, :]), ACT.Exp, scale=-1.0)
                    act.drain()
                    nc.scalar.activation(flat(e[:, :, :]), flat(e[:, :, :]), ACT.Ln, bias=core.eps[:, EPS_ONE:EPS_ONE + 1])
                    act.drain()
                    act.sem_inc(soft_ready.sem, 1)
                    act.wait_ge(dt_ready.sem, dt_ready.at(b, 1))
                    for g in range(NG):
                        act.wait_ge(hC_ready.sem, hC_ready.at(b, g + 1, 2))
                        for k in range(2):
                            for j in range(2):
                                n = 2 * g + j
                                nc.scalar.activation(dA[:, g % 2, k, j, 1:T], dt[:, k, 1:T], ACT.Exp, scale=A[:, k, n:n + 1])
                        act.drain()
                        act.sem_inc(dA_ready.sem, 1)

            @block.vector
            def _(dve):
                dve.wait_ge(loads, 160)
                dve.wait_ge(consts, 1)
                dve.sem_inc(hC_ready.sem, hC_ready.credit)
                with dve.Fori(0, NB) as b:
                    norm.dve_center(dve, b, x[:, cols(b)])
                    dve.wait_ge(scaled.sem, scaled.at(b, 1))
                    nc.vector.tensor_tensor(cent[:, :], cent[:, :], lrs[:, :], ALU.mult)
                    dve.drain()
                    nc.vector.tensor_scalar(h[:, :], cent[:, :], core.mod[1][:, 1, bass.ds(b, 1)],
                                            core.mod[1][:, 0, bass.ds(b, 1)], ALU.mult, ALU.add)
                    dve.drain()
                    dve.sem_inc(h_ready.sem, 1)
                    dve.wait_ge(xp_ready.sem, xp_ready.at(b, 1))
                    for k in range(2):
                        nc.vector.tensor_scalar(xc[:, k, :], xp[:, k, 0:T], cw[:, k, 0:1], cb[:, k:k + 1], ALU.mult, ALU.add)
                    for j in range(1, KC):
                        dve.drain()
                        for k in range(2):
                            nc.vector.scalar_tensor_tensor(xc[:, k, :], xp[:, k, j:j + T], cw[:, k, j:j + 1], xc[:, k, :],
                                                           ALU.mult, ALU.add)
                    dve.drain()
                    dve.sem_inc(conv_ready.sem, 1)
                    dve.wait_ge(*jobs.filled(b, "DT"))
                    for k in range(2):
                        last = nc.vector.tensor_scalar(u[:, k, :], jobs.out("DT")[:, k * T:(k + 1) * T], bdt[:, k:k + 1], None, ALU.add)
                    last.then_inc(jobs.sem_drained("DT"), 1)
                    dve.drain()
                    nc.vector.scalar_tensor_tensor(flat(e[:, :, :]), flat(u[:, :, :]), -1.0, flat(u[:, :, :]), ALU.mult, ALU.max)
                    dve.drain()
                    dve.sem_inc(u_ready.sem, 1)
                    dve.wait_ge(soft_ready.sem, soft_ready.at(b, 1))
                    nc.vector.scalar_tensor_tensor(flat(dt[:, :, :]), flat(u[:, :, :]), 0.0, flat(e[:, :, :]), ALU.max, ALU.add)
                    dve.drain()
                    dve.sem_inc(dt_ready.sem, 1)
                    nc.vector.tensor_tensor(flat(du[:, :, :]), flat(dt[:, :, :]), flat(xs[:, :, :]), ALU.mult)
                    dve.drain()
                    for g in range(NG):
                        s = g % 2
                        four = lambda t: t[:, s, :, :, :].rearrange("p k j l -> p k (j l)")
                        dve.wait_ge(*jobs.filled(b, f"B{g}"))
                        for k in range(2):
                            last = nc.vector.tensor_tensor(dBx[:, s, k, :, :], jobs.out(f"B{g}").rearrange("p (j l) -> p j l", j=2),
                                                           spread(du[:, k, :], 2), ALU.mult)
                        last.then_inc(jobs.sem_drained(f"B{g}"), 1)
                        dve.drain()
                        dve.wait_ge(dA_ready.sem, dA_ready.at(b, g + 1))
                        one_row = lambda t: t[:, s, :, :, :].rearrange("p k j l -> p (k j l)")
                        nc.vector.tensor_tensor_scan(one_row(hs), one_row(dA), one_row(dBx), 0.0, ALU.mult, ALU.add)
                        dve.drain()
                        dve.wait_ge(*jobs.filled(b, f"C{g}"))
                        dve.wait_ge(hC_used.sem, hC_used.at(b, g + 1, 2))
                        last = nc.vector.tensor_tensor(four(hC), four(hs), spread(jobs.out(f"C{g}"), 2), ALU.mult)
                        last.then_inc(jobs.sem_drained(f"C{g}"), 1)
                        dve.drain()
                        dve.sem_inc(hC_ready.sem, 1)
                    for k in range(2):
                        dve.wait_ge(*jobs.filled(b, f"Y{k}"))
                        nc.vector.scalar_tensor_tensor(yy[:, k, :], xs[:, k, :], Dp[:, k:k + 1],
                                                                    jobs.out(f"Y{k}")[:, 0:T], ALU.mult, ALU.add).then_inc(jobs.sem_drained(f"Y{k}"), 1)
                    dve.drain()
                    nc.vector.tensor_tensor(flat(yy[:, :, :]), flat(yy[:, :, :]), flat(sres[:, :, :]), ALU.mult)
                    dve.drain()
                    dve.sem_inc(yy_ready.sem, 1)
                    dve.wait_ge(*jobs.filled(b, "OUT"))
                    nc.vector.scalar_tensor_tensor(x[:, cols(b)], jobs.out("OUT")[:, 0:T],
                                                                core.mod[1][:, 2, bass.ds(b, 1)], x[:, cols(b)],
                                                                ALU.mult, ALU.add).then_inc(jobs.sem_drained("OUT"), 1)
                    dve.drain()
        jobs.close()



def local1(core):
    nc, d = core.nc, core.dram
    N = L1 * NB
    FC = len(FCH)
    with ExitStack() as ctx:
        sb = lambda *a: core.sb(ctx, *a)
        wqk, wv, wo, w1, w2 = sb("wqk", [128, 2 * H1 * E1]), sb("wv1", [128, H1 * E1]), sb("wo1", [128, H1 // 2, D]), sb("w1", [128, 2 * FI]), sb("w2", [128, FC, D])
        NPAR = 3 + 2 * FC
        par = sb("par", [128, NPAR])
        scales = sb("scales", [128, 4, L1 * E1])
        rot = sb("rot", [128, 4, NT, E1])
        tab = sb("tab", [128, L1, 4, NT, E1])
        wmask = sb("wmask", [128, NT, 2 * W])
        wmask_b = sb("wmask_b", [128, NT, 8, 2 * W], BF16)
        ident_b = sb("ident_b", [128, 128], BF16)
        Y = sb("Y", [128, NB * T])
        xs, xv, xs2 = sb("xs3", [128, T]), sb("xv3", [128, T]), sb("xs4", [128, T])
        cent, lsq, lrs = sb("cent3", [128, T]), sb("lsq3", [128, T]), sb("lrs3", [128, T])
        sq, a, bq, c = (sb(n + "3", [128, 2, H1, 2, EH]) for n in ("sq", "a", "bq", "c"))
        qn = sb("qn3", [128, NT, 2, H1, 2, EH])
        ss = sb("ss3", [128, 2, H1])
        V = sb("V3", [128, NT, H1 * E1])
        qT = sb("qT3", [128, NT, H1 // 2, 128])
        kT = sb("kT3", [128, H1 // 2, W + T])
        z = sb("z3", [128, NT, H1, 2 * W])
        pc = sb("pc3", [128, H1, 2, W])
        band = sb("band", [128, NT, H1, 128])
        edge = sb("edge", [128, H1, W])
        mx, sm = sb("mx3", [128, NT, H1]), sb("sm3", [128, NT, H1])
        oT = sb("oT3", [128, H1 // 2, T])
        gl, hid = sb("gl3", [128, FC, T]), sb("hid3", [128, FC, T])
        loads, consts = core.sem("l1f_loads"), core.sem("l1f_consts")
        S = lambda n, per, credit=0: Count(core.sem("l1f_" + n), per, credit)
        m_centered, m_squared, m_scaled = S("m_centered", 1), S("m_squared", 1), S("m_scaled", 1)
        jobs0 = Jobs(core.banks, [("mean", 6, 1), ("var", 7, 1)], NB)
        norm0 = Norm(core, jobs0, "", cent, lsq, lrs, m_centered, m_squared, m_scaled)
        x = core.xT

        with nc.Block() as block:
            @block.sync
            def _(sp):
                for dst, n in ((scales[:, :, :], "scales"), (rot[:, :, :, :], "rot"), (wmask[:, :, :], "wmask")):
                    sp.dma_start(dst, d[n]).then_inc(loads, 16)
                sp.wait_ge(loads, 48)

            @block.gpsimd
            def _(pool):
                nc.gpsimd.memset(xs[:, 0:1], 0.0)
                nc.gpsimd.memset(xs2[:, 0:1], 0.0)
                nc.gpsimd.memset(kT[:, :, 0:W], 0.0)
                nc.gpsimd.memset(band[:, :, :, :], 0.0)
                pool.drain()

            @block.tensor
            def _(pe):
                with pe.Fori(0, NB) as b:
                    norm0.pe_mean(pe, b, x[:, cols(b)])
                    norm0.pe_var(pe, b, 1)

            @block.scalar
            def _(act):
                act.preload_act_table_set("natural_log_exp_and_others")
                with act.Fori(0, NB) as b:
                    norm0.act_root(act, b, 1)

            @block.vector
            def _(dve):
                dve.wait_ge(loads, 48)
                nc.vector.tensor_copy(ident_b[:, :], core.ident[:, :])
                for t in range(NT):
                    nc.vector.tensor_copy(wmask_b[:, t, :, :], spread(wmask[:, t, :], 8))
                with dve.Fori(0, NB) as b:
                    norm0.dve_center(dve, b, x[:, cols(b)])
                    dve.wait_ge(m_scaled.sem, m_scaled.at(b, 1))
                    nc.vector.tensor_tensor(cent[:, :], cent[:, :], lrs[:, :], ALU.mult)
                    dve.drain()
                    nc.vector.tensor_scalar(Y[:, cols(b)], cent[:, :], core.mod[1][:, 4, bass.ds(b, 1)],
                                            core.mod[1][:, 3, bass.ds(b, 1)], ALU.mult, ALU.add)
                    dve.drain()
        jobs0.close()

        FRONT, MID, LATE = range(3)
        w_loaded = core.sem("l1f_weights")
        front_ok, values_ok, mid_ok, late_ok = (core.sem(f"l1f_{n}_weights") for n in ("front", "values", "mid", "late"))
        pe_steps = core.sem("l1f_pe_steps")
        qk_used, wv_used, wo_used, w1_used, w2_used = (core.sem(f"l1f_{n}_used") for n in ("wqk", "wv", "wo", "w1", "w2"))
        xs_ready, xv_ready, xs2_ready, V_ready = S("xs", 1), S("xv", 1), S("xs2", 1), S("V", NT)
        sq_ready, ab_ready, c_ready, ss_ready, rn_ready = S("sq", 2 * NT), S("ab", 2 * NT), S("c", 2 * NT, 2), S("ss", 2 * NT), S("rn", 2 * NT)
        qn_ready, t_ready = S("qn", 2 * NT, 2), S("turned", 2 * NT, 2 * NT)
        z_ready, e_ready, rs_ready, p_ready, band_ready = (S(n, NT) for n in ("z", "exps", "sums", "p", "band"))
        o_ready, pc_ready, band2_ready = S("o", NT), S("pc", NT), S("band2", NT, 1)
        centered, squared, scaled, xn_ready = S("centered", 1), S("squared", 1), S("scaled", 1), S("xn", 1)
        gl_ready, hid_ready = S("gl", FC), S("hid", FC)

        Z = lambda t, banks: [(FRONT, f"Z{t}.{y}.{s}", banks[2 * y + s]) for y in range(2) for s in range(2)]
        Tn = lambda part, t, banks: [(part, f"T{t}.{y}.{j}", banks[2 * y + j]) for y in range(2) for j in range(2)]
        two = lambda part, n, b0, b1: [(part, n + ".0", b0), (part, n + ".1", b1)]
        order = (two(MID, "S0", 5, 4) + [(LATE, "mean", 6)] + Z(0, (0, 1, 2, 7)) + [(LATE, "var", 6)] + Tn(MID, 1, (3, 5, 4, 6))
                 + two(MID, "S1", 3, 5) + two(MID, "V0", 4, 6) + two(MID, "V1", 0, 1)
                 + [(LATE, "F0", 2), (LATE, "F1", 7), (LATE, "F2", 4)] + Z(1, (0, 1, 6, 3)) + Tn(FRONT, 0, (5, 2, 7, 4))
                 + two(MID, "O0", 5, 2) + [(LATE, "OUT2", 4)] + two(MID, "O1", 7, 0) + [(MID, "WO", 1)])
        jobs = Jobs(core.banks, [(n, b, 1) for _, n, b in order], N + 2)
        norm = Norm(core, jobs, "", cent, lsq, lrs, centered, squared, scaled)
        heads_view = lambda ap: ap.rearrange("p (h e) -> p h e", e=EH)

        def every_iteration(eng, body):
            body(0, True, False, False)
            body(1, True, True, False)
            with eng.Fori(2, N) as it:
                body(it, True, True, True)
            body(N, False, True, True)
            body(N + 1, False, False, True)

        with nc.Block() as block:
            @block.sync
            def _(sp):
                with sp.Fori(0, L1) as l:
                    row = bass.ds(l * 128, 128)
                    sp.wait_ge(qk_used, l * NB + 1)
                    sp.dma_start(wqk[:, :], d["wqkv"][row, 0:2 * H1 * E1]).then_inc(w_loaded, 16)
                    sp.wait_ge(w_loaded, l * 96 + 16)
                    sp.sem_inc(front_ok, NB)
                    sp.wait_ge(wv_used, l * NB + 1)
                    sp.dma_start(wv[:, :], d["wqkv"][row, 2 * H1 * E1:3 * H1 * E1]).then_inc(w_loaded, 16)
                    sp.wait_ge(w_loaded, l * 96 + 32)
                    sp.sem_inc(values_ok, NB)
                    sp.wait_ge(wo_used, l * NB + 1)
                    sp.dma_start(wo[:, :, :], d["wo1"][row, :].rearrange("p (a b) -> p a b", b=D)).then_inc(w_loaded, 16)
                    sp.wait_ge(w_loaded, l * 96 + 48)
                    sp.sem_inc(mid_ok, NB)
                    for dst, n, used in ((w1, "w1", w1_used), (w2, "w2", w2_used), (par, "params", None)):
                        if used is not None:
                            sp.wait_ge(used, l * NB + 1)
                        src, dst = d[n][bass.ds(l * 128, 128), :], dst[:, :] if len(dst.shape) == 2 else dst[:, :, :]
                        if len(dst.shape) == 3:
                            src = src.rearrange("p (a b) -> p a b", b=D)
                        sp.dma_start(dst, src).then_inc(w_loaded, 16)
                    sp.wait_ge(w_loaded, l * 96 + 96)
                    sp.sem_inc(late_ok, NB)

            @block.tensor
            def _(pe):
                for used in (qk_used, wv_used, wo_used, w1_used, w2_used):
                    pe.sem_inc(used, 1)

                def skip(part, it):
                    pe.drain()
                    for _, n, b in [o for o in order if o[1] in part]:
                        pe.sem_inc(core.banks.filled[b], 1)
                        pe.sem_inc(core.banks.drained[b], 1)

                def project(it, names, tok, w):
                    for j, n in enumerate(names):
                        pe.wait_ge(*jobs.free(it, n))
                        nc.tensor.matmul(jobs.out(n), tok, w[:, j * 512:(j + 1) * 512],
                                         start=True, stop=True).then_inc(jobs.sem_filled(n), 1)

                def turn(it, t, step):
                    for y in range(2):
                        pe.wait_ge(qn_ready.sem, qn_ready.at(step, 2 * t + y + 1))
                        for j in range(2):
                            n = f"T{t}.{y}.{j}"
                            pe.wait_ge(*jobs.free(it, n))
                            for i in range(4):
                                src = qn[:, t, y, 8 * j + 2 * i:8 * j + 2 * i + 2, :, :].rearrange("p h s e -> p (h s e)")
                                last = nc.tensor.transpose(jobs.out(n)[:, i * 128:(i + 1) * 128], src, core.ident[:, :])
                            last.then_inc(jobs.sem_filled(n), 1)

                def scores(it, t):
                    for j in range(2):
                        pe.wait_ge(*jobs.free(it, f"S{t}.{j}"))
                        nc.tensor.matmul(jobs.out(f"S{t}.{j}"), ident_b[:, :], wmask_b[:, t, :, :], start=True, stop=False)
                    for i in range(H1):
                        j, m = i % 2, i // 2
                        p, n = 64 * j, f"S{t}.{j}"
                        for w in range(4):
                            k0 = t * 128 + w * W
                            last = nc.tensor.matmul(jobs.out(n)[w * W:(w + 1) * W, m * 64:(m + 1) * 64],
                                                    qT[p:p + 64, t, m, w * W:(w + 1) * W],
                                                    kT[p:p + 64, m, k0:k0 + 2 * W], start=False, stop=(m == H1 // 2 - 1),
                                                    tile_position=(p, w * W))
                        if i >= H1 - 2:
                            last.then_inc(jobs.sem_filled(n), 1)

                def values(it, t):
                    pe.wait_ge(band_ready.sem, band_ready.at(it - 1, t + 1))
                    pe.wait_ge(band2_ready.sem, band2_ready.at(it - 1, t + 1))
                    for j in range(2):
                        n = f"O{t}.{j}"
                        pe.wait_ge(*jobs.free(it, n))
                        pe.sem_inc(pe_steps, 1)
                        for i in range(8):
                            hd = 8 * j + i
                            p, at = 64 * (hd % 2), 8 * (hd % 2) + hd // 2
                            o = jobs.out(n)[p:p + 64, (i // 2) * 128:(i // 2 + 1) * 128]
                            last = nc.tensor.matmul(o, V[:, t, hd * E1:(hd + 1) * E1], band[:, t, at, :],
                                                    start=True, stop=(t == 0), tile_position=(0, p))
                            if t:
                                last = nc.tensor.matmul(o[:, 0:W], V[96:128, t - 1, hd * E1:(hd + 1) * E1],
                                                        edge[96:128, at, :], start=False, stop=True, tile_position=(96, p))
                        last.then_inc(jobs.sem_filled(n), 1)

                def body(it, front, mid, late):
                    m, n = it - 1, it - 2
                    Zs = lambda t: [f"Z{t}.{y}.{s}" for y in range(2) for s in range(2)]
                    Ts = lambda t: [f"T{t}.{y}.{s}" for y in range(2) for s in range(2)]
                    if mid:
                        pe.wait_ge(t_ready.sem, t_ready.at(m, NT))
                        scores(it, 0)
                    else:
                        skip(["S0.0", "S0.1"], it)
                    if late:
                        pe.wait_ge(xs2_ready.sem, xs2_ready.at(n, 1))
                        norm.pe_mean(pe, it, xs2[:, :])
                    else:
                        skip(["mean"], it)
                    if front:
                        pe.wait_ge(front_ok, it + 1)
                        pe.wait_ge(xs_ready.sem, xs_ready.at(it, 1))
                        project(it, Zs(0), xs[:, 0:128], wqk)
                    else:
                        skip(Zs(0), it)
                    if late:
                        pe.wait_ge(squared.sem, squared.at(n, 1))
                        norm.pe_var_ready(pe, it)
                    else:
                        skip(["var"], it)
                    if mid:
                        turn(it, 1, m)
                        pe.wait_ge(t_ready.sem, t_ready.at(m, 2 * NT))
                        scores(it, 1)
                        pe.wait_ge(values_ok, m + 1)
                        pe.wait_ge(xv_ready.sem, xv_ready.at(m, 1))
                        for t in range(NT):
                            project(it, [f"V{t}.0", f"V{t}.1"], xv[:, t * 128:(t + 1) * 128], wv)
                    else:
                        skip(Ts(1) + ["S1.0", "S1.1", "V0.0", "V0.1", "V1.0", "V1.1"], it)
                    if late:
                        pe.wait_ge(late_ok, n + 1)
                        pe.wait_ge(xn_ready.sem, xn_ready.at(n, 1))
                        for c_, (c0, cw) in enumerate(FCH):
                            name = f"F{c_}"
                            pe.wait_ge(*jobs.free(it, name))
                            for y in range(2):
                                last = nc.tensor.matmul(jobs.out(name)[0:cw, y * T:(y + 1) * T], w1[:, y * FI + c0:y * FI + c0 + cw],
                                                        cent[:, :], start=True, stop=True)
                            last.then_inc(jobs.sem_filled(name), 1)
                    else:
                        skip(["F0", "F1", "F2"], it)
                    if front:
                        project(it, Zs(1), xs[:, 128:T], wqk)
                        turn(it, 0, it)
                    else:
                        skip(Zs(1) + Ts(0), it)
                    if mid:
                        pe.wait_ge(V_ready.sem, V_ready.at(m, NT))
                        values(it, 0)
                    else:
                        skip(["O0.0", "O0.1"], it)
                    if late:
                        pe.wait_ge(*jobs.free(it, "OUT2"))
                        for c_, (c0, cw) in enumerate(FCH):
                            pe.wait_ge(hid_ready.sem, hid_ready.at(n, c_ + 1))
                            last = nc.tensor.matmul(jobs.out("OUT2")[:, 0:T], w2[0:cw, c_, :], hid[0:cw, c_, :],
                                                    start=(c_ == 0), stop=(c_ == FC - 1))
                        last.then_inc(jobs.sem_filled("OUT2"), 1)
                    else:
                        skip(["OUT2"], it)
                    if mid:
                        values(it, 1)
                        pe.wait_ge(mid_ok, m + 1)
                        pe.wait_ge(o_ready.sem, o_ready.at(m, NT))
                        pe.wait_ge(*jobs.free(it, "WO"))
                        for i in range(H1 // 2):
                            last = nc.tensor.matmul(jobs.out("WO")[:, 0:T], wo[:, i, :], oT[:, i, :],
                                                    start=(i == 0), stop=(i == H1 // 2 - 1))
                        last.then_inc(jobs.sem_filled("WO"), 1)
                    else:
                        skip(["O1.0", "O1.1", "WO"], it)

                every_iteration(pe, body)
                pe.wait_ge(pe_steps, 2 * NT * N)

            @block.scalar
            def _(act):
                act.preload_act_table_set("natural_log_exp_and_others")
                act.sem_inc(t_ready.sem, t_ready.credit)

                def squares(it, t, y):
                    for s in range(2):
                        act.wait_ge(*jobs.filled(it, f"Z{t}.{y}.{s}"))
                        nc.scalar.activation(sq[:, y, :, s, :], heads_view(jobs.out(f"Z{t}.{y}.{s}")), ACT.Square)
                    act.drain()
                    act.sem_inc(sq_ready.sem, 1)

                def roots(it, t, y):
                    act.wait_ge(ss_ready.sem, ss_ready.at(it, 2 * t + y + 1))
                    nc.scalar.activation(ss[:, y, :], ss[:, y, :], ACT.Ln, scale=2.0 ** 16)
                    act.drain()
                    nc.scalar.activation(ss[:, y, :], ss[:, y, :], ACT.Exp, scale=-0.5,
                                         bias=core.eps[:, EPS_HALFLOG:EPS_HALFLOG + 1])
                    act.drain()
                    act.sem_inc(rn_ready.sem, 1)

                def turned(it, t):
                    for y in range(2):
                        for j in range(2):
                            n = f"T{t}.{y}.{j}"
                            act.wait_ge(*jobs.filled(it, n))
                            src = jobs.out(n).rearrange("p (a b) -> p a b", b=128)
                            dst = qT[:, t, 4 * j:4 * j + 4, :] if y == 0 else kT[:, 4 * j:4 * j + 4, W + t * 128:W + (t + 1) * 128]
                            nc.scalar.activation(dst, src, ACT.Copy).then_inc(jobs.sem_drained(n), 1)
                        act.drain()
                        act.sem_inc(t_ready.sem, 1)

                def exps(m, t):
                    act.wait_ge(z_ready.sem, z_ready.at(m, t + 1))
                    zt = z[:, t, :, :].rearrange("p a b -> p (a b)")
                    nc.scalar.activation(zt, zt, ACT.Exp)
                    act.drain()
                    act.sem_inc(e_ready.sem, 1)

                def scatter(m, t):
                    act.wait_ge(pc_ready.sem, pc_ready.at(m, t + 1))
                    for w in (2, 3):
                        rows = slice(w * W, (w + 1) * W)
                        nc.scalar.activation(band[rows, t, :, rows], pc[rows, :, 1, :], ACT.Copy)
                        nc.scalar.activation(band[(w - 1) * W:w * W, t, :, rows], pc[rows, :, 0, :], ACT.Copy)
                    act.drain()
                    act.sem_inc(band2_ready.sem, 1)

                def take_values(it, t):
                    for j in range(2):
                        act.wait_ge(*jobs.filled(it, f"V{t}.{j}"))
                        nc.scalar.activation(V[:, t, j * 512:(j + 1) * 512], jobs.out(f"V{t}.{j}"), ACT.Copy).then_inc(jobs.sem_drained(f"V{t}.{j}"), 1)
                    act.drain()
                    act.sem_inc(V_ready.sem, 1)

                def take_outputs(it, t):
                    for j in range(2):
                        n = f"O{t}.{j}"
                        act.wait_ge(*jobs.filled(it, n))
                        nc.scalar.activation(oT[:, 4 * j:4 * j + 4, t * 128:(t + 1) * 128],
                                                          jobs.out(n).rearrange("p (a b) -> p a b", b=128), ACT.Copy).then_inc(jobs.sem_drained(n), 1)
                    act.drain()
                    act.sem_inc(o_ready.sem, 1)

                def body(it, front, mid, late):
                    m, n = it - 1, it - 2
                    if mid:
                        exps(m, 0)
                    if late:
                        norm.act_square(act, n)
                    if front:
                        squares(it, 0, 0)
                    if late:
                        norm.act_rsqrt(act, it)
                    if mid:
                        turned(it, 1)
                    if front:
                        squares(it, 0, 1)
                        roots(it, 0, 0)
                        roots(it, 0, 1)
                    if mid:
                        take_values(it, 0)
                        take_values(it, 1)
                        act.sem_inc(wv_used, 1)
                    if front:
                        act.wait_ge(xs_ready.sem, xs_ready.at(it, 1))
                        nc.scalar.activation(xv[:, :], xs[:, :], ACT.Copy).then_inc(xv_ready.sem, 1)
                    if mid:
                        exps(m, 1)
                        scatter(m, 0)
                    if late:
                        for c_, (c0, cw) in enumerate(FCH):
                            act.wait_ge(*jobs.filled(it, f"F{c_}"))
                            nc.scalar.activation(gl[0:cw, c_, :], jobs.out(f"F{c_}")[0:cw, T:2 * T], ACT.Gelu,
                                                 bias=par[0:cw, 3 + FC + c_:4 + FC + c_])
                            act.drain()
                            act.sem_inc(gl_ready.sem, 1)
                        act.preload_act_table_set("natural_log_exp_and_others")
                    if front:
                        squares(it, 1, 0)
                        squares(it, 1, 1)
                        act.sem_inc(qk_used, 1)
                        turned(it, 0)
                        roots(it, 1, 0)
                    if mid:
                        scatter(m, 1)
                        take_outputs(it, 0)
                        take_outputs(it, 1)
                    if front:
                        roots(it, 1, 1)

                every_iteration(act, body)

            @block.gpsimd
            def _(pool):
                pool.sem_inc(c_ready.sem, c_ready.credit)
                pool.sem_inc(qn_ready.sem, qn_ready.credit)

                def rotary_sum(it, t, y):
                    pool.wait_ge(ab_ready.sem, ab_ready.at(it, 2 * t + y + 1))
                    f = lambda q: q[:, y, :, :, :].rearrange("p h s e -> p (h s e)")
                    nc.gpsimd.tensor_tensor(f(c), f(a), f(bq), ALU.add)
                    pool.drain()
                    pool.sem_inc(c_ready.sem, 1)

                def unit(it, t, y):
                    pool.wait_ge(rn_ready.sem, rn_ready.at(it, 2 * t + y + 1))
                    pool.wait_ge(t_ready.sem, t_ready.at(it, 2 * t + y + 1, 2 * NT))
                    nc.gpsimd.tensor_tensor(qn[:, t, y, :, :, :].rearrange("p h s e -> p h (s e)"),
                                            c[:, y, :, :, :].rearrange("p h s e -> p h (s e)"), spread(ss[:, y, :], E1, 2), ALU.mult)
                    pool.drain()
                    pool.sem_inc(qn_ready.sem, 1)

                def by_sum(m, t):
                    pool.wait_ge(rs_ready.sem, rs_ready.at(m, t + 1))
                    nc.gpsimd.tensor_tensor(z[:, t, :, :], z[:, t, :, :], spread(sm[:, t, :], 2 * W, 2), ALU.mult)
                    pool.drain()
                    pool.sem_inc(p_ready.sem, 1)

                def body(it, front, mid, late):
                    m = it - 1
                    if front:
                        rotary_sum(it, 0, 0)
                        unit(it, 0, 0)
                    if mid:
                        by_sum(m, 0)
                    if front:
                        rotary_sum(it, 0, 1)
                        unit(it, 0, 1)
                    if mid:
                        by_sum(m, 1)
                    if front:
                        rotary_sum(it, 1, 0)
                        unit(it, 1, 0)
                        rotary_sum(it, 1, 1)
                        unit(it, 1, 1)

                every_iteration(pool, body)

            @block.vector
            def _(dve):
                for l in range(L1):
                    for j in range(4):
                        nc.vector.tensor_tensor(tab[:, l, j, :, :], rot[:, j, :, :], spread(scales[:, j, l * E1:(l + 1) * E1], NT), ALU.mult)
                dve.drain()

                def shifted(dst, b):
                    nc.vector.tensor_scalar(dst[0:64, :], Y[0:64, cols(b)], 1.0, None, ALU.mult)
                    nc.vector.tensor_scalar(dst[64:128, 1:T], Y[64:128, bass.ds(b * T, T - 1)], 1.0, None, ALU.mult)
                    dve.drain()

                def rotary(it, t, y):
                    dve.wait_ge(sq_ready.sem, sq_ready.at(it, 2 * t + y + 1))
                    if type(it) is int:
                        l = it // NB
                        table = lambda j, s: tab[:, l, 2 * y + j, t, s * EH:(s + 1) * EH]
                    else:
                        flat = tab[:, :, :, :, :].rearrange("p l j t e -> p (l j t e)")
                        table = lambda j, s: flat[:, bass.ds((it // NB) * (4 * NT * E1) + ((2 * y + j) * NT + t) * E1 + s * EH, EH)]
                    dve.wait_ge(c_ready.sem, c_ready.at(it, 2 * t + y + 1, 2))
                    for s in range(2):
                        Zs = heads_view(jobs.out(f"Z{t}.{y}.{s}"))
                        nc.vector.tensor_tensor(a[:, y, :, s, :], Zs, spread(table(0, s), H1), ALU.mult)
                        last = nc.vector.tensor_tensor(bq[:, y, :, 1 - s, :], Zs, spread(table(1, 1 - s), H1), ALU.mult)
                        last.then_inc(jobs.sem_drained(f"Z{t}.{y}.{s}"), 1)
                    dve.drain()
                    dve.sem_inc(ab_ready.sem, 1)
                    dve.wait_ge(qn_ready.sem, qn_ready.at(it, 2 * t + y + 1, 2))
                    nc.vector.tensor_reduce(ss[:, y, :], sq[:, y, :, :, :].rearrange("p h s e -> p h (s e)"), axis=AX.X, op=ALU.add)
                    dve.drain()
                    nc.vector.tensor_scalar(ss[:, y, :], ss[:, y, :], 1e-24, None, ALU.max)
                    dve.drain()
                    dve.sem_inc(ss_ready.sem, 1)

                def less_maximum(it, t):
                    ps = [jobs.out(f"S{t}.{j}").rearrange("p (h k) -> p h k", h=8) for j in range(2)]
                    for j in range(2):
                        dve.wait_ge(*jobs.filled(it, f"S{t}.{j}"))
                        nc.vector.tensor_reduce(mx[:, t, 8 * j:8 * j + 8], ps[j], axis=AX.X, op=ALU.max)
                    dve.drain()
                    for j in range(2):
                        nc.vector.tensor_tensor(z[:, t, 8 * j:8 * j + 8, :], ps[j],
                                                             spread(mx[:, t, 8 * j:8 * j + 8], 2 * W, 2), ALU.subtract).then_inc(jobs.sem_drained(f"S{t}.{j}"), 1)
                    dve.drain()
                    dve.sem_inc(z_ready.sem, 1)

                def sums(m, t):
                    dve.wait_ge(e_ready.sem, e_ready.at(m, t + 1))
                    nc.vector.tensor_reduce(sm[:, t, :], z[:, t, :, :], axis=AX.X, op=ALU.add)
                    dve.drain()
                    nc.vector.reciprocal(sm[:, t, :], sm[:, t, :])
                    dve.drain()
                    dve.sem_inc(rs_ready.sem, 1)

                def place(m, t):
                    dve.wait_ge(p_ready.sem, p_ready.at(m, t + 1))
                    dve.wait_ge(band2_ready.sem, band2_ready.at(m, t + 1, 1))
                    nc.vector.transpose(pc[:, :, :, :].rearrange("p h s k -> p (h s k)"), z[:, t, :, :].rearrange("p h k -> p (h k)"))
                    dve.drain()
                    dve.sem_inc(pc_ready.sem, 1)
                    for w in (0, 1):
                        rows = slice(w * W, (w + 1) * W)
                        nc.vector.tensor_copy(band[rows, t, :, rows], pc[rows, :, 1, :])
                        if w:
                            nc.vector.tensor_copy(band[(w - 1) * W:w * W, t, :, rows], pc[rows, :, 0, :])
                        elif t:
                            nc.vector.tensor_copy(edge[96:128, :, :], pc[rows, :, 0, :])
                    dve.drain()
                    dve.sem_inc(band_ready.sem, 1)

                def body(it, front, mid, late):
                    m, n = it - 1, it - 2
                    if mid:
                        less_maximum(it, 0)
                    if late:
                        norm.dve_center(dve, it, xs2[:, :])
                    if front:
                        rotary(it, 0, 0)
                    if mid:
                        sums(m, 0)
                    if late:
                        dve.wait_ge(late_ok, n + 1)
                        dve.wait_ge(scaled.sem, scaled.at(n, 1))
                        nc.vector.tensor_tensor(cent[:, :], cent[:, :], lrs[:, :], ALU.mult)
                        dve.drain()
                        nc.vector.tensor_scalar(cent[:, :], cent[:, :], par[:, 0:1], par[:, 1:2], ALU.mult, ALU.add)
                        dve.drain()
                        dve.sem_inc(xn_ready.sem, 1)
                    if front:
                        rotary(it, 0, 1)
                    if mid:
                        less_maximum(it, 1)
                        place(m, 0)
                        sums(m, 1)
                    if late:
                        for c_, (c0, cw) in enumerate(FCH):
                            dve.wait_ge(gl_ready.sem, gl_ready.at(n, c_ + 1))
                            nc.vector.scalar_tensor_tensor(hid[0:cw, c_, :], jobs.out(f"F{c_}")[0:cw, 0:T], par[0:cw, 3 + c_:4 + c_],
                                                           gl[0:cw, c_, :], ALU.add, ALU.mult)\
                                .then_inc(jobs.sem_drained(f"F{c_}"), 1)
                            dve.drain()
                            dve.sem_inc(hid_ready.sem, 1)
                        dve.sem_inc(w1_used, 1)
                    if front:
                        rotary(it, 1, 0)
                    if mid:
                        place(m, 1)
                    if front:
                        rotary(it, 1, 1)
                        dve.wait_ge(xv_ready.sem, xv_ready.at(it, 1))
                        shifted(xs, (it + 1) % NB)
                        dve.sem_inc(xs_ready.sem, 1)
                    if late:
                        b = n % NB
                        dve.wait_ge(*jobs.filled(it, "OUT2"))
                        nc.vector.scalar_tensor_tensor(Y[:, cols(b)], jobs.out("OUT2")[:, 0:T], par[:, 2:3], Y[:, cols(b)],
                                                       ALU.add, ALU.add).then_inc(jobs.sem_drained("OUT2"), 1)
                        dve.drain()
                        dve.sem_inc(w2_used, 1)
                    if mid:
                        b = m % NB
                        dve.wait_ge(*jobs.filled(it, "WO"))
                        nc.vector.tensor_tensor(Y[:, cols(b)], jobs.out("WO")[:, 0:T], Y[:, cols(b)], ALU.add)\
                            .then_inc(jobs.sem_drained("WO"), 1)
                        dve.drain()
                        dve.sem_inc(wo_used, 1)
                        shifted(xs2, b)
                        dve.sem_inc(xs2_ready.sem, 1)

                shifted(xs, 0)
                dve.sem_inc(xs_ready.sem, 1)
                dve.sem_inc(band2_ready.sem, band2_ready.credit)
                every_iteration(dve, body)
        jobs.close()

        with nc.Block() as block:
            @block.vector
            def _(dve):
                with dve.Fori(0, NB) as b:
                    nc.vector.scalar_tensor_tensor(x[:, cols(b)], Y[:, cols(b)], core.mod[1][:, 5, bass.ds(b, 1)],
                                                   x[:, cols(b)], ALU.mult, ALU.add)
                dve.drain()


def store(core, out):
    nc = core.nc
    stored = core.sem("stored")
    with nc.Block() as block:
        @block.sync
        def _(sp):
            sp.dma_start(out, core.xT[:, :]).then_inc(stored, 16)
            sp.wait_ge(stored, 16)


STAGES = [attention0, routed0, mamba1, local1]


def build(nc, dram, out):
    with ExitStack() as ctx:
        core = Core(nc, ctx, dram)
        with ExitStack() as early:
            core.routed = Routed(core, early, "qkv")
            prepare(core)
            for stage in STAGES:
                if stage in (attention0, routed0):
                    stage(core)
        for stage in STAGES:
            if stage not in (attention0, routed0):
                stage(core)
        store(core, out)


def layouts(v):
    a = {}
    a["xT"] = v["L0_attn_x"].transpose(2, 0, 1).reshape(D, NB * T)
    for i in range(2):
        a[f"c{i}"] = v[f"L{i}_c"].T
        a[f"wmod{i}"] = v[f"L{i}_wmod"]
    for n in ("wq", "wk", "wv"):
        a[n] = v["L0_attn_" + n].reshape(D, H0 * D)
    a["wo0"] = v["L0_attn_wo"].transpose(1, 0, 2).reshape(D, H0 * D)
    for n in "qkvf":
        w = lambda p: v[f"L0_ffn_{n}_{p}"]
        a[n + "_nw"] = np.pad(w("nw").T, ((0, 0), (0, 1)))
        a[n + "_nb"] = np.pad(w("nb")[None, :], ((0, 0), (0, 1)))
        a[n + "_w1"] = w("w1").transpose(1, 0, 2).reshape(D, NCH * 128)
        a[n + "_b1"] = w("b1").reshape(NCH, 128).T
        a[n + "_w2"] = w("w2").reshape(NCH, 128, D).transpose(1, 0, 2).reshape(128, NCH * D)
        a[n + "_b2"] = w("b2").reshape(2, 128, D).transpose(1, 0, 2).reshape(128, 2 * D)
    two = lambda w: w.reshape(2, 128, -1).transpose(1, 0, 2)
    m = lambda p: v["L1_attn_" + p]
    a["win"], a["wdt"] = m("W_in"), m("W_dt")
    a["wx"], a["wout"], a["convw"], a["A_log"] = two(m("W_x")), two(m("W_out")), two(m("conv_w")), two(m("A_log"))
    f = lambda p: v["L1_ffn_" + p]
    q, k, w = np.split(f("Wqkv"), 3, axis=-1)
    halves = lambda m: m.reshape(L1, D, H1, 2, EH).transpose(0, 1, 3, 2, 4).reshape(L1, D, H1 * E1)
    a["wqkv"] = np.concatenate([halves(q), halves(k), w], axis=-1).reshape(L1 * 128, 3 * H1 * E1)
    a["wo1"] = f("Wo").reshape(L1, H1 // 2, 128, D).transpose(0, 2, 1, 3).reshape(L1 * 128, H1 // 2 * D)
    a["w1"] = f("W1").reshape(L1 * 128, 2 * FI)
    pad = FCH[-1][0] + 128 - FI
    a["w2"] = np.pad(f("W2"), ((0, 0), (0, pad), (0, 0))).reshape(L1, len(FCH), 128, D).transpose(0, 2, 1, 3).reshape(L1 * 128, len(FCH) * D)
    b1 = np.pad(f("b1").reshape(L1, 2, FI), ((0, 0), (0, 0), (0, pad))).reshape(L1, 2 * len(FCH), 128)
    params = np.concatenate([f("ln_g")[:, None], f("ln_b")[:, None], f("b2")[:, None], b1], axis=1)
    a["params"] = params.transpose(0, 2, 1).reshape(L1 * 128, -1)
    swap = lambda m: m.reshape(L1, 2, EH)[:, ::-1].reshape(L1, E1)
    scales = np.stack([f("q_scale"), swap(f("q_scale")), f("k_scale"), swap(f("k_scale"))]).reshape(4, L1 * E1)
    a["scales"] = np.broadcast_to(scales[None], (128, 4, L1 * E1))
    a["convb"], a["bdt"], a["Dp"] = (m(p).reshape(2, 128).T for p in ("conv_b", "b_dt", "D"))
    return a


def constants():
    f = np.float32
    a = {"ident": np.eye(128, dtype=f)}
    half = D // 2
    freqs = np.power(f(1250), -np.arange(half, dtype=f) / f(half)).astype(f)
    rad = (np.arange(T, dtype=f)[:, None] * freqs[None, :]).astype(f)
    a["cos0"] = np.concatenate([np.cos(rad).T, np.cos(rad).T]).astype(f)
    a["sin0"] = np.concatenate([-np.sin(rad).T, np.sin(rad).T]).astype(f)
    k = np.arange(128)
    a["tri"] = (k[:, None] <= k[None, :]).astype(f)
    sel = np.zeros((96, 2 * NS, 128), f)
    sel[np.arange(DTR, 96), np.arange(2 * NS), :] = 1.0
    a["sel"] = sel.reshape(96, 2 * NS * 128)
    pairs = np.arange(0, E1, 2, dtype=f)
    inv_freq = (f(1) / f(10000) ** (pairs / f(E1))).astype(f)
    t = np.arange(T, dtype=f)
    freqs = np.tile(t[:, None] * inv_freq[None, :], 2)
    scale = np.tile((((pairs + f(0.4 * E1)) / f(1.4 * E1))[None, :] ** ((t - T // 2) / f(W // 2))[:, None]).astype(f), 2)
    sign = np.repeat(np.array([-1.0, 1.0], f), EH)[None, :]
    tables = [np.cos(freqs) * scale * 8, np.sin(freqs) * scale * 8 * sign, np.cos(freqs) / scale, np.sin(freqs) / scale * sign]
    a["rot"] = np.stack(tables).astype(f).reshape(4, NT, 128, E1).transpose(2, 0, 1, 3)
    i, j = np.arange(128)[:, None] % W, np.arange(2 * W)[None, :]
    seen = np.where(j < W, j >= i, j - W <= i)
    first = seen & ~((np.arange(128)[:, None] < W) & (j < W))
    a["wmask"] = np.where(np.stack([first, seen], 1), 0.0, -3e38).astype(f)
    return a


def kernel(**inputs):
    import concourse.bacc as bacc
    from concourse.bass_utils import run_bass_kernel_spmd

    nc = bacc.Bacc("TRN2", target_bir_lowering=False, num_devices=1)
    arrays, dram = {}, {}
    for name, value in {**layouts(inputs), **constants()}.items():
        value = np.ascontiguousarray(value)
        arrays[f"in_{name}"] = value
        dram[name] = nc.dram_tensor(f"in_{name}", value.shape, mybir.dt.from_np(value.dtype), kind="ExternalInput").ap()
    out = nc.dram_tensor("out_xT", (D, NB * T), F32, kind="ExternalOutput").ap()
    build(nc, dram, out)
    got = run_bass_kernel_spmd(nc, [arrays], core_ids=[0]).results[0]["out_xT"]
    return np.ascontiguousarray(got.reshape(D, NB, T).transpose(1, 2, 0))
```

```python
import math

import numpy as np
import concourse.bass as bass
from concourse import mybir
from contextlib import ExitStack

F32 = mybir.dt.float32
BF16 = mybir.dt.bfloat16
ALU = mybir.AluOpType
ACT = mybir.ActivationFunctionType
AX = mybir.AxisListType

NB, T, D = 8, 256, 128
NT = T // 128
H0 = 8
NLEAF, LW, DEPTH = 256, 16, 8
NCH = NLEAF * LW // 128
DI, NS, DTR, KC = 256, 16, 64, 4
L1, H1, E1, W = 6, 16, 64, 32
EH = E1 // 2
FI = int(D * 4 * 2 / 3)
FCH = [(c, min(128, FI - c)) for c in range(0, FI, 128)]
BIG = 1e30
LN_EPS = 1e-5


class Count:

    def __init__(self, sem, per, credit=0):
        self.sem, self.per, self.credit = sem, per, credit

    def at(self, it, k, lag=0):
        return it * self.per + (k + self.credit - lag)


class Banks:

    def __init__(self, nc, ctx):
        self.ps = ctx.enter_context(nc.psum_tensor("ps", [128, 8, 512], F32))
        self.filled = [ctx.enter_context(nc.semaphore(f"filled{b}")) for b in range(8)]
        self.drained = [ctx.enter_context(nc.semaphore(f"drained{b}")) for b in range(8)]
        self.base_filled, self.base_drained = [0] * 8, [0] * 8


class Jobs:

    def __init__(self, banks, plan, iterations):
        self.banks, self.iterations, self.at = banks, iterations, {}
        self.nf, self.nd = [0] * 8, [0] * 8
        for name, b, readers in plan:
            assert name not in self.at
            self.at[name] = (b, self.nf[b] + 1, self.nd[b])
            self.nf[b] += 1
            self.nd[b] += readers

    def out(self, name):
        return self.banks.ps[:, self.at[name][0], :]

    def free(self, it, name):
        b, _, before = self.at[name]
        return self.banks.drained[b], it * self.nd[b] + (self.banks.base_drained[b] + before + 1)

    def filled(self, it, name):
        b, n, _ = self.at[name]
        return self.banks.filled[b], it * self.nf[b] + (self.banks.base_filled[b] + n)

    def sem_filled(self, name):
        return self.banks.filled[self.at[name][0]]

    def sem_drained(self, name):
        return self.banks.drained[self.at[name][0]]

    def close(self):
        for b in range(8):
            self.banks.base_filled[b] += self.iterations * self.nf[b]
            self.banks.base_drained[b] += self.iterations * self.nd[b]


class Core:

    def __init__(self, nc, ctx, dram):
        self.nc, self.ctx, self.dram = nc, ctx, dram
        self.banks = Banks(nc, ctx)
        self.xT = self.sb(ctx, "xT", [128, NB * T])
        self.mod = [self.sb(ctx, f"mod{i}", [128, 6, NB]) for i in range(2)]
        self.mean_w = self.sb(ctx, "mean_w", [128, 128])
        self.ident = self.sb(ctx, "ident", [128, 128])
        self.eps = self.sb(ctx, "eps", [128, 6])
        self.tiny = self.sb(ctx, "tiny", [128, 1])
        self.one = self.sem("one")

    def sb(self, ctx, name, shape, dt=F32):
        return ctx.enter_context(self.nc.sbuf_tensor(name, shape, dt))

    def sem(self, name):
        return self.ctx.enter_context(self.nc.semaphore(name))


EPS_LN, EPS_RMS, EPS_TINY, EPS_HALFLOG, EPS_ONE = range(5)
EPS_VALUES = (LN_EPS, 1e-6, 1e-5, 0.5 * math.log(2.0 ** 16), 1.0)


class Norm:

    def __init__(self, core, jobs, name, cent, sq, rs, centered, squared, scaled):
        self.c, self.jobs, self.name = core, jobs, name
        self.cent, self.sq, self.rs = cent, sq, rs
        self.centered, self.squared, self.scaled = centered, squared, scaled

    def pe_mean(self, pe, it, src):
        pe.wait_ge(*self.jobs.free(it, self.name + "mean"))
        self.c.nc.tensor.matmul(self.jobs.out(self.name + "mean")[:, 0:T], self.c.mean_w[:, :], src,
                                               start=True, stop=True).then_inc(self.jobs.sem_filled(self.name + "mean"), 1)

    def pe_var(self, pe, it, k):
        pe.wait_ge(self.squared.sem, self.squared.at(it, k))
        self.pe_var_ready(pe, it)

    def pe_var_ready(self, pe, it):
        pe.wait_ge(*self.jobs.free(it, self.name + "var"))
        self.c.nc.tensor.matmul(self.jobs.out(self.name + "var")[:, 0:T], self.c.mean_w[:, :],
                                               self.sq[:, :], start=True, stop=True).then_inc(self.jobs.sem_filled(self.name + "var"), 1)

    def dve_center(self, dve, it, src):
        dve.wait_ge(*self.jobs.filled(it, self.name + "mean"))
        self.c.nc.vector.tensor_tensor(self.cent[:, :], src,
                                                         self.jobs.out(self.name + "mean")[:, 0:T],
                                                         ALU.subtract).then_inc(self.jobs.sem_drained(self.name + "mean"), 1)
        dve.drain()
        dve.sem_inc(self.centered.sem, 1)

    def act_square(self, act, it, k=1):
        act.wait_ge(self.centered.sem, self.centered.at(it, k))
        self.c.nc.scalar.activation(self.sq[:, :], self.cent[:, :], ACT.Square).then_inc(self.squared.sem, 1)

    def act_root(self, act, it, k, sample=False):
        self.act_square(act, it, k)
        self.act_rsqrt(act, it, sample)

    def act_rsqrt(self, act, it, sample=False):
        nc, eps = self.c.nc, self.c.eps
        act.wait_ge(*self.jobs.filled(it, self.name + "var"))
        out = self.jobs.out(self.name + "var")[:, 0:T]
        if sample:
            act.wait_ge(self.c.one, 1)
            nc.scalar.activation(self.rs[:, :], out, ACT.Ln, scale=D / (D - 1.0), bias=self.c.tiny[:, 0:1])
            act.drain()
            nc.scalar.activation(self.rs[:, :], self.rs[:, :], ACT.Exp, scale=0.5)
            act.drain()
            nc.scalar.activation(self.rs[:, :], self.rs[:, :], ACT.Ln, bias=eps[:, EPS_TINY:EPS_TINY + 1])
        else:
            nc.scalar.activation(self.rs[:, :], out, ACT.Ln, bias=eps[:, EPS_LN:EPS_LN + 1])
        act.drain()
        last = nc.scalar.activation(self.rs[:, :], self.rs[:, :], ACT.Exp, scale=-0.5)
        last.then_inc(self.jobs.sem_drained(self.name + "var"), 1)
        act.drain()
        act.sem_inc(self.scaled.sem, 1)


def cols(b):
    return bass.ds(b * T, T)


def spread(ap, n, at=1):
    shape = list(ap.shape)
    shape.insert(at, n)
    return ap.unsqueeze(at).broadcast_to(shape)



def prepare(core):
    nc, d = core.nc, core.dram
    with ExitStack() as ctx:
        sb = lambda *a: core.sb(ctx, *a)
        c = sb("c", [128, 2, NB])
        s = sb("s", [128, 2, NB])
        wmod = sb("wmod", [128, 2, 6 * D])
        sign = sb("sign", [128, 2, NB])
        loads, ready, silu, have_one = (core.sem(n) for n in ("prep_loads", "prep_consts", "prep_silu", "prep_mod"))
        jobs = Jobs(core.banks, [("mod0", 0, 1), ("mod1", 1, 1)], 1)
        with nc.Block() as block:
            @block.sync
            def _(sp):
                for i in range(2):
                    sp.dma_start(c[:, i, :], d[f"c{i}"]).then_inc(loads, 16)
                    sp.dma_start(wmod[:, i, :], d[f"wmod{i}"]).then_inc(loads, 16)
                sp.dma_start(core.xT[:, :], d["xT"]).then_inc(loads, 16)
                sp.dma_start(core.ident[:, :], d["ident"]).then_inc(loads, 16)
                sp.wait_ge(loads, 96)

            @block.gpsimd
            def _(pool):
                for b in range(8):
                    pool.sem_inc(core.banks.drained[b], 1)
                pool.sem_inc(core.one, 1)
                nc.gpsimd.memset(core.mean_w[:, :], 1.0 / D)
                for j, v in enumerate(EPS_VALUES):
                    nc.gpsimd.memset(core.eps[:, j:j + 1], v)
                nc.gpsimd.memset(core.tiny[:, :], 1e-19)
                pool.drain()

            @block.scalar
            def _(act):
                act.wait_ge(loads, 96)
                nc.scalar.activation(s[:, :, :], c[:, :, :], ACT.Silu).then_inc(silu, 1)

            @block.tensor
            def _(pe):
                pe.wait_ge(silu, 1)
                for i in range(2):
                    pe.wait_ge(*jobs.free(0, f"mod{i}"))
                    for j in range(6):
                        last = nc.tensor.matmul(jobs.out(f"mod{i}")[:, j * NB:(j + 1) * NB],
                                                wmod[:, i, j * D:(j + 1) * D], s[:, i, :], start=True, stop=True)
                    last.then_inc(jobs.sem_filled(f"mod{i}"), 1)

            @block.vector
            def _(dve):
                for i in range(2):
                    m = core.mod[i]
                    dve.wait_ge(*jobs.filled(0, f"mod{i}"))
                    nc.vector.tensor_copy(m[:, :, :].rearrange("p a b -> p (a b)"),
                                                       jobs.out(f"mod{i}")[:, 0:6 * NB]).then_inc(jobs.sem_drained(f"mod{i}"), 1)
                    dve.drain()
                    for j in (1, 4):
                        nc.vector.tensor_scalar(m[:, j, :], m[:, j, :], 1.0, None, ALU.add)
                    for j in (2, 5):
                        nc.vector.tensor_scalar(sign[:, j // 3, :], m[:, j, :], 0.0, 2.0, ALU.is_ge, ALU.mult)
                        dve.drain()
                        nc.vector.scalar_tensor_tensor(m[:, j, :], m[:, j, :], -1.0, m[:, j, :], ALU.mult, ALU.max)
                        dve.drain()
                        nc.vector.tensor_scalar(m[:, j, :], m[:, j, :], 0.25, None, ALU.max)
                        dve.drain()
                        nc.vector.scalar_tensor_tensor(m[:, j, :], sign[:, j // 3, :], -1.0, m[:, j, :],
                                                       ALU.add, ALU.mult)
                        dve.drain()
        jobs.close()



def attention0(core):
    nc, d = core.nc, core.dram
    with ExitStack() as ctx:
        sb = lambda *a: core.sb(ctx, *a)
        wq, wk, wv, wo = (sb(n, [128, H0 * D]) for n in ("wq0", "wk0", "wv0", "wo0"))
        cos, sin = sb("cos0", [128, 2, T]), sb("sin0", [128, 2, T])
        tri = sb("tri0", [128, 2, 128])
        ones = sb("ones0", [128, 128])
        h = sb("h0", [128, T])
        cent, lsq, lrs = sb("cent0", [128, T]), sb("lsq0", [128, T]), sb("lrs0", [128, T])
        V = sb("V0", [128, NT, H0 * D])
        sq, a, bq, c, rq, qk = (sb(n + "0", [128, 2, 2 * T]) for n in ("sq", "a", "bq", "cq", "rq", "qkn"))
        P = sb("P0", [128, 2, 384])
        rd = sb("rd0", [128, 2, T])
        oT = sb("oT0", [128, H0, T])
        loads = core.sem("l0a_loads")
        S = lambda n, per, credit=0: Count(core.sem("l0a_" + n), per, credit)
        centered, squared, scaled, h_ready = S("centered", 1), S("squared", 1), S("scaled", 1), S("h_ready", 1)
        V_ready, sq_ready, ab_ready, c_ready = S("V_ready", 4), S("sq_ready", H0), S("ab_ready", H0), S("c_ready", H0)
        rq_ready, qkn_ready = S("rq_ready", H0), S("qkn_ready", H0, 2)
        P_ready, P_masked = S("P_ready", H0, 2), S("P_masked", H0)
        rd_ready, o_ready = S("rd_ready", H0), S("o_ready", H0, 2)
        plan = [("mean", 6, 1), ("var", 7, 1)] + [(f"V{j}", j % 4, 1) for j in range(4)]
        for s in range(H0 + 3):
            if s < H0:
                plan.append((f"qk{s}", s % 2, 1))
            if 0 <= s - 1 < H0:
                plan.append((f"ss{s - 1}", 2, 1))
            if 0 <= s - 2 < H0:
                plan.append((f"S{s - 2}", 3 + s % 2, 1))
            if 0 <= s - 3 < H0:
                plan.append((f"OD{s - 3}", 5 + s % 2, 1))
        plan.append(("WO", 7, 1))
        jobs = Jobs(core.banks, plan, NB)
        norm = Norm(core, jobs, "", cent, lsq, lrs, centered, squared, scaled)
        x = core.xT

        with nc.Block() as block:
            @block.sync
            def _(sp):
                for dst, n in ((wq, "wq"), (wk, "wk"), (wv, "wv"), (wo, "wo0")):
                    sp.dma_start(dst[:, :], d[n]).then_inc(loads, 16)
                for i in range(2):
                    sp.dma_start(cos[:, i, :], d["cos0"]).then_inc(loads, 16)
                    sp.dma_start(sin[:, i, :], d["sin0"]).then_inc(loads, 16)
                    sp.dma_start(tri[:, i, :], d["tri"]).then_inc(loads, 16)
                core.routed.load(core, sp)
                sp.wait_ge(loads, 160)

            @block.tensor
            def _(pe):
                pe.wait_ge(loads, 160)
                with pe.Fori(0, NB) as b:
                    norm.pe_mean(pe, b, x[:, cols(b)])
                    norm.pe_var(pe, b, 1)
                    pe.wait_ge(h_ready.sem, h_ready.at(b, 1))
                    for t in range(NT):
                        for j in range(2):
                            n = f"V{2 * t + j}"
                            pe.wait_ge(*jobs.free(b, n))
                            nc.tensor.matmul(jobs.out(n), h[:, t * 128:(t + 1) * 128],
                                                       wv[:, j * 512:(j + 1) * 512], start=True, stop=True).then_inc(jobs.sem_filled(n), 1)
                    for s in range(H0 + 3):
                        if s < H0:
                            n = f"qk{s}"
                            pe.wait_ge(*jobs.free(b, n))
                            nc.tensor.matmul(jobs.out(n)[:, 0:T], wq[:, s * D:(s + 1) * D], h[:, :], start=True, stop=True)
                            nc.tensor.matmul(jobs.out(n)[:, T:2 * T], wk[:, s * D:(s + 1) * D], h[:, :],
                                                       start=True, stop=True).then_inc(jobs.sem_filled(n), 1)
                        if 0 <= s - 1 < H0:
                            n, i = f"ss{s - 1}", s - 1
                            pe.wait_ge(sq_ready.sem, sq_ready.at(b, i + 1))
                            pe.wait_ge(*jobs.free(b, n))
                            nc.tensor.matmul(jobs.out(n), core.mean_w[:, :], sq[:, i % 2, :],
                                                       start=True, stop=True).then_inc(jobs.sem_filled(n), 1)
                        if 0 <= s - 2 < H0:
                            n, i = f"S{s - 2}", s - 2
                            pe.wait_ge(qkn_ready.sem, qkn_ready.at(b, i + 1))
                            pe.wait_ge(*jobs.free(b, n))
                            q = qk[:, i % 2, :]
                            nc.tensor.matmul(jobs.out(n)[:, 0:T], q[:, T:T + 128], q[:, 0:T], start=True, stop=True)
                            nc.tensor.matmul(jobs.out(n)[:, T:T + 128], q[:, T + 128:2 * T], q[:, 128:T],
                                                       start=True, stop=True).then_inc(jobs.sem_filled(n), 1)
                        if 0 <= s - 3 < H0:
                            n, i = f"OD{s - 3}", s - 3
                            pe.wait_ge(V_ready.sem, V_ready.at(b, 4))
                            pe.wait_ge(P_masked.sem, P_masked.at(b, i + 1))
                            pe.wait_ge(*jobs.free(b, n))
                            for k, (w0, w1) in enumerate(((V[:, 0, i * D:(i + 1) * D], V[:, 1, i * D:(i + 1) * D]),
                                                          (ones[:, :], ones[:, :]))):
                                o = jobs.out(n)[:, k * T:(k + 1) * T]
                                nc.tensor.matmul(o[:, 0:128], w0, P[:, i % 2, 0:128], start=True, stop=True)
                                nc.tensor.matmul(o[:, 128:T], w0, P[:, i % 2, 128:T], start=True, stop=False)
                                last = nc.tensor.matmul(o[:, 128:T], w1, P[:, i % 2, T:384], start=False, stop=True)
                            last.then_inc(jobs.sem_filled(n), 1)
                    pe.wait_ge(o_ready.sem, o_ready.at(b, H0))
                    pe.wait_ge(*jobs.free(b, "WO"))
                    for i in range(H0):
                        last = nc.tensor.matmul(jobs.out("WO")[:, 0:T], wo[:, i * D:(i + 1) * D], oT[:, i, :],
                                                start=(i == 0), stop=(i == H0 - 1))
                    last.then_inc(jobs.sem_filled("WO"), 1)

            @block.scalar
            def _(act):
                act.wait_ge(loads, 160)
                act.preload_act_table_set("natural_log_exp_and_others")
                with act.Fori(0, NB) as b:
                    norm.act_root(act, b, 1)
                    for j in range(4):
                        act.wait_ge(*jobs.filled(b, f"V{j}"))
                        last = nc.scalar.activation(V[:, j // 2, (j % 2) * 512:(j % 2 + 1) * 512], jobs.out(f"V{j}"), ACT.Copy)
                        last.then_inc(jobs.sem_drained(f"V{j}"), 1)
                        act.drain()
                        act.sem_inc(V_ready.sem, 1)
                    for s in range(H0 + 3):
                        if s < H0:
                            act.wait_ge(*jobs.filled(b, f"qk{s}"))
                            nc.scalar.activation(sq[:, s % 2, :], jobs.out(f"qk{s}"), ACT.Square)
                            act.drain()
                            act.sem_inc(sq_ready.sem, 1)
                        if 0 <= s - 1 < H0:
                            i = s - 1
                            act.wait_ge(*jobs.filled(b, f"ss{i}"))
                            act.wait_ge(qkn_ready.sem, qkn_ready.at(b, i + 1, 2))
                            act.wait_ge(core.one, 1)
                            nc.scalar.activation(rq[:, i % 2, :], jobs.out(f"ss{i}"), ACT.Ln,
                                                              bias=core.eps[:, EPS_RMS:EPS_RMS + 1]).then_inc(jobs.sem_drained(f"ss{i}"), 1)
                            act.drain()
                            nc.scalar.activation(rq[:, i % 2, :], rq[:, i % 2, :], ACT.Exp, scale=-0.5)\
                                .then_inc(rq_ready.sem, 1)
                            act.drain()
                        if 0 <= s - 2 < H0:
                            i = s - 2
                            act.wait_ge(*jobs.filled(b, f"S{i}"))
                            nc.scalar.activation(P[:, i % 2, :], jobs.out(f"S{i}")[:, 0:384], ACT.Exp,
                                                              scale=1.0 / D).then_inc(jobs.sem_drained(f"S{i}"), 1)
                            act.drain()
                            act.sem_inc(P_ready.sem, 1)
                        if 0 <= s - 3 < H0:
                            i = s - 3
                            act.wait_ge(*jobs.filled(b, f"OD{i}"))
                            act.wait_ge(o_ready.sem, o_ready.at(b, i + 1, 2))
                            act.wait_ge(core.one, 1)
                            nc.scalar.activation(rd[:, i % 2, :], jobs.out(f"OD{i}")[:, T:2 * T], ACT.Ln)
                            act.drain()
                            nc.scalar.activation(rd[:, i % 2, :], rd[:, i % 2, :], ACT.Exp, scale=-1.0)\
                                .then_inc(rd_ready.sem, 1)
                            act.drain()

            @block.gpsimd
            def _(pool):
                nc.gpsimd.memset(ones[:, :], 1.0)
                pool.drain()
                pool.wait_ge(loads, 160)
                pool.sem_inc(P_ready.sem, P_ready.credit)
                with pool.Fori(0, NB) as b:
                    for s in range(H0 + 2):
                        if s < H0:
                            pool.wait_ge(ab_ready.sem, ab_ready.at(b, s + 1))
                            pool.wait_ge(qkn_ready.sem, qkn_ready.at(b, s + 1, 2))
                            nc.gpsimd.tensor_tensor(c[:, s % 2, :], a[:, s % 2, :], bq[:, s % 2, :], ALU.add)\
                                .then_inc(c_ready.sem, 1)
                        if 0 <= s - 2 < H0:
                            i = s - 2
                            pool.wait_ge(P_ready.sem, P_ready.at(b, i + 1))
                            p = P[:, i % 2, :].rearrange("p (n q) -> p n q", q=128)[:, 0:3:2, :]
                            nc.gpsimd.tensor_tensor(p, p, tri[:, :, :], ALU.mult).then_inc(P_masked.sem, 1)
                    pool.drain()

            @block.vector
            def _(dve):
                dve.wait_ge(loads, 160)
                dve.sem_inc(qkn_ready.sem, qkn_ready.credit)
                dve.sem_inc(o_ready.sem, o_ready.credit)
                with dve.Fori(0, NB) as b:
                    norm.dve_center(dve, b, x[:, cols(b)])
                    dve.wait_ge(scaled.sem, scaled.at(b, 1))
                    nc.vector.tensor_tensor(cent[:, :], cent[:, :], lrs[:, :], ALU.mult)
                    dve.drain()
                    nc.vector.tensor_scalar(h[:, :], cent[:, :], core.mod[0][:, 1, bass.ds(b, 1)],
                                            core.mod[0][:, 0, bass.ds(b, 1)], ALU.mult, ALU.add)\
                        .then_inc(h_ready.sem, 1)
                    dve.drain()
                    for s in range(H0 + 3):
                        if s < H0:
                            dve.wait_ge(*jobs.filled(b, f"qk{s}"))
                            dve.wait_ge(sq_ready.sem, sq_ready.at(b, s + 1))
                            o = jobs.out(f"qk{s}")
                            cs = cos[:, :, :].rearrange("p a b -> p (a b)")
                            sn = sin[:, :, :].rearrange("p a b -> p (a b)")
                            nc.vector.tensor_tensor(a[:, s % 2, :], o, cs, ALU.mult)
                            nc.vector.tensor_tensor(bq[0:64, s % 2, :], o[64:128, :], sn[0:64, :], ALU.mult)
                            nc.vector.tensor_tensor(bq[64:128, s % 2, :], o[0:64, :], sn[64:128, :],
                                                                 ALU.mult).then_inc(jobs.sem_drained(f"qk{s}"), 1)
                            dve.drain()
                            dve.sem_inc(ab_ready.sem, 1)
                        if 0 <= s - 1 < H0:
                            i = s - 1
                            dve.wait_ge(c_ready.sem, c_ready.at(b, i + 1))
                            dve.wait_ge(rq_ready.sem, rq_ready.at(b, i + 1))
                            dve.wait_ge(P_ready.sem, P_ready.at(b, i + 1, 2))
                            nc.vector.tensor_tensor(qk[:, i % 2, :], c[:, i % 2, :], rq[:, i % 2, :], ALU.mult)\
                                .then_inc(qkn_ready.sem, 1)
                        if 0 <= s - 3 < H0:
                            i = s - 3
                            dve.wait_ge(*jobs.filled(b, f"OD{i}"))
                            dve.wait_ge(rd_ready.sem, rd_ready.at(b, i + 1))
                            last = nc.vector.tensor_tensor(oT[:, i, :], jobs.out(f"OD{i}")[:, 0:T], rd[:, i % 2, :], ALU.mult)
                            last.then_inc(jobs.sem_drained(f"OD{i}"), 1)
                            dve.drain()
                            dve.sem_inc(o_ready.sem, 1)
                    dve.wait_ge(*jobs.filled(b, "WO"))
                    nc.vector.scalar_tensor_tensor(x[:, cols(b)], jobs.out("WO")[:, 0:T],
                                                                core.mod[0][:, 2, bass.ds(b, 1)], x[:, cols(b)],
                                                                ALU.mult, ALU.add).then_inc(jobs.sem_drained("WO"), 1)
                    dve.drain()
        jobs.close()



NETS = ("q", "k", "v", "f")


class Routed:

    def __init__(self, core, ctx, nets):
        sb = lambda *a: core.sb(ctx, *a)
        self.nets = nets
        self.nw = [sb(f"nw_{n}", [128, NLEAF]) for n in nets]
        self.nb = [sb(f"nb_{n}", [1, NLEAF]) for n in nets]
        self.w1 = [sb(f"w1_{n}", [128, NCH * 128]) for n in nets]
        self.b1 = [sb(f"b1_{n}", [128, NCH]) for n in nets]
        self.w2 = [sb(f"w2_{n}", [128, NCH * D]) for n in nets]
        self.b2 = [sb(f"b2_{n}", [128, 2 * D]) for n in nets]
        self.loads = core.sem(f"loads_{nets}")
        self.total = 16 * 6 * len(nets)

    def load(self, core, sp):
        for i, n in enumerate(self.nets):
            for part in ("nw", "nb", "w1", "b1", "w2", "b2"):
                dst = {"nw": self.nw, "nb": self.nb, "w1": self.w1, "b1": self.b1, "w2": self.w2, "b2": self.b2}[part][i]
                sp.dma_start(dst[:, :], core.dram[f"{n}_{part}"]).then_inc(self.loads, 16)


def routed0(core):
    nc, R = core.nc, core.routed
    G = 3 * NT
    NP = NCH // 2
    net_of = lambda i: R if i < 3 else F
    with ExitStack() as ctx:
        sb = lambda *a: core.sb(ctx, *a)
        F = Routed(core, ctx, "f")
        h, xn, yT, yf = (sb(n, [128, T]) for n in ("h1", "xn1", "yT1", "yf1"))
        cent, lsq, lrs = sb("cent1", [128, T]), sb("lsq1", [128, T]), sb("lrs1", [128, T])
        rows1 = sb("rows1", [1, 128])
        expand = sb("expand", [128, 16 * 128], BF16)
        bits, pa, pb = (sb(n, [128, G, NLEAF]) for n in ("bits", "path_a", "path_b"))
        pb3 = sb("path_b3", [128, NT, NLEAF])
        ohT = sb("ohT", [128, 4, 2 * T])
        mask = sb("leafmask", [128, 4, 2 * T], BF16)
        hid = sb("hid", [128, 4, 2 * T])
        qkv = sb("qkv1", [128, 3, T])
        P = sb("P1", [128, NT, T])
        mx, sm, rsm = (sb(n, [128, NT]) for n in ("mx1", "sm1", "rsm1"))
        S = lambda n, per, credit=0: Count(core.sem("l0f_" + n), per, credit)
        centered, squared, scaled = S("centered", 2), S("squared", 2), S("scaled", 2)
        h_ready, xn_ready, oh_ready, oh3_ready = (S(n, 1) for n in ("h_ready", "xn_ready", "onehot", "onehot3"))
        mask_ready, oht_ready, mask3_ready, oht3_ready = S("mask", 3), S("ohT", 3), S("mask3", 1), S("ohT3", 1)
        hid_act, hid_dve, hid_used = S("hid_act", 4 * NP // 2), S("hid_dve", 4 * NP // 2), S("hid_used", 4 * NP, 4)
        qkv_ready, V_ready, mx_ready, e_ready, P_ready, PT_ready, y_ready, yf_ready = (
            S("qkv", 3), S("V", 1), S("max", 1), S("exps", 1), S("P", 1), S("PT", 1), S("y", 1), S("yf", 1))
        consts = S("consts", 1)
        FRONT, MID, LATE = range(3)
        order, ring = [], 0
        for i in range(4):
            order.append((LATE if i == 3 else MID, f"A{i}", 4 + i % 2))
            for p in range(NP):
                order.append((LATE if i == 3 else MID, f"H{i}.{p}", ring % 4))
                ring += 1
        order += [(MID, "Vt", 6), (MID, "S", 7), (FRONT, "mean", 6), (FRONT, "var", 6), (FRONT, "xmean", 7), (MID, "PT", 6),
                  (FRONT, "xvar", 7), (MID, "AV", 6), (MID, "R3", 7), (FRONT, "R0", 6), (FRONT, "R1", 7), (FRONT, "R2", 6),
                  (MID, "T3", 7), (FRONT, "T0", 6), (FRONT, "T1", 7), (FRONT, "T2", 6)]
        jobs = Jobs(core.banks, [(n, b, 1) for _, n, b in order], NB + 2)
        args = (cent, lsq, lrs, centered, squared, scaled)
        norm, xnorm = Norm(core, jobs, "", *args), Norm(core, jobs, "x", *args)
        x = core.xT

        def every_iteration(eng, body):
            body(0, True, False, False)
            body(1, True, True, False)
            with eng.Fori(2, NB) as it:
                body(it, True, True, True)
            body(NB, False, True, True)
            body(NB + 1, False, False, True)

        with nc.Block() as block:
            @block.sync
            def _(sp):
                F.load(core, sp)

            @block.tensor
            def _(pe):
                pe.wait_ge(R.loads, R.total)
                pe.wait_ge(consts.sem, 1)
                pe.sem_inc(hid_used.sem, hid_used.credit)

                def route(b, i, src):
                    pe.wait_ge(*jobs.free(b, f"R{i}"))
                    for t in range(NT):
                        o = jobs.out(f"R{i}")[:, t * NLEAF:(t + 1) * NLEAF]
                        nc.tensor.matmul(o, src[:, t * 128:(t + 1) * 128], net_of(i).nw[i % 3][:, :], start=True, stop=False)
                        last = nc.tensor.matmul(o, rows1[:, :], net_of(i).nb[i % 3][:, :], start=False, stop=True)
                    last.then_inc(jobs.sem_filled(f"R{i}"), 1)

                def turn(b, i, path, g):
                    pe.wait_ge(*jobs.free(b, f"T{i}"))
                    for lt in range(2):
                        for t in range(NT):
                            last = nc.tensor.transpose(jobs.out(f"T{i}")[:, lt * T + t * 128:lt * T + (t + 1) * 128],
                                                       path[:, g + t, lt * 128:(lt + 1) * 128], core.ident[:, :])
                    last.then_inc(jobs.sem_filled(f"T{i}"), 1)

                def net(b, i, src, between):
                    acc = jobs.out(f"A{i}")[:, 0:T]
                    pe.wait_ge(*jobs.free(b, f"A{i}"))
                    for p in range(NP + 1):
                        if p < NP:
                            n = f"H{i}.{p}"
                            pe.wait_ge(*jobs.free(b, n))
                            for c in (2 * p, 2 * p + 1):
                                o = jobs.out(n)[:, (c % 2) * T:(c % 2 + 1) * T]
                                lt = c // 16
                                nc.tensor.matmul(o, expand[:, (c % 16) * 128:(c % 16 + 1) * 128],
                                                 mask[:, i, lt * T:(lt + 1) * T], start=True, stop=False)
                                last = nc.tensor.matmul(o, net_of(i).w1[i % 3][:, c * 128:(c + 1) * 128], src[:, :],
                                                        start=False, stop=True)
                            last.then_inc(jobs.sem_filled(n), 1)
                        if p == 0:
                            for lt in range(2):
                                nc.tensor.matmul(acc, net_of(i).b2[i % 3][:, lt * D:(lt + 1) * D], ohT[:, i, lt * T:(lt + 1) * T],
                                                 start=(lt == 0), stop=False)
                        else:
                            m = p - 1
                            made = hid_act if m % 2 == 0 else hid_dve
                            pe.wait_ge(made.sem, made.at(b - 1, i * (NP // 2) + m // 2 + 1))
                            for c in (2 * m, 2 * m + 1):
                                last = nc.tensor.matmul(acc, net_of(i).w2[i % 3][:, c * D:(c + 1) * D],
                                                        hid[:, m % 4, (c % 2) * T:(c % 2 + 1) * T],
                                                        start=False, stop=(c == NCH - 1))
                            if m < NP - 1:
                                last.then_inc(hid_used.sem, 1)
                        between(p)
                    last.then_inc(jobs.sem_filled(f"A{i}"), 1)
                    pe.sem_inc(hid_used.sem, 1)

                def skip(names):
                    pe.drain()
                    for _, n, b in order:
                        if n in names:
                            pe.sem_inc(core.banks.filled[b], 1)
                            pe.sem_inc(core.banks.drained[b], 1)

                def small(it, front, mid, p):
                    m = it - 1
                    for there, at, names in ((mid, 1, ["Vt", "S"]), (front, 2, ["mean"]), (front, 3, ["var"]), (front, 6, ["xmean"]),
                                             (mid, 7, ["PT"]), (front, 8, ["xvar"]), (mid, 9, ["AV"]), (mid, 11, ["R3"]),
                                             (front, 12, ["R0", "R1", "R2"]), (mid, NP, ["T3"])):
                        if p == at and not there:
                            skip(names)
                    if mid and p == 1:
                        pe.wait_ge(qkv_ready.sem, qkv_ready.at(m, 3))
                        pe.wait_ge(*jobs.free(it, "Vt"))
                        for t in range(NT):
                            last = nc.tensor.transpose(jobs.out("Vt")[:, t * 128:(t + 1) * 128],
                                                       qkv[:, 2, t * 128:(t + 1) * 128], core.ident[:, :])
                        last.then_inc(jobs.sem_filled("Vt"), 1)
                        pe.wait_ge(*jobs.free(it, "S"))
                        for t in range(NT):
                            last = nc.tensor.matmul(jobs.out("S")[:, t * T:(t + 1) * T], qkv[:, 0, t * 128:(t + 1) * 128],
                                                    qkv[:, 1, :], start=True, stop=True)
                        last.then_inc(jobs.sem_filled("S"), 1)
                    if front and p == 2:
                        norm.pe_mean(pe, it, x[:, bass.ds(it * T, T)])
                    if front and p == 3:
                        pe.wait_ge(squared.sem, squared.at(it, 1))
                        norm.pe_var_ready(pe, it)
                    if front and p == 6:
                        pe.wait_ge(h_ready.sem, h_ready.at(it, 1))
                        xnorm.pe_mean(pe, it, h[:, :])
                    if mid and p == 7:
                        pe.wait_ge(P_ready.sem, P_ready.at(m, 1))
                        pe.wait_ge(*jobs.free(it, "PT"))
                        for kt in range(NT):
                            for t in range(NT):
                                last = nc.tensor.transpose(jobs.out("PT")[:, kt * T + t * 128:kt * T + (t + 1) * 128],
                                                           P[:, t, kt * 128:(kt + 1) * 128], core.ident[:, :])
                        last.then_inc(jobs.sem_filled("PT"), 1)
                    if front and p == 8:
                        pe.wait_ge(squared.sem, squared.at(it, 2))
                        xnorm.pe_var_ready(pe, it)
                    if mid and p == 9:
                        pe.wait_ge(PT_ready.sem, PT_ready.at(m, 1))
                        pe.wait_ge(V_ready.sem, V_ready.at(m, 1))
                        pe.wait_ge(*jobs.free(it, "AV"))
                        for kt in range(NT):
                            last = nc.tensor.matmul(jobs.out("AV")[:, 0:T], qkv[:, 2, kt * 128:(kt + 1) * 128], P[:, kt, :],
                                                    start=(kt == 0), stop=(kt == NT - 1))
                        last.then_inc(jobs.sem_filled("AV"), 1)
                    if mid and p == 11:
                        pe.wait_ge(y_ready.sem, y_ready.at(m, 1))
                        pe.wait_ge(F.loads, F.total)
                        route(it, 3, yT)
                    if front and p == 12:
                        pe.wait_ge(xn_ready.sem, xn_ready.at(it, 1))
                        for i in range(3):
                            route(it, i, xn)
                    if p == NP:
                        if mid:
                            pe.wait_ge(oh3_ready.sem, oh3_ready.at(m, 1))
                            turn(it, 3, pb3, 0)
                        if front:
                            pe.wait_ge(oh_ready.sem, oh_ready.at(it, 1))
                            for i in range(3):
                                turn(it, i, pb, i * NT)
                        else:
                            skip(["T0", "T1", "T2"])

                def body(it, front, mid, late):
                    if mid:
                        for i in range(3):
                            pe.wait_ge(mask_ready.sem, mask_ready.at(it - 1, i + 1))
                            pe.wait_ge(oht_ready.sem, oht_ready.at(it - 1, i + 1))
                            net(it, i, xn, lambda p: None)
                    else:
                        skip([n for part, n, _ in order if part == MID and n[0] in "AH" and n != "AV"])
                        if late:
                            pe.sem_inc(hid_used.sem, 3 * NP)
                    if late:
                        pe.wait_ge(mask3_ready.sem, mask3_ready.at(it - 2, 1))
                        pe.wait_ge(oht3_ready.sem, oht3_ready.at(it - 2, 1))
                        pe.wait_ge(yf_ready.sem, yf_ready.at(it - 2, 1))
                        net(it, 3, yf, lambda p: small(it, front, mid, p))
                    else:
                        skip([n for part, n, _ in order if part == LATE])
                        if mid:
                            pe.sem_inc(hid_used.sem, NP)
                        for p in range(NP + 1):
                            small(it, front, mid, p)
                every_iteration(pe, body)

            @block.scalar
            def _(act):
                act.wait_ge(R.loads, R.total)
                act.preload_act_table_set("natural_log_exp_and_others")

                def hidden(b, i, func, pairs, between=None):
                    for p in pairs:
                        n = f"H{i}.{p}"
                        act.wait_ge(hid_used.sem, hid_used.at(b - 1, i * NP + p + 1, 4))
                        act.wait_ge(*jobs.filled(b, n))
                        for c in (2 * p, 2 * p + 1):
                            last = nc.scalar.activation(hid[:, p % 4, (c % 2) * T:(c % 2 + 1) * T],
                                                        jobs.out(n)[:, (c % 2) * T:(c % 2 + 1) * T], func,
                                                        bias=net_of(i).b1[i % 3][:, c:c + 1])
                        last.then_inc(jobs.sem_drained(n), 1)
                        act.drain()
                        act.sem_inc((hid_act if p % 2 == 0 else hid_dve).sem, 1)
                        if between is not None:
                            between(p)

                def small(it, front, mid, p):
                    m = it - 1
                    if mid and p == 1:
                        act.wait_ge(*jobs.filled(it, "Vt"))
                        nc.scalar.activation(qkv[:, 2, :], jobs.out("Vt")[:, 0:T], ACT.Copy).then_inc(jobs.sem_drained("Vt"), 1)
                        act.drain()
                        act.sem_inc(V_ready.sem, 1)
                    if front and p == 2:
                        norm.act_square(act, it, 1)
                    if p == 3:
                        act.preload_act_table_set("natural_log_exp_and_others")
                    if mid and p == 3:
                        act.wait_ge(mx_ready.sem, mx_ready.at(m, 1))
                        for t in range(NT):
                            last = nc.scalar.activation(P[:, t, :], jobs.out("S")[:, t * T:(t + 1) * T], ACT.Exp,
                                                        scale=1.0 / math.sqrt(D), bias=mx[:, t:t + 1], accum_out=sm[:, t:t + 1])
                        last.then_inc(jobs.sem_drained("S"), 1)
                        act.drain()
                        act.sem_inc(e_ready.sem, 1)
                    if front and p == 3:
                        norm.act_rsqrt(act, it)
                    if front and p == 7:
                        xnorm.act_square(act, it, 2)
                    if mid and p == 7:
                        act.wait_ge(*jobs.filled(it, "PT"))
                        nc.scalar.activation(P[:, :, :].rearrange("p a b -> p (a b)"), jobs.out("PT"), ACT.Copy)\
                            .then_inc(jobs.sem_drained("PT"), 1)
                        act.drain()
                        act.sem_inc(PT_ready.sem, 1)
                    if front and p == 8:
                        act.preload_act_table_set("natural_log_exp_and_others")
                        xnorm.act_rsqrt(act, it, sample=True)
                    if p == NP - 1:
                        if mid:
                            act.wait_ge(*jobs.filled(it, "T3"))
                            nc.scalar.activation(mask[:, 3, :], jobs.out("T3"), ACT.Copy, scale=BIG, bias=-BIG)\
                                .then_inc(jobs.sem_drained("T3"), 1)
                            act.drain()
                            act.sem_inc(mask3_ready.sem, 1)
                        if front:
                            for i in range(3):
                                act.wait_ge(*jobs.filled(it, f"T{i}"))
                                nc.scalar.activation(mask[:, i, :], jobs.out(f"T{i}"), ACT.Copy, scale=BIG, bias=-BIG)\
                                    .then_inc(jobs.sem_drained(f"T{i}"), 1)
                                act.drain()
                                act.sem_inc(mask_ready.sem, 1)

                def body(it, front, mid, late):
                    if mid:
                        for i in range(3):
                            hidden(it, i, ACT.Relu, range(0, NP, 2))
                            act.wait_ge(*jobs.filled(it, f"A{i}"))
                            nc.scalar.activation(qkv[:, i, :], jobs.out(f"A{i}")[:, 0:T], ACT.Copy)\
                                .then_inc(jobs.sem_drained(f"A{i}"), 1)
                            act.drain()
                            act.sem_inc(qkv_ready.sem, 1)
                    elif late:
                        act.sem_inc(hid_act.sem, 3 * NP // 2)
                        act.sem_inc(hid_dve.sem, 3 * NP // 2)
                    if late:
                        act.wait_ge(F.loads, F.total)
                        hidden(it, 3, ACT.Gelu, range(NP), lambda p: small(it, front, mid, p))
                    else:
                        for p in range(NP):
                            small(it, front, mid, p)
                        if mid:
                            act.sem_inc(hid_act.sem, NP // 2)
                            act.sem_inc(hid_dve.sem, NP // 2)

                every_iteration(act, body)

            @block.gpsimd
            def _(pool):
                nc.gpsimd.memset(expand[:, :], 1.0)
                nc.gpsimd.memset(rows1[:, :], 1.0)
                pool.drain()
                nc.gpsimd.affine_select(out=expand[:, :], in_=expand[:, :], compare_op=ALU.is_ge, fill=0.0, base=0,
                                        pattern=[[1, 16 * 128]], channel_multiplier=-LW)
                pool.drain()
                nc.gpsimd.affine_select(out=expand[:, :], in_=expand[:, :], compare_op=ALU.is_ge, fill=0.0, base=LW - 1,
                                        pattern=[[-1, 16 * 128]], channel_multiplier=LW)
                pool.drain()
                pool.sem_inc(consts.sem, 1)

            @block.vector
            def _(dve):
                dve.wait_ge(R.loads, R.total)

                def decide(b, ids, bits, pa, pb, g):
                    for i in ids:
                        dve.wait_ge(*jobs.filled(b, f"R{i}"))
                        k = (i % 3) * NT
                        nc.vector.tensor_scalar(bits[:, k:k + NT, :].rearrange("p a b -> p (a b)"),
                                                jobs.out(f"R{i}"), 0.0, None, ALU.is_gt).then_inc(jobs.sem_drained(f"R{i}"), 1)
                    dve.drain()
                    path = [pa, pb]
                    two = lambda t, n: t[:, 0:g, 0:2 * n].rearrange("p g (n two) -> p g n two", two=2)
                    nc.vector.tensor_copy(two(pa, 1)[:, :, :, 1], bits[:, 0:g, 0:1])
                    nc.vector.tensor_scalar(two(pa, 1)[:, :, :, 0], bits[:, 0:g, 0:1], -1.0, 1.0, ALU.mult, ALU.add)
                    dve.drain()
                    for lv in range(1, DEPTH):
                        n = 2 ** lv
                        src, dst = path[(lv + 1) % 2][:, 0:g, 0:n], two(path[lv % 2], n)
                        nc.vector.tensor_tensor(dst[:, :, :, 1], src, bits[:, 0:g, n - 1:2 * n - 1], ALU.mult)
                        dve.drain()
                        nc.vector.tensor_tensor(dst[:, :, :, 0], src, dst[:, :, :, 1], ALU.subtract)
                        dve.drain()

                def onehots(i):
                    nc.vector.tensor_scalar(ohT[:, i, :], mask[:, i, :], 0.0, None, ALU.is_equal)
                    dve.drain()

                def hidden(b, i):
                    for p in range(1, NP, 2):
                        n = f"H{i}.{p}"
                        dve.wait_ge(hid_used.sem, hid_used.at(b - 1, i * NP + p + 1, 4))
                        dve.wait_ge(*jobs.filled(b, n))
                        for c in (2 * p, 2 * p + 1):
                            last = nc.vector.tensor_scalar(hid[:, p % 4, (c % 2) * T:(c % 2 + 1) * T],
                                                           jobs.out(n)[:, (c % 2) * T:(c % 2 + 1) * T],
                                                           net_of(i).b1[i % 3][:, c:c + 1], 0.0, ALU.add, ALU.max)
                        last.then_inc(jobs.sem_drained(n), 1)
                        dve.drain()
                        dve.sem_inc(hid_dve.sem, 1)

                def body(it, front, mid, late):
                    m = it - 1
                    if mid:
                        for i in range(3):
                            hidden(it, i)
                        dve.wait_ge(*jobs.filled(it, "S"))
                        nc.vector.tensor_reduce(mx[:, :], jobs.out("S").rearrange("p (a b) -> p a b", a=NT), axis=AX.X, op=ALU.max)
                        dve.drain()
                        nc.vector.tensor_scalar(mx[:, :], mx[:, :], -1.0 / math.sqrt(D), None, ALU.mult)
                        dve.drain()
                        dve.sem_inc(mx_ready.sem, 1)
                    if front:
                        xb = x[:, bass.ds(it * T, T)]
                        norm.dve_center(dve, it, xb)
                    if mid:
                        dve.wait_ge(e_ready.sem, e_ready.at(m, 1))
                        nc.vector.reciprocal(rsm[:, :], sm[:, :])
                        dve.drain()
                        for t in range(NT):
                            nc.vector.tensor_scalar(P[:, t, :], P[:, t, :], rsm[:, t:t + 1], None, ALU.mult)
                        dve.drain()
                        dve.sem_inc(P_ready.sem, 1)
                    if front:
                        dve.wait_ge(scaled.sem, scaled.at(it, 1))
                        nc.vector.tensor_tensor(cent[:, :], cent[:, :], lrs[:, :], ALU.mult)
                        dve.drain()
                        nc.vector.tensor_scalar(h[:, :], cent[:, :], core.mod[0][:, 4, bass.ds(it, 1)],
                                                core.mod[0][:, 3, bass.ds(it, 1)], ALU.mult, ALU.add)
                        dve.drain()
                        dve.sem_inc(h_ready.sem, 1)
                        xnorm.dve_center(dve, it, h[:, :])
                    if mid:
                        dve.wait_ge(*jobs.filled(it, "AV"))
                        nc.vector.tensor_tensor(yT[:, :], jobs.out("AV")[:, 0:T], xn[:, :], ALU.add)\
                            .then_inc(jobs.sem_drained("AV"), 1)
                        dve.drain()
                        dve.sem_inc(y_ready.sem, 1)
                    if front:
                        dve.wait_ge(scaled.sem, scaled.at(it, 2))
                        nc.vector.tensor_tensor(xn[:, :], cent[:, :], lrs[:, :], ALU.mult)
                        dve.drain()
                        dve.sem_inc(xn_ready.sem, 1)
                    if mid:
                        decide(it, (3,), bits, pa, pb3, NT)
                        dve.sem_inc(oh3_ready.sem, 1)
                    if front:
                        decide(it, range(3), bits, pa, pb, G)
                        dve.sem_inc(oh_ready.sem, 1)
                    if late:
                        b = it - 2
                        dve.wait_ge(*jobs.filled(it, "A3"))
                        nc.vector.tensor_tensor(lsq[:, :], jobs.out("A3")[:, 0:T], yf[:, :], ALU.add)\
                            .then_inc(jobs.sem_drained("A3"), 1)
                        dve.drain()
                        xb = x[:, bass.ds(b * T, T)]
                        nc.vector.scalar_tensor_tensor(xb, lsq[:, :], core.mod[0][:, 5, bass.ds(b, 1)], xb, ALU.mult, ALU.add)
                        dve.drain()
                    if front:
                        for i in range(3):
                            dve.wait_ge(mask_ready.sem, mask_ready.at(it, i + 1))
                            onehots(i)
                            dve.sem_inc(oht_ready.sem, 1)
                    if mid:
                        nc.vector.tensor_copy(yf[:, :], yT[:, :])
                        dve.drain()
                        dve.sem_inc(yf_ready.sem, 1)
                        dve.wait_ge(mask3_ready.sem, mask3_ready.at(m, 1))
                        onehots(3)
                        dve.sem_inc(oht3_ready.sem, 1)

                every_iteration(dve, body)
        jobs.close()



def mamba1(core):
    nc, d = core.nc, core.dram
    NG = NS // 2
    with ExitStack() as ctx:
        sb = lambda *a: core.sb(ctx, *a)
        win, wx, wdt, wout = sb("win", [128, 2 * DI]), sb("wx", [128, 2, 96]), sb("wdt", [64, DI]), sb("wout", [128, 2, D])
        cw, cb, bdt = sb("convw", [128, 2, KC]), sb("convb", [128, 2]), sb("bdt", [128, 2])
        A, Dp = sb("A", [128, 2, NS]), sb("Dp", [128, 2])
        sel = sb("sel", [96, 2 * NS * 128])
        sel_b = sb("sel_b", [96, 2 * NS * 128], BF16)
        parts2, rest = sb("parts", [96, 2, T], BF16), sb("rest", [32, T])
        h = sb("h2", [128, T])
        cent, lsq, lrs = sb("cent2", [128, T]), sb("lsq2", [128, T]), sb("lrs2", [128, T])
        xp = sb("xp", [128, 2, T + KC - 1])
        xc, u, e, yy = (sb(n + "2", [128, 2, T]) for n in ("xc", "u", "e", "yy"))
        xs2, sres2, dt2, du2 = (sb(n + "2", [128, 2, 2, T]) for n in ("xs", "sres", "dt", "du"))
        xdbl = sb("xdbl", [96, T])
        dA, dBx, hs, hC = (sb(n, [128, 2, 2, 2, T]) for n in ("dA", "dBx", "hs", "hC"))
        loads = core.sem("l1a_loads")
        S = lambda n, per, credit=0: Count(core.sem("l1a_" + n), per, credit)
        centered, squared, scaled, h_ready = S("centered", 1), S("squared", 1), S("scaled", 1), S("h_ready", 1)
        xp_ready, conv_ready, xs_ready, xdbl_ready, u_ready, soft_ready = (
            S(n, 1) for n in ("xp", "conv", "xs", "xdbl", "u", "soft"))
        parts_ready = S("parts", 1)
        dt_ready, dA_ready, hC_ready, hC_used, yy_ready = (
            S("dt", 1), S("dA", NG), S("hC", NG, 2), S("hC_used", NG, 2), S("yy", 1))
        consts = core.sem("l1a_consts")
        jobs = Jobs(core.banks, [("mean", 6, 1), ("var", 7, 1), ("X0", 6, 1), ("X1", 7, 1), ("XD", 6, 1), ("DT", 7, 1)], NB)
        plan = [("Y0", 0, 1), ("Y1", 1, 1)]
        for g in range(NG):
            plan += [(f"B{g}", 2 + g % 2, 1), (f"C{g}", 4 + g % 2, 1)]
        scan = Jobs(core.banks, plan + [("OUT", 0, 1)], NB)
        norm = Norm(core, jobs, "", cent, lsq, lrs, centered, squared, scaled)
        x = core.xT
        flat = lambda ap: ap.rearrange("p a b -> p (a b)")

        def every_iteration(eng, body):
            body(0, 0, True, False)
            with eng.Fori(0, (NB - 2) // 2) as pair:
                body(pair * 2 + 1, 1, True, True)
                body(pair * 2 + 2, 0, True, True)
            body(NB - 1, 1, True, True)
            body(NB, 0, False, True)

        with nc.Block() as block:
            @block.sync
            def _(sp):
                for dst, n in ((win[:, :], "win"), (wx[:, :, :], "wx"), (wdt[:, :], "wdt"), (wout[:, :, :], "wout"),
                               (cw[:, :, :], "convw"), (cb[:, :], "convb"), (bdt[:, :], "bdt"), (A[:, :, :], "A_log"),
                               (Dp[:, :], "Dp"), (sel[:, :], "sel")):
                    sp.dma_start(dst, d[n]).then_inc(loads, 16)
                sp.wait_ge(loads, 160)

            @block.gpsimd
            def _(pool):
                nc.gpsimd.memset(dA[:, :, :, :, 0:1], 0.0)
                nc.gpsimd.memset(xp[:, :, 0:KC - 1], 0.0)
                pool.drain()
                pool.sem_inc(consts, 1)

            @block.tensor
            def _(pe):
                pe.wait_ge(loads, 160)
                pe.sem_inc(hC_used.sem, hC_used.credit)

                def front_step(b, y, step):
                    xs, parts = xs2[:, y, :, :], parts2[:, y, :]
                    if step == 0:
                        norm.pe_mean(pe, b, x[:, cols(b)])
                    if step == 1:
                        norm.pe_var(pe, b, 1)
                    if step == 3:
                        pe.wait_ge(h_ready.sem, h_ready.at(b, 1))
                        for i in range(2):
                            pe.wait_ge(*jobs.free(b, f"X{i}"))
                            for k in range(2):
                                last = nc.tensor.matmul(jobs.out(f"X{i}")[:, k * T:(k + 1) * T],
                                                        win[:, (2 * i + k) * 128:(2 * i + k + 1) * 128], h[:, :],
                                                        start=True, stop=True)
                            last.then_inc(jobs.sem_filled(f"X{i}"), 1)
                    if step == 5:
                        pe.wait_ge(xs_ready.sem, xs_ready.at(b, 1))
                        pe.wait_ge(*jobs.free(b, "XD"))
                        for k in range(2):
                            last = nc.tensor.matmul(jobs.out("XD")[0:96, 0:T], wx[:, k, :], xs[:, k, :], start=(k == 0), stop=(k == 1))
                        last.then_inc(jobs.sem_filled("XD"), 1)
                    if step == 6:
                        pe.wait_ge(xdbl_ready.sem, xdbl_ready.at(b, 1))
                        pe.wait_ge(*jobs.free(b, "DT"))
                        for k in range(2):
                            last = nc.tensor.matmul(jobs.out("DT")[:, k * T:(k + 1) * T], wdt[:, k * 128:(k + 1) * 128],
                                                    xdbl[0:DTR, :], start=True, stop=True)
                        last.then_inc(jobs.sem_filled("DT"), 1)

                def body(it, y, front, mid):
                    b = it - 1
                    parts = parts2[:, 1 - y, :]
                    if mid:
                        pe.wait_ge(parts_ready.sem, parts_ready.at(b, 1))
                    for g in range(NG + 1):
                        if mid and g < NG:
                            for name, at in ((f"B{g}", 0), (f"C{g}", NS)):
                                pe.wait_ge(*scan.free(b, name))
                                for j in range(2):
                                    n = at + 2 * g + j
                                    last = nc.tensor.matmul(scan.out(name)[:, j * T:(j + 1) * T],
                                                            sel_b[:, n * 128:(n + 1) * 128], parts,
                                                            start=True, stop=True)
                                last.then_inc(scan.sem_filled(name), 1)
                        if front:
                            front_step(it, y, g)
                        if mid and g >= 1:
                            i = g - 1
                            pe.wait_ge(hC_ready.sem, hC_ready.at(b, i + 1))
                            for k in range(2):
                                if i == 0:
                                    pe.wait_ge(*scan.free(b, f"Y{k}"))
                                for j in range(2):
                                    last = nc.tensor.matmul(scan.out(f"Y{k}")[:, 0:T], core.ident[:, :], hC[:, i % 2, k, j, :],
                                                            start=(i == 0 and j == 0), stop=(i == NG - 1 and j == 1))
                                if i == NG - 1:
                                    last.then_inc(scan.sem_filled(f"Y{k}"), 1)
                            if i < NG - 1:
                                last.then_inc(hC_used.sem, 1)
                            else:
                                pe.sem_inc(hC_used.sem, 1)
                    if mid:
                        pe.wait_ge(yy_ready.sem, yy_ready.at(b, 1))
                        pe.wait_ge(*scan.free(b, "OUT"))
                        for k in range(2):
                            last = nc.tensor.matmul(scan.out("OUT")[:, 0:T], wout[:, k, :], yy[:, k, :], start=(k == 0), stop=(k == 1))
                        last.then_inc(scan.sem_filled("OUT"), 1)

                every_iteration(pe, body)

            @block.scalar
            def _(act):
                act.wait_ge(loads, 160)
                act.wait_ge(consts, 1)
                act.preload_act_table_set("natural_log_exp_and_others")
                nc.scalar.activation(flat(A[:, :, :]), flat(A[:, :, :]), ACT.Exp)
                act.drain()
                nc.scalar.activation(flat(A[:, :, :]), flat(A[:, :, :]), ACT.Copy, scale=-1.0)
                act.drain()

                def front_step(b, y, step):
                    xs, sres = xs2[:, y, :, :], sres2[:, y, :, :]
                    if step == 0:
                        norm.act_square(act, b, 1)
                    if step == 1:
                        norm.act_rsqrt(act, b)
                    if step == 3:
                        act.wait_ge(*jobs.filled(b, "X0"))
                        nc.scalar.activation(xp[:, :, KC - 1:], jobs.out("X0").rearrange("p (a b) -> p a b", a=2), ACT.Copy)\
                            .then_inc(jobs.sem_drained("X0"), 1)
                        act.drain()
                        act.sem_inc(xp_ready.sem, 1)
                    if step == 4:
                        act.wait_ge(*jobs.filled(b, "X1"))
                        nc.scalar.activation(flat(sres), jobs.out("X1"), ACT.Silu).then_inc(jobs.sem_drained("X1"), 1)
                        act.wait_ge(conv_ready.sem, conv_ready.at(b, 1))
                        nc.scalar.activation(flat(xs), flat(xc[:, :, :]), ACT.Silu)
                        act.drain()
                        act.sem_inc(xs_ready.sem, 1)
                        act.preload_act_table_set("natural_log_exp_and_others")
                    if step == 5:
                        act.wait_ge(*jobs.filled(b, "XD"))
                        nc.scalar.activation(xdbl[:, :], jobs.out("XD")[0:96, 0:T], ACT.Copy).then_inc(jobs.sem_drained("XD"), 1)
                        act.drain()
                        act.sem_inc(xdbl_ready.sem, 1)
                    if step == 7:
                        act.wait_ge(u_ready.sem, u_ready.at(b, 1))
                        nc.scalar.activation(flat(e[:, :, :]), flat(e[:, :, :]), ACT.Exp, scale=-1.0)
                        act.drain()
                        nc.scalar.activation(flat(e[:, :, :]), flat(e[:, :, :]), ACT.Ln, bias=core.eps[:, EPS_ONE:EPS_ONE + 1])
                        act.drain()
                        act.sem_inc(soft_ready.sem, 1)

                def body(it, y, front, mid):
                    b, dt = it - 1, dt2[:, 1 - y, :, :]
                    if mid:
                        act.wait_ge(dt_ready.sem, dt_ready.at(b, 1))
                    for g in range(NG):
                        if mid:
                            act.wait_ge(hC_ready.sem, hC_ready.at(b, g + 1, 2))
                            for k in range(2):
                                for j in range(2):
                                    n = 2 * g + j
                                    nc.scalar.activation(dA[:, g % 2, k, j, 1:T], dt[:, k, 1:T], ACT.Exp, scale=A[:, k, n:n + 1])
                            act.drain()
                            act.sem_inc(dA_ready.sem, 1)
                        if front:
                            front_step(it, y, g)

                every_iteration(act, body)

            @block.vector
            def _(dve):
                dve.wait_ge(loads, 160)
                dve.wait_ge(consts, 1)
                nc.vector.tensor_copy(sel_b[:, :], sel[:, :])
                dve.drain()
                dve.sem_inc(hC_ready.sem, hC_ready.credit)

                def front_step(b, y, step):
                    xs, dt, du, parts = xs2[:, y, :, :], dt2[:, y, :, :], du2[:, y, :, :], parts2[:, y, :]
                    if step == 0:
                        norm.dve_center(dve, b, x[:, cols(b)])
                    if step == 1:
                        dve.wait_ge(scaled.sem, scaled.at(b, 1))
                        nc.vector.tensor_tensor(cent[:, :], cent[:, :], lrs[:, :], ALU.mult)
                        dve.drain()
                        nc.vector.tensor_scalar(h[:, :], cent[:, :], core.mod[1][:, 1, bass.ds(b, 1)],
                                                core.mod[1][:, 0, bass.ds(b, 1)], ALU.mult, ALU.add)
                        dve.drain()
                        dve.sem_inc(h_ready.sem, 1)
                    if step == 3:
                        dve.wait_ge(xp_ready.sem, xp_ready.at(b, 1))
                        for k in range(2):
                            nc.vector.tensor_scalar(xc[:, k, :], xp[:, k, 0:T], cw[:, k, 0:1], cb[:, k:k + 1], ALU.mult, ALU.add)
                        for j in range(1, KC):
                            dve.drain()
                            for k in range(2):
                                nc.vector.scalar_tensor_tensor(xc[:, k, :], xp[:, k, j:j + T], cw[:, k, j:j + 1], xc[:, k, :],
                                                               ALU.mult, ALU.add)
                        dve.drain()
                        dve.sem_inc(conv_ready.sem, 1)
                    if step == 6:
                        dve.wait_ge(*jobs.filled(b, "DT"))
                        for k in range(2):
                            last = nc.vector.tensor_scalar(u[:, k, :], jobs.out("DT")[:, k * T:(k + 1) * T], bdt[:, k:k + 1], None, ALU.add)
                        last.then_inc(jobs.sem_drained("DT"), 1)
                        dve.drain()
                        nc.vector.scalar_tensor_tensor(flat(e[:, :, :]), flat(u[:, :, :]), -1.0, flat(u[:, :, :]), ALU.mult, ALU.max)
                        dve.drain()
                        dve.sem_inc(u_ready.sem, 1)
                        dve.wait_ge(xdbl_ready.sem, xdbl_ready.at(b, 1))
                        bc = xdbl[DTR:96, :]
                        nc.vector.tensor_copy(parts[0:32, :], bc)
                        dve.drain()
                        nc.vector.tensor_tensor(rest[:, :], bc, parts[0:32, :], ALU.subtract)
                        dve.drain()
                        nc.vector.tensor_copy(parts[32:64, :], rest[:, :])
                        dve.drain()
                        nc.vector.tensor_tensor(rest[:, :], rest[:, :], parts[32:64, :], ALU.subtract)
                        dve.drain()
                        nc.vector.tensor_copy(parts[64:96, :], rest[:, :])
                        dve.drain()
                        dve.sem_inc(parts_ready.sem, 1)
                    if step == NG:
                        dve.wait_ge(soft_ready.sem, soft_ready.at(b, 1))
                        nc.vector.scalar_tensor_tensor(flat(dt), flat(u[:, :, :]), 0.0, flat(e[:, :, :]), ALU.max, ALU.add)
                        dve.drain()
                        dve.sem_inc(dt_ready.sem, 1)
                        nc.vector.tensor_tensor(flat(du), flat(dt), flat(xs), ALU.mult)
                        dve.drain()

                def body(it, y, front, mid):
                    b = it - 1
                    xs, sres, du = xs2[:, 1 - y, :, :], sres2[:, 1 - y, :, :], du2[:, 1 - y, :, :]
                    for g in range(NG):
                        if mid:
                            s = g % 2
                            four = lambda t: t[:, s, :, :, :].rearrange("p k j l -> p k (j l)")
                            dve.wait_ge(*scan.filled(b, f"B{g}"))
                            for k in range(2):
                                last = nc.vector.tensor_tensor(dBx[:, s, k, :, :], scan.out(f"B{g}").rearrange("p (j l) -> p j l", j=2),
                                                               spread(du[:, k, :], 2), ALU.mult)
                            last.then_inc(scan.sem_drained(f"B{g}"), 1)
                            dve.drain()
                            dve.wait_ge(dA_ready.sem, dA_ready.at(b, g + 1))
                            one_row = lambda t: t[:, s, :, :, :].rearrange("p k j l -> p (k j l)")
                            nc.vector.tensor_tensor_scan(one_row(hs), one_row(dA), one_row(dBx), 0.0, ALU.mult, ALU.add)
                            dve.drain()
                            dve.wait_ge(*scan.filled(b, f"C{g}"))
                            dve.wait_ge(hC_used.sem, hC_used.at(b, g + 1, 2))
                            last = nc.vector.tensor_tensor(four(hC), four(hs), spread(scan.out(f"C{g}"), 2), ALU.mult)
                            last.then_inc(scan.sem_drained(f"C{g}"), 1)
                            dve.drain()
                            dve.sem_inc(hC_ready.sem, 1)
                        if front:
                            front_step(it, y, g)
                    if front:
                        front_step(it, y, NG)
                    if mid:
                        for k in range(2):
                            dve.wait_ge(*scan.filled(b, f"Y{k}"))
                            nc.vector.scalar_tensor_tensor(yy[:, k, :], xs[:, k, :], Dp[:, k:k + 1],
                                                           scan.out(f"Y{k}")[:, 0:T], ALU.mult, ALU.add).then_inc(scan.sem_drained(f"Y{k}"), 1)
                        dve.drain()
                        nc.vector.tensor_tensor(flat(yy[:, :, :]), flat(yy[:, :, :]), flat(sres), ALU.mult)
                        dve.drain()
                        dve.sem_inc(yy_ready.sem, 1)
                        dve.wait_ge(*scan.filled(b, "OUT"))
                        nc.vector.scalar_tensor_tensor(x[:, cols(b)], scan.out("OUT")[:, 0:T],
                                                       core.mod[1][:, 2, bass.ds(b, 1)], x[:, cols(b)],
                                                       ALU.mult, ALU.add).then_inc(scan.sem_drained("OUT"), 1)
                        dve.drain()

                every_iteration(dve, body)
        jobs.close()
        scan.close()



def local1(core):
    nc, d = core.nc, core.dram
    N = L1 * NB
    FC = len(FCH)
    with ExitStack() as ctx:
        sb = lambda *a: core.sb(ctx, *a)
        wqk, wv, wo, w1, w2 = sb("wqk", [128, 2 * H1 * E1]), sb("wv1", [128, H1 * E1]), sb("wo1", [128, H1 // 2, D]), sb("w1", [128, 2 * FI]), sb("w2", [128, FC, D])
        NPAR = 3 + 2 * FC
        par = sb("par", [128, NPAR])
        scales = sb("scales", [128, 4, L1 * E1])
        rot = sb("rot", [128, 4, NT, E1])
        tab = sb("tab", [128, L1, 4, NT, E1])
        wmask = sb("wmask", [128, NT, 2 * W])
        wmask_b = sb("wmask_b", [128, NT, 8, 2 * W], BF16)
        ident_b = sb("ident_b", [128, 128], BF16)
        Y = sb("Y", [128, NB * T])
        xs, xv, xs2 = sb("xs3", [128, T]), sb("xv3", [128, T]), sb("xs4", [128, T])
        cent, lsq, lrs = sb("cent3", [128, T]), sb("lsq3", [128, T]), sb("lrs3", [128, T])
        sq, a, bq, c = (sb(n + "3", [128, 2, H1, 2, EH]) for n in ("sq", "a", "bq", "c"))
        qn = sb("qn3", [128, NT, 2, H1, 2, EH])
        ss = sb("ss3", [128, 2, H1])
        V = sb("V3", [128, NT, H1 * E1])
        qT = sb("qT3", [128, NT, H1 // 2, 128])
        kT = sb("kT3", [128, H1 // 2, W + T])
        z = sb("z3", [128, NT, H1, 2 * W])
        pc = sb("pc3", [128, H1, 2, W])
        band = sb("band", [128, NT, H1, 128])
        edge = sb("edge", [128, H1, W])
        mx, sm = sb("mx3", [128, NT, H1]), sb("sm3", [128, NT, H1])
        oT = sb("oT3", [128, H1 // 2, T])
        gl, hid = sb("gl3", [128, FC, T]), sb("hid3", [128, FC, T])
        loads, consts = core.sem("l1f_loads"), core.sem("l1f_consts")
        S = lambda n, per, credit=0: Count(core.sem("l1f_" + n), per, credit)
        m_centered, m_squared, m_scaled = S("m_centered", 1), S("m_squared", 1), S("m_scaled", 1)
        jobs0 = Jobs(core.banks, [("mean", 6, 1), ("var", 7, 1)], NB)
        norm0 = Norm(core, jobs0, "", cent, lsq, lrs, m_centered, m_squared, m_scaled)
        x = core.xT

        with nc.Block() as block:
            @block.sync
            def _(sp):
                for dst, n in ((scales[:, :, :], "scales"), (rot[:, :, :, :], "rot"), (wmask[:, :, :], "wmask")):
                    sp.dma_start(dst, d[n]).then_inc(loads, 16)
                sp.wait_ge(loads, 48)

            @block.gpsimd
            def _(pool):
                nc.gpsimd.memset(xs[:, 0:1], 0.0)
                nc.gpsimd.memset(xs2[:, 0:1], 0.0)
                nc.gpsimd.memset(kT[:, :, 0:W], 0.0)
                nc.gpsimd.memset(band[:, :, :, :], 0.0)
                pool.drain()

            @block.tensor
            def _(pe):
                with pe.Fori(0, NB) as b:
                    norm0.pe_mean(pe, b, x[:, cols(b)])
                    norm0.pe_var(pe, b, 1)

            @block.scalar
            def _(act):
                act.preload_act_table_set("natural_log_exp_and_others")
                with act.Fori(0, NB) as b:
                    norm0.act_root(act, b, 1)

            @block.vector
            def _(dve):
                dve.wait_ge(loads, 48)
                nc.vector.tensor_copy(ident_b[:, :], core.ident[:, :])
                for t in range(NT):
                    nc.vector.tensor_copy(wmask_b[:, t, :, :], spread(wmask[:, t, :], 8))
                with dve.Fori(0, NB) as b:
                    norm0.dve_center(dve, b, x[:, cols(b)])
                    dve.wait_ge(m_scaled.sem, m_scaled.at(b, 1))
                    nc.vector.tensor_tensor(cent[:, :], cent[:, :], lrs[:, :], ALU.mult)
                    dve.drain()
                    nc.vector.tensor_scalar(Y[:, cols(b)], cent[:, :], core.mod[1][:, 4, bass.ds(b, 1)],
                                            core.mod[1][:, 3, bass.ds(b, 1)], ALU.mult, ALU.add)
                    dve.drain()
        jobs0.close()

        FRONT, MID, LATE = range(3)
        w_loaded = core.sem("l1f_weights")
        front_ok, values_ok, mid_ok, late_ok = (core.sem(f"l1f_{n}_weights") for n in ("front", "values", "mid", "late"))
        pe_steps = core.sem("l1f_pe_steps")
        qk_used, wv_used, wo_used, w1_used, w2_used = (core.sem(f"l1f_{n}_used") for n in ("wqk", "wv", "wo", "w1", "w2"))
        xs_ready, xv_ready, xs2_ready, V_ready = S("xs", 1), S("xv", 1), S("xs2", 1), S("V", NT)
        sq_ready, ab_ready, c_ready, ss_ready, rn_ready = S("sq", 2 * NT), S("ab", 2 * NT), S("c", 2 * NT, 2), S("ss", 2 * NT), S("rn", 2 * NT)
        qn_ready, t_ready = S("qn", 2 * NT, 2), S("turned", 2 * NT, 2 * NT)
        z_ready, e_ready, rs_ready, p_ready, band_ready = (S(n, NT) for n in ("z", "exps", "sums", "p", "band"))
        o_ready, pc_ready, band2_ready = S("o", NT), S("pc", NT), S("band2", NT, 1)
        centered, squared, scaled, xn_ready = S("centered", 1), S("squared", 1), S("scaled", 1), S("xn", 1)
        gl_ready, hid_ready = S("gl", FC), S("hid", FC)

        Z = lambda t, banks: [(FRONT, f"Z{t}.{y}.{s}", banks[2 * y + s]) for y in range(2) for s in range(2)]
        Tn = lambda part, t, banks: [(part, f"T{t}.{y}.{j}", banks[2 * y + j]) for y in range(2) for j in range(2)]
        two = lambda part, n, b0, b1: [(part, n + ".0", b0), (part, n + ".1", b1)]
        order = (two(MID, "S0", 5, 4) + [(LATE, "mean", 6)] + Z(0, (0, 1, 2, 7)) + [(LATE, "var", 6)] + Tn(MID, 1, (3, 5, 4, 6))
                 + two(MID, "S1", 3, 5) + two(MID, "V0", 4, 6) + two(MID, "V1", 0, 1)
                
                 + Z(1, (0, 1, 6, 3)) + [(LATE, "F0", 2), (LATE, "F1", 7), (LATE, "F2", 4)] + Tn(FRONT, 0, (5, 2, 7, 4))
                 + two(MID, "O0", 5, 2) + [(LATE, "OUT2", 4)] + two(MID, "O1", 7, 0) + [(MID, "WO", 1)])
        jobs = Jobs(core.banks, [(n, b, 1) for _, n, b in order], N + 2)
        norm = Norm(core, jobs, "", cent, lsq, lrs, centered, squared, scaled)
        heads_view = lambda ap: ap.rearrange("p (h e) -> p h e", e=EH)

        def every_iteration(eng, body):
            body(0, True, False, False)
            body(1, True, True, False)
            with eng.Fori(2, N) as it:
                body(it, True, True, True)
            body(N, False, True, True)
            body(N + 1, False, False, True)

        with nc.Block() as block:
            @block.sync
            def _(sp):
                with sp.Fori(0, L1) as l:
                    row = bass.ds(l * 128, 128)
                    sp.wait_ge(qk_used, l * NB + 1)
                    sp.dma_start(wqk[:, :], d["wqkv"][row, 0:2 * H1 * E1]).then_inc(w_loaded, 16)
                    sp.wait_ge(w_loaded, l * 96 + 16)
                    sp.sem_inc(front_ok, NB)
                    sp.wait_ge(wv_used, l * NB + 1)
                    sp.dma_start(wv[:, :], d["wqkv"][row, 2 * H1 * E1:3 * H1 * E1]).then_inc(w_loaded, 16)
                    sp.wait_ge(w_loaded, l * 96 + 32)
                    sp.sem_inc(values_ok, NB)
                    sp.wait_ge(wo_used, l * NB + 1)
                    sp.dma_start(wo[:, :, :], d["wo1"][row, :].rearrange("p (a b) -> p a b", b=D)).then_inc(w_loaded, 16)
                    sp.wait_ge(w_loaded, l * 96 + 48)
                    sp.sem_inc(mid_ok, NB)
                    for dst, n, used in ((w1, "w1", w1_used), (w2, "w2", w2_used), (par, "params", None)):
                        if used is not None:
                            sp.wait_ge(used, l * NB + 1)
                        src, dst = d[n][bass.ds(l * 128, 128), :], dst[:, :] if len(dst.shape) == 2 else dst[:, :, :]
                        if len(dst.shape) == 3:
                            src = src.rearrange("p (a b) -> p a b", b=D)
                        sp.dma_start(dst, src).then_inc(w_loaded, 16)
                    sp.wait_ge(w_loaded, l * 96 + 96)
                    sp.sem_inc(late_ok, NB)

            @block.tensor
            def _(pe):
                for used in (qk_used, wv_used, wo_used, w1_used, w2_used):
                    pe.sem_inc(used, 1)

                def skip(part, it):
                    pe.drain()
                    for _, n, b in [o for o in order if o[1] in part]:
                        pe.sem_inc(core.banks.filled[b], 1)
                        pe.sem_inc(core.banks.drained[b], 1)

                def project(it, names, tok, w):
                    for j, n in enumerate(names):
                        pe.wait_ge(*jobs.free(it, n))
                        nc.tensor.matmul(jobs.out(n), tok, w[:, j * 512:(j + 1) * 512],
                                         start=True, stop=True).then_inc(jobs.sem_filled(n), 1)

                def turn(it, t, step):
                    for y in range(2):
                        pe.wait_ge(qn_ready.sem, qn_ready.at(step, 2 * t + y + 1))
                        for j in range(2):
                            n = f"T{t}.{y}.{j}"
                            pe.wait_ge(*jobs.free(it, n))
                            for i in range(4):
                                src = qn[:, t, y, 8 * j + 2 * i:8 * j + 2 * i + 2, :, :].rearrange("p h s e -> p (h s e)")
                                last = nc.tensor.transpose(jobs.out(n)[:, i * 128:(i + 1) * 128], src, core.ident[:, :])
                            last.then_inc(jobs.sem_filled(n), 1)

                def scores(it, t):
                    for j in range(2):
                        pe.wait_ge(*jobs.free(it, f"S{t}.{j}"))
                        nc.tensor.matmul(jobs.out(f"S{t}.{j}"), ident_b[:, :], wmask_b[:, t, :, :], start=True, stop=False)
                    for i in range(H1):
                        j, m = i % 2, i // 2
                        p, n = 64 * j, f"S{t}.{j}"
                        for w in range(4):
                            k0 = t * 128 + w * W
                            last = nc.tensor.matmul(jobs.out(n)[w * W:(w + 1) * W, m * 64:(m + 1) * 64],
                                                    qT[p:p + 64, t, m, w * W:(w + 1) * W],
                                                    kT[p:p + 64, m, k0:k0 + 2 * W], start=False, stop=(m == H1 // 2 - 1),
                                                    tile_position=(p, w * W))
                        if i >= H1 - 2:
                            last.then_inc(jobs.sem_filled(n), 1)

                def values(it, t):
                    pe.wait_ge(band_ready.sem, band_ready.at(it - 1, t + 1))
                    pe.wait_ge(band2_ready.sem, band2_ready.at(it - 1, t + 1))
                    for j in range(2):
                        n = f"O{t}.{j}"
                        pe.wait_ge(*jobs.free(it, n))
                        pe.sem_inc(pe_steps, 1)
                        for i in range(8):
                            hd = 8 * j + i
                            p, at = 64 * (hd % 2), 8 * (hd % 2) + hd // 2
                            o = jobs.out(n)[p:p + 64, (i // 2) * 128:(i // 2 + 1) * 128]
                            last = nc.tensor.matmul(o, V[:, t, hd * E1:(hd + 1) * E1], band[:, t, at, :],
                                                    start=True, stop=(t == 0), tile_position=(0, p))
                            if t:
                                last = nc.tensor.matmul(o[:, 0:W], V[96:128, t - 1, hd * E1:(hd + 1) * E1],
                                                        edge[96:128, at, :], start=False, stop=True, tile_position=(96, p))
                        last.then_inc(jobs.sem_filled(n), 1)

                def body(it, front, mid, late):
                    m, n = it - 1, it - 2
                    Zs = lambda t: [f"Z{t}.{y}.{s}" for y in range(2) for s in range(2)]
                    Ts = lambda t: [f"T{t}.{y}.{s}" for y in range(2) for s in range(2)]
                    if mid:
                        pe.wait_ge(t_ready.sem, t_ready.at(m, NT))
                        scores(it, 0)
                    else:
                        skip(["S0.0", "S0.1"], it)
                    if late:
                        pe.wait_ge(xs2_ready.sem, xs2_ready.at(n, 1))
                        norm.pe_mean(pe, it, xs2[:, :])
                    else:
                        skip(["mean"], it)
                    if front:
                        pe.wait_ge(front_ok, it + 1)
                        pe.wait_ge(xs_ready.sem, xs_ready.at(it, 1))
                        project(it, Zs(0), xs[:, 0:128], wqk)
                    else:
                        skip(Zs(0), it)
                    if late:
                        pe.wait_ge(squared.sem, squared.at(n, 1))
                        norm.pe_var_ready(pe, it)
                    else:
                        skip(["var"], it)
                    if mid:
                        turn(it, 1, m)
                        pe.wait_ge(t_ready.sem, t_ready.at(m, 2 * NT))
                        scores(it, 1)
                        pe.wait_ge(values_ok, m + 1)
                        pe.wait_ge(xv_ready.sem, xv_ready.at(m, 1))
                        for t in range(NT):
                            project(it, [f"V{t}.0", f"V{t}.1"], xv[:, t * 128:(t + 1) * 128], wv)
                    else:
                        skip(Ts(1) + ["S1.0", "S1.1", "V0.0", "V0.1", "V1.0", "V1.1"], it)
                    if front:
                        project(it, Zs(1), xs[:, 128:T], wqk)
                    else:
                        skip(Zs(1), it)
                    if late:
                        pe.wait_ge(late_ok, n + 1)
                        pe.wait_ge(xn_ready.sem, xn_ready.at(n, 1))
                        for c_, (c0, cw) in enumerate(FCH):
                            name = f"F{c_}"
                            pe.wait_ge(*jobs.free(it, name))
                            for y in range(2):
                                last = nc.tensor.matmul(jobs.out(name)[0:cw, y * T:(y + 1) * T], w1[:, y * FI + c0:y * FI + c0 + cw],
                                                        cent[:, :], start=True, stop=True)
                            last.then_inc(jobs.sem_filled(name), 1)
                    else:
                        skip(["F0", "F1", "F2"], it)
                    if front:
                        turn(it, 0, it)
                    else:
                        skip(Ts(0), it)
                    if mid:
                        pe.wait_ge(V_ready.sem, V_ready.at(m, NT))
                        values(it, 0)
                    else:
                        skip(["O0.0", "O0.1"], it)
                    if late:
                        pe.wait_ge(*jobs.free(it, "OUT2"))
                        for c_, (c0, cw) in enumerate(FCH):
                            pe.wait_ge(hid_ready.sem, hid_ready.at(n, c_ + 1))
                            last = nc.tensor.matmul(jobs.out("OUT2")[:, 0:T], w2[0:cw, c_, :], hid[0:cw, c_, :],
                                                    start=(c_ == 0), stop=(c_ == FC - 1))
                        last.then_inc(jobs.sem_filled("OUT2"), 1)
                    else:
                        skip(["OUT2"], it)
                    if mid:
                        values(it, 1)
                        pe.wait_ge(mid_ok, m + 1)
                        pe.wait_ge(o_ready.sem, o_ready.at(m, NT))
                        pe.wait_ge(*jobs.free(it, "WO"))
                        for i in range(H1 // 2):
                            last = nc.tensor.matmul(jobs.out("WO")[:, 0:T], wo[:, i, :], oT[:, i, :],
                                                    start=(i == 0), stop=(i == H1 // 2 - 1))
                        last.then_inc(jobs.sem_filled("WO"), 1)
                    else:
                        skip(["O1.0", "O1.1", "WO"], it)

                every_iteration(pe, body)
                pe.wait_ge(pe_steps, 2 * NT * N)

            @block.scalar
            def _(act):
                act.preload_act_table_set("natural_log_exp_and_others")
                act.sem_inc(t_ready.sem, t_ready.credit)

                def squares(it, t, y):
                    for s in range(2):
                        act.wait_ge(*jobs.filled(it, f"Z{t}.{y}.{s}"))
                        nc.scalar.activation(sq[:, y, :, s, :], heads_view(jobs.out(f"Z{t}.{y}.{s}")), ACT.Square)
                    act.drain()
                    act.sem_inc(sq_ready.sem, 1)

                def roots(it, t, y):
                    act.wait_ge(ss_ready.sem, ss_ready.at(it, 2 * t + y + 1))
                    nc.scalar.activation(ss[:, y, :], ss[:, y, :], ACT.Ln, scale=2.0 ** 16)
                    act.drain()
                    nc.scalar.activation(ss[:, y, :], ss[:, y, :], ACT.Exp, scale=-0.5,
                                         bias=core.eps[:, EPS_HALFLOG:EPS_HALFLOG + 1])
                    act.drain()
                    act.sem_inc(rn_ready.sem, 1)

                def turned(it, t):
                    for y in range(2):
                        for j in range(2):
                            n = f"T{t}.{y}.{j}"
                            act.wait_ge(*jobs.filled(it, n))
                            src = jobs.out(n).rearrange("p (a b) -> p a b", b=128)
                            dst = qT[:, t, 4 * j:4 * j + 4, :] if y == 0 else kT[:, 4 * j:4 * j + 4, W + t * 128:W + (t + 1) * 128]
                            nc.scalar.activation(dst, src, ACT.Copy).then_inc(jobs.sem_drained(n), 1)
                        act.drain()
                        act.sem_inc(t_ready.sem, 1)

                def exps(m, t):
                    act.wait_ge(z_ready.sem, z_ready.at(m, t + 1))
                    zt = z[:, t, :, :].rearrange("p a b -> p (a b)")
                    nc.scalar.activation(zt, zt, ACT.Exp)
                    act.drain()
                    act.sem_inc(e_ready.sem, 1)

                def scatter(m, t):
                    act.wait_ge(pc_ready.sem, pc_ready.at(m, t + 1))
                    for w in (2, 3):
                        rows = slice(w * W, (w + 1) * W)
                        nc.scalar.activation(band[rows, t, :, rows], pc[rows, :, 1, :], ACT.Copy)
                        nc.scalar.activation(band[(w - 1) * W:w * W, t, :, rows], pc[rows, :, 0, :], ACT.Copy)
                    act.drain()
                    act.sem_inc(band2_ready.sem, 1)

                def take_values(it, t):
                    for j in range(2):
                        act.wait_ge(*jobs.filled(it, f"V{t}.{j}"))
                        nc.scalar.activation(V[:, t, j * 512:(j + 1) * 512], jobs.out(f"V{t}.{j}"), ACT.Copy).then_inc(jobs.sem_drained(f"V{t}.{j}"), 1)
                    act.drain()
                    act.sem_inc(V_ready.sem, 1)

                def take_outputs(it, t):
                    for j in range(2):
                        n = f"O{t}.{j}"
                        act.wait_ge(*jobs.filled(it, n))
                        nc.scalar.activation(oT[:, 4 * j:4 * j + 4, t * 128:(t + 1) * 128],
                                                          jobs.out(n).rearrange("p (a b) -> p a b", b=128), ACT.Copy).then_inc(jobs.sem_drained(n), 1)
                    act.drain()
                    act.sem_inc(o_ready.sem, 1)

                def body(it, front, mid, late):
                    m, n = it - 1, it - 2
                    if mid:
                        exps(m, 0)
                    if late:
                        norm.act_square(act, n)
                    if front:
                        squares(it, 0, 0)
                    if late:
                        norm.act_rsqrt(act, it)
                    if mid:
                        turned(it, 1)
                    if front:
                        squares(it, 0, 1)
                        roots(it, 0, 0)
                        roots(it, 0, 1)
                    if mid:
                        take_values(it, 0)
                        take_values(it, 1)
                        act.sem_inc(wv_used, 1)
                    if front:
                        act.wait_ge(xs_ready.sem, xs_ready.at(it, 1))
                        nc.scalar.activation(xv[:, :], xs[:, :], ACT.Copy).then_inc(xv_ready.sem, 1)
                    if mid:
                        exps(m, 1)
                    if front:
                        squares(it, 1, 0)
                    if mid:
                        scatter(m, 0)
                    if late:
                        for c_, (c0, cw) in enumerate(FCH):
                            act.wait_ge(*jobs.filled(it, f"F{c_}"))
                            nc.scalar.activation(gl[0:cw, c_, :], jobs.out(f"F{c_}")[0:cw, T:2 * T], ACT.Gelu,
                                                 bias=par[0:cw, 3 + FC + c_:4 + FC + c_])
                            act.drain()
                            act.sem_inc(gl_ready.sem, 1)
                        act.preload_act_table_set("natural_log_exp_and_others")
                    if front:
                        squares(it, 1, 1)
                        act.sem_inc(qk_used, 1)
                        turned(it, 0)
                        roots(it, 1, 0)
                    if mid:
                        scatter(m, 1)
                        take_outputs(it, 0)
                        take_outputs(it, 1)
                    if front:
                        roots(it, 1, 1)

                every_iteration(act, body)

            @block.gpsimd
            def _(pool):
                pool.sem_inc(c_ready.sem, c_ready.credit)
                pool.sem_inc(qn_ready.sem, qn_ready.credit)

                def rotary_sum(it, t, y):
                    pool.wait_ge(ab_ready.sem, ab_ready.at(it, 2 * t + y + 1))
                    f = lambda q: q[:, y, :, :, :].rearrange("p h s e -> p (h s e)")
                    nc.gpsimd.tensor_tensor(f(c), f(a), f(bq), ALU.add)
                    pool.drain()
                    pool.sem_inc(c_ready.sem, 1)

                def unit(it, t, y):
                    pool.wait_ge(rn_ready.sem, rn_ready.at(it, 2 * t + y + 1))
                    pool.wait_ge(t_ready.sem, t_ready.at(it, 2 * t + y + 1, 2 * NT))
                    nc.gpsimd.tensor_tensor(qn[:, t, y, :, :, :].rearrange("p h s e -> p h (s e)"),
                                            c[:, y, :, :, :].rearrange("p h s e -> p h (s e)"), spread(ss[:, y, :], E1, 2), ALU.mult)
                    pool.drain()
                    pool.sem_inc(qn_ready.sem, 1)

                def by_sum(m, t):
                    pool.wait_ge(rs_ready.sem, rs_ready.at(m, t + 1))
                    nc.gpsimd.tensor_tensor(z[:, t, :, :], z[:, t, :, :], spread(sm[:, t, :], 2 * W, 2), ALU.mult)
                    pool.drain()
                    pool.sem_inc(p_ready.sem, 1)

                def body(it, front, mid, late):
                    m = it - 1
                    if front:
                        rotary_sum(it, 0, 0)
                        unit(it, 0, 0)
                    if mid:
                        by_sum(m, 0)
                    if front:
                        rotary_sum(it, 0, 1)
                        unit(it, 0, 1)
                    if mid:
                        by_sum(m, 1)
                    if front:
                        rotary_sum(it, 1, 0)
                        unit(it, 1, 0)
                        rotary_sum(it, 1, 1)
                        unit(it, 1, 1)

                every_iteration(pool, body)

            @block.vector
            def _(dve):
                for l in range(L1):
                    for j in range(4):
                        nc.vector.tensor_tensor(tab[:, l, j, :, :], rot[:, j, :, :], spread(scales[:, j, l * E1:(l + 1) * E1], NT), ALU.mult)
                dve.drain()

                def shifted(dst, b):
                    nc.vector.tensor_scalar(dst[0:64, :], Y[0:64, cols(b)], 1.0, None, ALU.mult)
                    nc.vector.tensor_scalar(dst[64:128, 1:T], Y[64:128, bass.ds(b * T, T - 1)], 1.0, None, ALU.mult)
                    dve.drain()

                def rotary(it, t, y):
                    dve.wait_ge(sq_ready.sem, sq_ready.at(it, 2 * t + y + 1))
                    if type(it) is int:
                        l = it // NB
                        table = lambda j, s: tab[:, l, 2 * y + j, t, s * EH:(s + 1) * EH]
                    else:
                        flat = tab[:, :, :, :, :].rearrange("p l j t e -> p (l j t e)")
                        table = lambda j, s: flat[:, bass.ds((it // NB) * (4 * NT * E1) + ((2 * y + j) * NT + t) * E1 + s * EH, EH)]
                    dve.wait_ge(c_ready.sem, c_ready.at(it, 2 * t + y + 1, 2))
                    for s in range(2):
                        Zs = heads_view(jobs.out(f"Z{t}.{y}.{s}"))
                        nc.vector.tensor_tensor(a[:, y, :, s, :], Zs, spread(table(0, s), H1), ALU.mult)
                        last = nc.vector.tensor_tensor(bq[:, y, :, 1 - s, :], Zs, spread(table(1, 1 - s), H1), ALU.mult)
                        last.then_inc(jobs.sem_drained(f"Z{t}.{y}.{s}"), 1)
                    dve.drain()
                    dve.sem_inc(ab_ready.sem, 1)
                    dve.wait_ge(qn_ready.sem, qn_ready.at(it, 2 * t + y + 1, 2))
                    nc.vector.tensor_reduce(ss[:, y, :], sq[:, y, :, :, :].rearrange("p h s e -> p h (s e)"), axis=AX.X, op=ALU.add)
                    dve.drain()
                    nc.vector.tensor_scalar(ss[:, y, :], ss[:, y, :], 1e-24, None, ALU.max)
                    dve.drain()
                    dve.sem_inc(ss_ready.sem, 1)

                def less_maximum(it, t):
                    ps = [jobs.out(f"S{t}.{j}").rearrange("p (h k) -> p h k", h=8) for j in range(2)]
                    for j in range(2):
                        dve.wait_ge(*jobs.filled(it, f"S{t}.{j}"))
                        nc.vector.tensor_reduce(mx[:, t, 8 * j:8 * j + 8], ps[j], axis=AX.X, op=ALU.max)
                    dve.drain()
                    for j in range(2):
                        nc.vector.tensor_tensor(z[:, t, 8 * j:8 * j + 8, :], ps[j],
                                                             spread(mx[:, t, 8 * j:8 * j + 8], 2 * W, 2), ALU.subtract).then_inc(jobs.sem_drained(f"S{t}.{j}"), 1)
                    dve.drain()
                    dve.sem_inc(z_ready.sem, 1)

                def sums(m, t):
                    dve.wait_ge(e_ready.sem, e_ready.at(m, t + 1))
                    nc.vector.tensor_reduce(sm[:, t, :], z[:, t, :, :], axis=AX.X, op=ALU.add)
                    dve.drain()
                    nc.vector.reciprocal(sm[:, t, :], sm[:, t, :])
                    dve.drain()
                    dve.sem_inc(rs_ready.sem, 1)

                def place(m, t):
                    dve.wait_ge(p_ready.sem, p_ready.at(m, t + 1))
                    dve.wait_ge(band2_ready.sem, band2_ready.at(m, t + 1, 1))
                    nc.vector.transpose(pc[:, :, :, :].rearrange("p h s k -> p (h s k)"), z[:, t, :, :].rearrange("p h k -> p (h k)"))
                    dve.drain()
                    dve.sem_inc(pc_ready.sem, 1)
                    for w in (0, 1):
                        rows = slice(w * W, (w + 1) * W)
                        nc.vector.tensor_copy(band[rows, t, :, rows], pc[rows, :, 1, :])
                        if w:
                            nc.vector.tensor_copy(band[(w - 1) * W:w * W, t, :, rows], pc[rows, :, 0, :])
                        elif t:
                            nc.vector.tensor_copy(edge[96:128, :, :], pc[rows, :, 0, :])
                    dve.drain()
                    dve.sem_inc(band_ready.sem, 1)

                def body(it, front, mid, late):
                    m, n = it - 1, it - 2
                    if mid:
                        less_maximum(it, 0)
                    if late:
                        norm.dve_center(dve, it, xs2[:, :])
                    if mid:
                        sums(m, 0)
                    if front:
                        rotary(it, 0, 0)
                    if late:
                        dve.wait_ge(late_ok, n + 1)
                        dve.wait_ge(scaled.sem, scaled.at(n, 1))
                        nc.vector.tensor_tensor(cent[:, :], cent[:, :], lrs[:, :], ALU.mult)
                        dve.drain()
                        nc.vector.tensor_scalar(cent[:, :], cent[:, :], par[:, 0:1], par[:, 1:2], ALU.mult, ALU.add)
                        dve.drain()
                        dve.sem_inc(xn_ready.sem, 1)
                    if front:
                        rotary(it, 0, 1)
                    if mid:
                        less_maximum(it, 1)
                        place(m, 0)
                        sums(m, 1)
                    if front:
                        rotary(it, 1, 0)
                    if late:
                        for c_, (c0, cw) in enumerate(FCH):
                            dve.wait_ge(gl_ready.sem, gl_ready.at(n, c_ + 1))
                            nc.vector.scalar_tensor_tensor(hid[0:cw, c_, :], jobs.out(f"F{c_}")[0:cw, 0:T], par[0:cw, 3 + c_:4 + c_],
                                                           gl[0:cw, c_, :], ALU.add, ALU.mult)\
                                .then_inc(jobs.sem_drained(f"F{c_}"), 1)
                            dve.drain()
                            dve.sem_inc(hid_ready.sem, 1)
                        dve.sem_inc(w1_used, 1)
                    if mid:
                        place(m, 1)
                    if front:
                        rotary(it, 1, 1)
                        dve.wait_ge(xv_ready.sem, xv_ready.at(it, 1))
                        shifted(xs, (it + 1) % NB)
                        dve.sem_inc(xs_ready.sem, 1)
                    if late:
                        b = n % NB
                        dve.wait_ge(*jobs.filled(it, "OUT2"))
                        nc.vector.scalar_tensor_tensor(Y[:, cols(b)], jobs.out("OUT2")[:, 0:T], par[:, 2:3], Y[:, cols(b)],
                                                       ALU.add, ALU.add).then_inc(jobs.sem_drained("OUT2"), 1)
                        dve.drain()
                        dve.sem_inc(w2_used, 1)
                    if mid:
                        b = m % NB
                        dve.wait_ge(*jobs.filled(it, "WO"))
                        nc.vector.tensor_tensor(Y[:, cols(b)], jobs.out("WO")[:, 0:T], Y[:, cols(b)], ALU.add)\
                            .then_inc(jobs.sem_drained("WO"), 1)
                        dve.drain()
                        dve.sem_inc(wo_used, 1)
                        shifted(xs2, b)
                        dve.sem_inc(xs2_ready.sem, 1)

                shifted(xs, 0)
                dve.sem_inc(xs_ready.sem, 1)
                dve.sem_inc(band2_ready.sem, band2_ready.credit)
                every_iteration(dve, body)
        jobs.close()

        with nc.Block() as block:
            @block.vector
            def _(dve):
                with dve.Fori(0, NB) as b:
                    nc.vector.scalar_tensor_tensor(x[:, cols(b)], Y[:, cols(b)], core.mod[1][:, 5, bass.ds(b, 1)],
                                                   x[:, cols(b)], ALU.mult, ALU.add)
                dve.drain()


def store(core, out):
    nc = core.nc
    stored = core.sem("stored")
    with nc.Block() as block:
        @block.sync
        def _(sp):
            sp.dma_start(out, core.xT[:, :]).then_inc(stored, 16)
            sp.wait_ge(stored, 16)


STAGES = [attention0, routed0, mamba1, local1]


def build(nc, dram, out):
    with ExitStack() as ctx:
        core = Core(nc, ctx, dram)
        with ExitStack() as early:
            core.routed = Routed(core, early, "qkv")
            prepare(core)
            for stage in STAGES:
                if stage in (attention0, routed0):
                    stage(core)
        for stage in STAGES:
            if stage not in (attention0, routed0):
                stage(core)
        store(core, out)


def layouts(v):
    a = {}
    a["xT"] = v["L0_attn_x"].transpose(2, 0, 1).reshape(D, NB * T)
    for i in range(2):
        a[f"c{i}"] = v[f"L{i}_c"].T
        a[f"wmod{i}"] = v[f"L{i}_wmod"]
    for n in ("wq", "wk", "wv"):
        a[n] = v["L0_attn_" + n].reshape(D, H0 * D)
    a["wo0"] = v["L0_attn_wo"].transpose(1, 0, 2).reshape(D, H0 * D)
    for n in "qkvf":
        w = lambda p: v[f"L0_ffn_{n}_{p}"]
        a[n + "_nw"] = np.pad(w("nw").T, ((0, 0), (0, 1)))
        a[n + "_nb"] = np.pad(w("nb")[None, :], ((0, 0), (0, 1)))
        a[n + "_w1"] = w("w1").transpose(1, 0, 2).reshape(D, NCH * 128)
        a[n + "_b1"] = w("b1").reshape(NCH, 128).T
        a[n + "_w2"] = w("w2").reshape(NCH, 128, D).transpose(1, 0, 2).reshape(128, NCH * D)
        a[n + "_b2"] = w("b2").reshape(2, 128, D).transpose(1, 0, 2).reshape(128, 2 * D)
    two = lambda w: w.reshape(2, 128, -1).transpose(1, 0, 2)
    m = lambda p: v["L1_attn_" + p]
    a["win"], a["wdt"] = m("W_in"), m("W_dt")
    a["wx"], a["wout"], a["convw"], a["A_log"] = two(m("W_x")), two(m("W_out")), two(m("conv_w")), two(m("A_log"))
    f = lambda p: v["L1_ffn_" + p]
    q, k, w = np.split(f("Wqkv"), 3, axis=-1)
    halves = lambda m: m.reshape(L1, D, H1, 2, EH).transpose(0, 1, 3, 2, 4).reshape(L1, D, H1 * E1)
    a["wqkv"] = np.concatenate([halves(q), halves(k), w], axis=-1).reshape(L1 * 128, 3 * H1 * E1)
    a["wo1"] = f("Wo").reshape(L1, H1 // 2, 128, D).transpose(0, 2, 1, 3).reshape(L1 * 128, H1 // 2 * D)
    a["w1"] = f("W1").reshape(L1 * 128, 2 * FI)
    pad = FCH[-1][0] + 128 - FI
    a["w2"] = np.pad(f("W2"), ((0, 0), (0, pad), (0, 0))).reshape(L1, len(FCH), 128, D).transpose(0, 2, 1, 3).reshape(L1 * 128, len(FCH) * D)
    b1 = np.pad(f("b1").reshape(L1, 2, FI), ((0, 0), (0, 0), (0, pad))).reshape(L1, 2 * len(FCH), 128)
    params = np.concatenate([f("ln_g")[:, None], f("ln_b")[:, None], f("b2")[:, None], b1], axis=1)
    a["params"] = params.transpose(0, 2, 1).reshape(L1 * 128, -1)
    swap = lambda m: m.reshape(L1, 2, EH)[:, ::-1].reshape(L1, E1)
    scales = np.stack([f("q_scale"), swap(f("q_scale")), f("k_scale"), swap(f("k_scale"))]).reshape(4, L1 * E1)
    a["scales"] = np.broadcast_to(scales[None], (128, 4, L1 * E1))
    a["convb"], a["bdt"], a["Dp"] = (m(p).reshape(2, 128).T for p in ("conv_b", "b_dt", "D"))
    return a


def constants():
    f = np.float32
    a = {"ident": np.eye(128, dtype=f)}
    half = D // 2
    freqs = np.power(f(1250), -np.arange(half, dtype=f) / f(half)).astype(f)
    rad = (np.arange(T, dtype=f)[:, None] * freqs[None, :]).astype(f)
    a["cos0"] = np.concatenate([np.cos(rad).T, np.cos(rad).T]).astype(f)
    a["sin0"] = np.concatenate([-np.sin(rad).T, np.sin(rad).T]).astype(f)
    k = np.arange(128)
    a["tri"] = (k[:, None] <= k[None, :]).astype(f)
    sel = np.zeros((96, 2 * NS, 128), f)
    sel[np.arange(96), np.arange(96) % (2 * NS), :] = 1.0
    a["sel"] = sel.reshape(96, 2 * NS * 128)
    pairs = np.arange(0, E1, 2, dtype=f)
    inv_freq = (f(1) / f(10000) ** (pairs / f(E1))).astype(f)
    t = np.arange(T, dtype=f)
    freqs = np.tile(t[:, None] * inv_freq[None, :], 2)
    scale = np.tile((((pairs + f(0.4 * E1)) / f(1.4 * E1))[None, :] ** ((t - T // 2) / f(W // 2))[:, None]).astype(f), 2)
    sign = np.repeat(np.array([-1.0, 1.0], f), EH)[None, :]
    tables = [np.cos(freqs) * scale * 8, np.sin(freqs) * scale * 8 * sign, np.cos(freqs) / scale, np.sin(freqs) / scale * sign]
    a["rot"] = np.stack(tables).astype(f).reshape(4, NT, 128, E1).transpose(2, 0, 1, 3)
    i, j = np.arange(128)[:, None] % W, np.arange(2 * W)[None, :]
    seen = np.where(j < W, j >= i, j - W <= i)
    first = seen & ~((np.arange(128)[:, None] < W) & (j < W))
    a["wmask"] = np.where(np.stack([first, seen], 1), 0.0, -3e38).astype(f)
    return a


def kernel(**inputs):
    import concourse.bacc as bacc
    from concourse.bass_utils import run_bass_kernel_spmd

    nc = bacc.Bacc("TRN2", target_bir_lowering=False, num_devices=1)
    arrays, dram = {}, {}
    for name, value in {**layouts(inputs), **constants()}.items():
        value = np.ascontiguousarray(value)
        arrays[f"in_{name}"] = value
        dram[name] = nc.dram_tensor(f"in_{name}", value.shape, mybir.dt.from_np(value.dtype), kind="ExternalInput").ap()
    out = nc.dram_tensor("out_xT", (D, NB * T), F32, kind="ExternalOutput").ap()
    build(nc, dram, out)
    got = run_bass_kernel_spmd(nc, [arrays], core_ids=[0]).results[0]["out_xT"]
    return np.ascontiguousarray(got.reshape(D, NB, T).transpose(1, 2, 0))
```
